# Optimizing a Trainium2 kernel written in Bass

```python
import numpy as np
import jax
import jax.numpy as jnp

def _softmax(x, axis=-1):
    return jax.nn.softmax(x, axis=axis)

def _gelu(x):
    return jax.nn.gelu(x, approximate=True)

def _silu(x):
    return jax.nn.silu(x)

def _sigmoid(x):
    return jax.nn.sigmoid(x)

def _layernorm(x, axis=-1, eps=1e-05):
    m = jnp.mean(x, axis=axis, keepdims=True)
    v = jnp.var(x, axis=axis, keepdims=True)
    return (x - m) / jnp.sqrt(v + eps)

def _scatter_add(tgt, idx, src, axis=0):
    return tgt.at[idx].add(src)

def _segment_sum(src, seg, n):
    return jax.ops.segment_sum(src, seg, n)
kernel_name = 'mk_decoder_postln_d4_seqx_r8_a7f5aa'

def setup_inputs(seed: int=0):
    np.random.seed(seed)
    _w = jnp.asarray

    def _rec_inputs():
        import jax
        import jax.numpy as jnp
        _rk = jax.random.key(seed)
        x = 7.22e-05 + 1 * jax.random.normal(jax.random.fold_in(_rk, 1), (4, 512, 128), jnp.float32)
        _lenS = 512 - jax.random.randint(jax.random.fold_in(_rk, 7), (4,), 0, max(1, 512 // 4) + 1, jnp.int32)
        _lenS2 = 77 - jax.random.randint(jax.random.fold_in(_rk, 8), (4,), 0, max(1, 77 // 4) + 1, jnp.int32)
        _ctx_1024P = jax.random.normal(jax.random.fold_in(_rk, 11), (4, 16, 128), jnp.float32)
        _ctx_1024c = jax.random.dirichlet(jax.random.fold_in(_rk, 511), 0.3 * jnp.ones((16,), jnp.float32), (4, 77))
        _ctx_1024t = jnp.einsum('bsk,bkd->bsd', _ctx_1024c, _ctx_1024P)
        _ctx_1024t = _ctx_1024t * jax.lax.rsqrt(jnp.mean(jnp.square(_ctx_1024t)) + 1e-12) * 0.953939
        ctx_1024 = 4.13588e-05 + 0.999923 * (_ctx_1024t + 0.3 * jax.random.normal(jax.random.fold_in(_rk, 611), (4, 77, 128), jnp.float32))
        _validS = jnp.arange(512)[None, :] < _lenS[:, None]
        _validS2 = jnp.arange(77)[None, :] < _lenS2[:, None]
        _causal = jnp.tril(jnp.ones((512, 512), dtype=bool))
        mask_BxSxS2_if1 = jnp.where(jnp.ones((4, 512, 77), dtype=bool), 1, 0).astype(jnp.int32)
        return (x, ctx_1024, mask_BxSxS2_if1)
    x, ctx_1024, mask_BxSxS2_if1 = _rec_inputs()

    def _L0_attn_setup():
        import jax, jax.numpy as jnp
        import numpy as np
        D_MODEL = 128
        NUM_LAYERS = 4
        D_STATE = 16
        D_CONV = 4
        EXPAND = 2
        D_INNER = EXPAND * D_MODEL
        DT_RANK = (D_MODEL + 15) // 16
        B, L = (4, 256)
        EPS = 1e-05

        def layer_norm(x, w, b):
            mu = jnp.mean(x, axis=-1, keepdims=True)
            var = jnp.mean(jnp.square(x - mu), axis=-1, keepdims=True)
            return (x - mu) * jax.lax.rsqrt(var + EPS) * w + b

        def mamba_block(x, Wi, cw, cb, Wx, Wdt, bdt, Alog, Dp, Wo):
            b, l, _ = x.shape
            xz = x @ Wi.T
            xs, z = jnp.split(xz, 2, axis=-1)
            xc = jnp.swapaxes(xs, 1, 2)
            xc = jax.lax.conv_general_dilated(xc, cw[:, None, :], (1,), [(D_CONV - 1, 0)], feature_group_count=D_INNER, dimension_numbers=('NCW', 'OIW', 'NCW'))
            u = jax.nn.silu(jnp.swapaxes(xc, 1, 2) + cb)
            xdbl = u @ Wx.T
            dt, Bc, Cc = jnp.split(xdbl, [DT_RANK, DT_RANK + D_STATE], axis=-1)
            dt = jax.nn.softplus(dt @ Wdt.T + bdt)
            A = -jnp.exp(Alog)

            def step(h, inp):
                dt_t, B_t, C_t, u_t = inp
                dA = jnp.exp(dt_t[:, :, None] * A)
                h = dA * h + dt_t[:, :, None] * B_t[:, None, :] * u_t[:, :, None]
                y = jnp.einsum('bds,bs->bd', h, C_t)
                return (h, y)
            h0 = jnp.zeros((b, D_INNER, D_STATE), x.dtype)
            xs_t = (jnp.swapaxes(dt, 0, 1), jnp.swapaxes(Bc, 0, 1), jnp.swapaxes(Cc, 0, 1), jnp.swapaxes(u, 0, 1))
            _, ys = jax.lax.scan(step, h0, xs_t)
            y = jnp.swapaxes(ys, 0, 1) + u * Dp
            y = y * jax.nn.silu(z)
            return y @ Wo.T
        key = jax.random.key(seed)
        ks = jax.random.split(key, 12)
        s = 0.02
        nl = NUM_LAYERS
        inp = {'x': jax.random.normal(ks[0], (B, L, D_MODEL), jnp.float32), 'W_in': jax.random.normal(ks[1], (nl, 2 * D_INNER, D_MODEL), jnp.float32) * s, 'conv_w': jax.random.normal(ks[2], (nl, D_INNER, D_CONV), jnp.float32) * s, 'conv_b': jnp.zeros((nl, D_INNER), jnp.float32), 'W_x': jax.random.normal(ks[3], (nl, DT_RANK + 2 * D_STATE, D_INNER), jnp.float32) * s, 'W_dt': jax.random.normal(ks[4], (nl, D_INNER, DT_RANK), jnp.float32) * s, 'b_dt': jnp.full((nl, D_INNER), -4.6, jnp.float32), 'A_log': jnp.broadcast_to(jnp.log(jnp.arange(1, D_STATE + 1, dtype=jnp.float32)), (nl, D_INNER, D_STATE)) * jnp.ones((nl, D_INNER, 1), jnp.float32), 'Dp': jnp.ones((nl, D_INNER), jnp.float32), 'W_out': jax.random.normal(ks[5], (nl, D_MODEL, D_INNER), jnp.float32) * s, 'ln_w': jnp.ones((nl, D_MODEL), jnp.float32), 'ln_b': jnp.zeros((nl, D_MODEL), jnp.float32)}
        return inp
    _L0_attn_all = _L0_attn_setup()
    _L0_attn_in = {k: v for k, v in _L0_attn_all.items() if k in ('W_in', 'conv_w', 'conv_b', 'W_x', 'W_dt', 'b_dt', 'A_log', 'Dp', 'W_out', 'ln_w', 'ln_b')}
    del _L0_attn_all

    def _L0_xattn_setup():
        import jax, jax.numpy as jnp
        import numpy as np
        import math
        D_MODEL = 128
        H = 16
        D_K = D_MODEL // H
        key = jax.random.key(seed)
        ks = jax.random.split(key, 8)
        B, S = (4, 256)
        xavier = math.sqrt(2.0 / (D_MODEL + D_MODEL))
        return {'Q': jax.random.normal(ks[0], (B, S, D_MODEL), dtype=jnp.float32), 'K': jax.random.normal(ks[1], (B, S, D_MODEL), dtype=jnp.float32), 'V': jax.random.normal(ks[2], (B, S, D_MODEL), dtype=jnp.float32), 'mask': jnp.ones((B, S, S), dtype=jnp.int32), 'W_Q': jax.random.normal(ks[3], (D_MODEL, D_MODEL), dtype=jnp.float32) * xavier, 'W_K': jax.random.normal(ks[4], (D_MODEL, D_MODEL), dtype=jnp.float32) * xavier, 'W_V': jax.random.normal(ks[5], (D_MODEL, D_MODEL), dtype=jnp.float32) * xavier, 'W_O': jax.random.normal(ks[6], (D_MODEL, D_MODEL), dtype=jnp.float32) * xavier}
    _L0_xattn_all = _L0_xattn_setup()
    _L0_xattn_in = {k: v for k, v in _L0_xattn_all.items() if k in ('W_Q', 'W_K', 'W_V', 'W_O')}
    del _L0_xattn_all

    def _L0_ffn_setup():
        import jax, jax.numpy as jnp
        import numpy as np
        E = 8
        K = 2
        CAP_RATIO = 1.05
        key = jax.random.key(seed)
        ks = jax.random.split(key, 4)
        B, S, D, H = (2, 256, 128, 512)
        x = jax.random.normal(ks[0], (B, S, D), jnp.float32)
        Wg = jax.random.normal(ks[1], (E, D), jnp.float32) * 0.02
        W1 = jax.random.normal(ks[2], (E, D, H), jnp.float32) * 0.02
        b1 = jnp.zeros((E, H), jnp.float32)
        W2 = jax.random.normal(ks[3], (E, H, D), jnp.float32) * 0.02
        b2 = jnp.zeros((E, D), jnp.float32)
        return {'x': x, 'Wg': Wg, 'W1': W1, 'b1': b1, 'W2': W2, 'b2': b2}
    _L0_ffn_all = _L0_ffn_setup()
    _L0_ffn_in = {k: v for k, v in _L0_ffn_all.items() if k in ('Wg', 'W1', 'b1', 'W2', 'b2')}
    del _L0_ffn_all

    def _L1_attn_setup():
        import jax, jax.numpy as jnp
        import numpy as np
        import math
        NUM_HEADS = 16
        MAX_REL = 64
        LOCAL_WINDOW = 32
        key = jax.random.key(seed)
        k1, k2, k3, k4 = jax.random.split(key, 4)
        B, L, D = (4, 128, 128)
        x = jax.random.normal(k1, (B, L, D), dtype=jnp.float32)
        w_qkv = jax.random.normal(k2, (3 * D, D), dtype=jnp.float32) * (1.0 / math.sqrt(D))
        w_out = jax.random.normal(k3, (D, D), dtype=jnp.float32) * (1.0 / math.sqrt(D))
        rel_emb = jax.random.normal(k4, (2 * MAX_REL + 1, D // NUM_HEADS), dtype=jnp.float32)
        return {'x': x, 'w_qkv': w_qkv, 'w_out': w_out, 'rel_emb': rel_emb}
    _L1_attn_all = _L1_attn_setup()
    _L1_attn_in = {k: v for k, v in _L1_attn_all.items() if k in ('w_qkv', 'w_out', 'rel_emb')}
    del _L1_attn_all

    def _L1_xattn_setup():
        import jax, jax.numpy as jnp
        import numpy as np
        E, TPE, H, F = (64, 64, 128, 128)
        key = jax.random.key(seed)
        k1, k2, k3, k4 = jax.random.split(key, 4)
        scale = 1.0 / np.sqrt(H)
        return {'x': jax.random.normal(k1, (E, TPE, H), dtype=jnp.float32), 'w1': jax.random.normal(k2, (E, F, H), dtype=jnp.float32) * scale, 'v1': jax.random.normal(k3, (E, F, H), dtype=jnp.float32) * scale, 'w2': jax.random.normal(k4, (E, F, H), dtype=jnp.float32) * scale}
    _L1_xattn_all = _L1_xattn_setup()
    _L1_xattn_in = {k: v for k, v in _L1_xattn_all.items() if k in ()}
    del _L1_xattn_all

    def _L1_ffn_setup():
        import jax, jax.numpy as jnp
        import numpy as np
        MICRO_BATCHES = 2
        TOP_K = 2
        NUM_EXPERTS = 8
        B, S, D = (4, 512, 128)
        H = 4 * D
        key = jax.random.key(seed)
        ks = jax.random.split(key, 8)
        s = 0.02
        return {'x': jax.random.normal(ks[0], (B, S, D), jnp.float32), 'ln_scale': jnp.ones((D,), jnp.float32), 'ln_bias': jnp.zeros((D,), jnp.float32), 'attn_w': jax.random.normal(ks[1], (D, D), jnp.float32) * s, 'attn_b': jnp.zeros((D,), jnp.float32), 'gate_w': jax.random.normal(ks[2], (NUM_EXPERTS, D), jnp.float32) * s, 'w1': jax.random.normal(ks[3], (NUM_EXPERTS, D, H), jnp.float32) * s, 'b1': jnp.zeros((NUM_EXPERTS, H), jnp.float32), 'w2': jax.random.normal(ks[4], (NUM_EXPERTS, H, D), jnp.float32) * s, 'b2': jnp.zeros((NUM_EXPERTS, D), jnp.float32), 'next_w': jax.random.normal(ks[5], (D, D), jnp.float32) * s, 'next_b': jnp.zeros((D,), jnp.float32)}
    _L1_ffn_all = _L1_ffn_setup()
    _L1_ffn_in = {k: v for k, v in _L1_ffn_all.items() if k in ('ln_scale', 'ln_bias', 'attn_w', 'attn_b', 'gate_w', 'w1', 'b1', 'w2', 'b2', 'next_w', 'next_b')}
    del _L1_ffn_all

    def _L2_attn_setup():
        import jax, jax.numpy as jnp
        import numpy as np
        B, S, DIM = (2, 1024, 128)
        NH, NKV, HD = (16, 4, 64)
        GROUPS = NH // NKV
        CHUNK = 128
        THETA = 10000.0

        def _slopes(h):
            return jnp.asarray([2.0 ** (-8.0 / h * (i + 1)) for i in range(h)], dtype=jnp.float32)

        def _rope_tables(s, d):
            inv = 1.0 / THETA ** (np.arange(0, d, 2, dtype=np.float64) / d)
            freqs = np.outer(np.arange(s, dtype=np.float64), inv)
            emb = np.concatenate([freqs, freqs], axis=-1)
            return (jnp.asarray(np.cos(emb), jnp.float32), jnp.asarray(np.sin(emb), jnp.float32))

        def _apply_rope(x, cos, sin):
            x1, x2 = jnp.split(x, 2, axis=-1)
            rot = jnp.concatenate([-x2, x1], axis=-1)
            return x * cos + rot * sin

        def _lightning_attn(q, k, v, slopes, chunk):
            b, h, s, d = q.shape
            nc = s // chunk
            t = jnp.arange(chunk, dtype=jnp.float32)
            sl = slopes[:, None, None]
            mask = jnp.where(t[:, None] >= t[None, :], jnp.exp(-sl * (t[:, None] - t[None, :])), 0.0)
            q_dec = jnp.exp(-slopes[:, None] * (t + 1.0))[..., None]
            k_dec = jnp.exp(-slopes[:, None] * (chunk - 1.0 - t))[..., None]
            blk_dec = jnp.exp(-slopes * chunk)[None, :, None, None]

            def to_chunks(x):
                return x.reshape(b, h, nc, chunk, d).transpose(2, 0, 1, 3, 4)
            qc, kc, vc = (to_chunks(q), to_chunks(k), to_chunks(v))

            def step(kv, inp):
                qi, ki, vi = inp
                scores = jnp.einsum('bhtd,bhsd->bhts', qi, ki) * mask
                o = jnp.einsum('bhts,bhsd->bhtd', scores, vi) + jnp.einsum('bhtd,bhde->bhte', qi * q_dec, kv)
                kv = blk_dec * kv + jnp.einsum('bhtd,bhte->bhde', ki * k_dec, vi)
                return (kv, o)
            kv0 = jnp.zeros((b, h, d, d), q.dtype)
            _, outs = jax.lax.scan(step, kv0, (qc, kc, vc))
            return outs.transpose(1, 2, 0, 3, 4).reshape(b, h, s, d)
        key = jax.random.key(seed)
        k0, k1, k2, k3, k4 = jax.random.split(key, 5)
        x = jax.random.normal(k0, (B, S, DIM), jnp.float32)
        Wq = jax.random.normal(k1, (NH * HD, DIM), jnp.float32) * 0.02
        Wk = jax.random.normal(k2, (NKV * HD, DIM), jnp.float32) * 0.02
        Wv = jax.random.normal(k3, (NKV * HD, DIM), jnp.float32) * 0.02
        Wo = jax.random.normal(k4, (DIM, NH * HD), jnp.float32) * 0.02
        return {'x': x, 'Wq': Wq, 'Wk': Wk, 'Wv': Wv, 'Wo': Wo}
    _L2_attn_all = _L2_attn_setup()
    _L2_attn_in = {k: v for k, v in _L2_attn_all.items() if k in ('Wq', 'Wk', 'Wv', 'Wo')}
    del _L2_attn_all

    def _L2_xattn_setup():
        import jax, jax.numpy as jnp
        import numpy as np
        EMBED = 128
        HEADS = 16
        HEAD_DIM = EMBED // HEADS
        key = jax.random.key(seed)
        ks = jax.random.split(key, 10)
        B, N, M = (4, 256, 256)
        s = 1.0 / np.sqrt(EMBED)
        return {'xq': jax.random.normal(ks[0], (B, N, EMBED), jnp.float32), 'xk': jax.random.normal(ks[1], (B, M, EMBED), jnp.float32), 'xv': jax.random.normal(ks[2], (B, M, EMBED), jnp.float32), 'Wq': jax.random.normal(ks[3], (EMBED, EMBED), jnp.float32) * s, 'bq': jnp.zeros((EMBED,), jnp.float32), 'Wk': jax.random.normal(ks[4], (EMBED, EMBED), jnp.float32) * s, 'bk': jnp.zeros((EMBED,), jnp.float32), 'Wv': jax.random.normal(ks[5], (EMBED, EMBED), jnp.float32) * s, 'bv': jnp.zeros((EMBED,), jnp.float32), 'Wo': jax.random.normal(ks[6], (EMBED, EMBED), jnp.float32) * s}
    _L2_xattn_all = _L2_xattn_setup()
    _L2_xattn_in = {k: v for k, v in _L2_xattn_all.items() if k in ('Wq', 'bq', 'Wk', 'bk', 'Wv', 'bv', 'Wo')}
    del _L2_xattn_all

    def _L2_ffn_setup():
        import jax, jax.numpy as jnp
        import numpy as np
        B, T, D = (1, 256, 128)
        E, DFF = (8, 512)

        def _gating(logits):
            S, num_e = logits.shape
            gates = jax.nn.softmax(logits.astype(jnp.float32), axis=1)
            idx1 = jnp.argmax(gates, axis=1)
            mask1 = jax.nn.one_hot(idx1, num_e, dtype=jnp.int32)
            logits_ex1 = jnp.where(mask1.astype(bool), -jnp.inf, logits)
            idx2 = jnp.argmax(logits_ex1, axis=1)
            mask2 = jax.nn.one_hot(idx2, num_e, dtype=jnp.int32)
            loc1 = jnp.cumsum(mask1, axis=0) - 1
            loc2 = jnp.cumsum(mask2, axis=0) - 1 + jnp.sum(mask1, axis=0, keepdims=True)
            loc1_s = jnp.sum(loc1 * mask1, axis=1)
            loc2_s = jnp.sum(loc2 * mask2, axis=1)
            g1 = jnp.sum(gates * mask1, axis=1)
            g2 = jnp.sum(gates * mask2, axis=1)
            denom = jnp.maximum(g1 + g2, jnp.finfo(jnp.float32).eps)
            g1, g2 = (g1 / denom, g2 / denom)
            cap = S
            loc1_sc = jax.nn.one_hot(loc1_s, cap, dtype=jnp.float32)
            loc2_sc = jax.nn.one_hot(loc2_s, cap, dtype=jnp.float32)
            combine = (g1[:, None] * mask1)[:, :, None] * loc1_sc[:, None, :] + (g2[:, None] * mask2)[:, :, None] * loc2_sc[:, None, :]
            dispatch_mask = combine != 0
            return (combine.astype(logits.dtype), dispatch_mask)
        key = jax.random.key(seed)
        k1, k2, k3, k4 = jax.random.split(key, 4)
        x = jax.random.normal(k1, (B, T, D), dtype=jnp.float32)
        Wg = jax.random.normal(k2, (D, E), dtype=jnp.float32) * (1.0 / np.sqrt(D))
        w1 = jax.random.normal(k3, (D, DFF), dtype=jnp.float32) * (1.0 / np.sqrt(D))
        w2 = jax.random.normal(k4, (DFF, D), dtype=jnp.float32) * (1.0 / np.sqrt(DFF))
        return {'x': x, 'Wg': Wg, 'w1': w1, 'w2': w2}
    _L2_ffn_all = _L2_ffn_setup()
    _L2_ffn_in = {k: v for k, v in _L2_ffn_all.items() if k in ('Wg', 'w1', 'w2')}
    del _L2_ffn_all

    def _L3_attn_setup():
        import math
        import jax, jax.numpy as jnp
        import numpy as np
        B, T, D_MODEL = (4, 128, 128)
        N_HEADS = 16
        HEAD_DIM = D_MODEL // N_HEADS
        TOP_K = 64

        def _scatter_last(base, idx, vals):
            d = base.shape[-1]
            k = idx.shape[-1]
            fb = base.reshape(-1, d)
            fi = idx.reshape(-1, k)
            fv = vals.reshape(-1, k)
            rows = jnp.arange(fb.shape[0])[:, None]
            return fb.at[rows, fi].set(fv).reshape(base.shape)

        def _sparsify_last_dim_topk(x, keep_k):
            if keep_k >= x.shape[-1]:
                return x
            _, idx = jax.lax.top_k(jnp.abs(x), keep_k)
            vals = jnp.take_along_axis(x, idx, axis=-1)
            return _scatter_last(jnp.zeros_like(x), idx, vals)

        def _forward(x, wq, wk, wv, wo):
            Bx, Tx, C = x.shape
            k_keep = min(TOP_K, Tx)
            feature_keep = min(HEAD_DIM, max(1, math.ceil(HEAD_DIM * (k_keep / Tx))))

            def proj(w):
                y = jnp.einsum('btc,dc->btd', x, w)
                return y.reshape(Bx, Tx, N_HEADS, HEAD_DIM).transpose(0, 2, 1, 3)
            q = _sparsify_last_dim_topk(proj(wq), feature_keep)
            k = _sparsify_last_dim_topk(proj(wk), feature_keep)
            v = _sparsify_last_dim_topk(proj(wv), feature_keep)
            scores = jnp.einsum('bhqd,bhkd->bhqk', q, k) / math.sqrt(HEAD_DIM)
            causal = jnp.triu(jnp.ones((Tx, Tx), dtype=bool), k=1)
            neg_inf = jnp.float32(-jnp.inf)
            scores = jnp.where(causal[None, None], neg_inf, scores)
            topk_vals, topk_idx = jax.lax.top_k(scores, k_keep)
            sparse_scores = _scatter_last(jnp.full_like(scores, neg_inf), topk_idx, topk_vals)
            attn = jax.nn.softmax(sparse_scores, axis=-1)
            out = jnp.einsum('bhqk,bhkd->bhqd', attn, v)
            out = out.transpose(0, 2, 1, 3).reshape(Bx, Tx, C)
            return jnp.einsum('btc,dc->btd', out, wo)
        key = jax.random.key(seed)
        kx, kq, kk, kv, ko = jax.random.split(key, 5)
        scale = 0.02
        x = jax.random.normal(kx, (B, T, D_MODEL), dtype=jnp.float32)
        wq = jax.random.normal(kq, (D_MODEL, D_MODEL), dtype=jnp.float32) * scale
        wk = jax.random.normal(kk, (D_MODEL, D_MODEL), dtype=jnp.float32) * scale
        wv = jax.random.normal(kv, (D_MODEL, D_MODEL), dtype=jnp.float32) * scale
        wo = jax.random.normal(ko, (D_MODEL, D_MODEL), dtype=jnp.float32) * scale
        return {'x': x, 'wq': wq, 'wk': wk, 'wv': wv, 'wo': wo}
    _L3_attn_all = _L3_attn_setup()
    _L3_attn_in = {k: v for k, v in _L3_attn_all.items() if k in ('wq', 'wk', 'wv', 'wo')}
    del _L3_attn_all

    def _L3_xattn_setup():
        import jax, jax.numpy as jnp
        import numpy as np
        HIDDEN = 128
        NUM_HEADS = 16
        HEAD_DIM = HIDDEN // NUM_HEADS
        SCALE = 1.0 / float(np.sqrt(HEAD_DIM))
        key = jax.random.key(seed)
        ks = jax.random.split(key, 10)
        B, SQ, SKV = (2, 256, 512)
        init = 0.02
        return {'query_states': jax.random.normal(ks[0], (B, SQ, HIDDEN), dtype=jnp.float32), 'key_value_states': jax.random.normal(ks[1], (B, SKV, HIDDEN), dtype=jnp.float32), 'Wq': jax.random.normal(ks[2], (HIDDEN, HIDDEN), dtype=jnp.float32) * init, 'bq': jnp.zeros((HIDDEN,), dtype=jnp.float32), 'Wk': jax.random.normal(ks[3], (HIDDEN, HIDDEN), dtype=jnp.float32) * init, 'bk': jnp.zeros((HIDDEN,), dtype=jnp.float32), 'Wv': jax.random.normal(ks[4], (HIDDEN, HIDDEN), dtype=jnp.float32) * init, 'bv': jnp.zeros((HIDDEN,), dtype=jnp.float32), 'Wo': jax.random.normal(ks[5], (HIDDEN, HIDDEN), dtype=jnp.float32) * init, 'bo': jnp.zeros((HIDDEN,), dtype=jnp.float32)}
    _L3_xattn_all = _L3_xattn_setup()
    _L3_xattn_in = {k: v for k, v in _L3_xattn_all.items() if k in ('Wq', 'bq', 'Wk', 'bk', 'Wv', 'bv', 'Wo', 'bo')}
    del _L3_xattn_all

    def _L3_ffn_setup():
        import jax, jax.numpy as jnp
        import numpy as np
        MAX_VAL = 100.0
        key = jax.random.key(seed)
        k1, k2, k3 = jax.random.split(key, 3)
        B, S, D_IN, D_OUT = (4, 1024, 128, 128)
        x = jax.random.normal(k1, (B, S, D_IN), dtype=jnp.float32)
        weights = jax.random.normal(k2, (D_OUT, D_IN), dtype=jnp.float32)
        scale = jnp.ones((D_OUT,), dtype=jnp.float32)
        bias = jax.random.normal(k3, (D_OUT,), dtype=jnp.float32)
        return {'x': x, 'weights': weights, 'scale': scale, 'bias': bias}
    _L3_ffn_all = _L3_ffn_setup()
    _L3_ffn_in = {k: v for k, v in _L3_ffn_all.items() if k in ('weights', 'scale', 'bias')}
    del _L3_ffn_all
    return {'x': x, 'ctx_1024': ctx_1024, 'mask_BxSxS2_if1': mask_BxSxS2_if1, 'L0_attn_W_in': _L0_attn_in['W_in'], 'L0_attn_conv_w': _L0_attn_in['conv_w'], 'L0_attn_conv_b': _L0_attn_in['conv_b'], 'L0_attn_W_x': _L0_attn_in['W_x'], 'L0_attn_W_dt': _L0_attn_in['W_dt'], 'L0_attn_b_dt': _L0_attn_in['b_dt'], 'L0_attn_A_log': _L0_attn_in['A_log'], 'L0_attn_Dp': _L0_attn_in['Dp'], 'L0_attn_W_out': _L0_attn_in['W_out'], 'L0_attn_ln_w': _L0_attn_in['ln_w'], 'L0_attn_ln_b': _L0_attn_in['ln_b'], 'L0_xattn_W_Q': _L0_xattn_in['W_Q'], 'L0_xattn_W_K': _L0_xattn_in['W_K'], 'L0_xattn_W_V': _L0_xattn_in['W_V'], 'L0_xattn_W_O': _L0_xattn_in['W_O'], 'L0_ffn_Wg': _L0_ffn_in['Wg'], 'L0_ffn_W1': _L0_ffn_in['W1'], 'L0_ffn_b1': _L0_ffn_in['b1'], 'L0_ffn_W2': _L0_ffn_in['W2'], 'L0_ffn_b2': _L0_ffn_in['b2'], 'L1_attn_w_qkv': _L1_attn_in['w_qkv'], 'L1_attn_w_out': _L1_attn_in['w_out'], 'L1_attn_rel_emb': _L1_attn_in['rel_emb'], 'L1_ffn_ln_scale': _L1_ffn_in['ln_scale'], 'L1_ffn_ln_bias': _L1_ffn_in['ln_bias'], 'L1_ffn_attn_w': _L1_ffn_in['attn_w'], 'L1_ffn_attn_b': _L1_ffn_in['attn_b'], 'L1_ffn_gate_w': _L1_ffn_in['gate_w'], 'L1_ffn_w1': _L1_ffn_in['w1'], 'L1_ffn_b1': _L1_ffn_in['b1'], 'L1_ffn_w2': _L1_ffn_in['w2'], 'L1_ffn_b2': _L1_ffn_in['b2'], 'L1_ffn_next_w': _L1_ffn_in['next_w'], 'L1_ffn_next_b': _L1_ffn_in['next_b'], 'L2_attn_Wq': _L2_attn_in['Wq'], 'L2_attn_Wk': _L2_attn_in['Wk'], 'L2_attn_Wv': _L2_attn_in['Wv'], 'L2_attn_Wo': _L2_attn_in['Wo'], 'L2_xattn_Wq': _L2_xattn_in['Wq'], 'L2_xattn_bq': _L2_xattn_in['bq'], 'L2_xattn_Wk': _L2_xattn_in['Wk'], 'L2_xattn_bk': _L2_xattn_in['bk'], 'L2_xattn_Wv': _L2_xattn_in['Wv'], 'L2_xattn_bv': _L2_xattn_in['bv'], 'L2_xattn_Wo': _L2_xattn_in['Wo'], 'L2_ffn_Wg': _L2_ffn_in['Wg'], 'L2_ffn_w1': _L2_ffn_in['w1'], 'L2_ffn_w2': _L2_ffn_in['w2'], 'L3_attn_wq': _L3_attn_in['wq'], 'L3_attn_wk': _L3_attn_in['wk'], 'L3_attn_wv': _L3_attn_in['wv'], 'L3_attn_wo': _L3_attn_in['wo'], 'L3_xattn_Wq': _L3_xattn_in['Wq'], 'L3_xattn_bq': _L3_xattn_in['bq'], 'L3_xattn_Wk': _L3_xattn_in['Wk'], 'L3_xattn_bk': _L3_xattn_in['bk'], 'L3_xattn_Wv': _L3_xattn_in['Wv'], 'L3_xattn_bv': _L3_xattn_in['bv'], 'L3_xattn_Wo': _L3_xattn_in['Wo'], 'L3_xattn_bo': _L3_xattn_in['bo'], 'L3_ffn_weights': _L3_ffn_in['weights'], 'L3_ffn_scale': _L3_ffn_in['scale'], 'L3_ffn_bias': _L3_ffn_in['bias']}

def reference(x, ctx_1024, mask_BxSxS2_if1, L0_attn_W_in, L0_attn_conv_w, L0_attn_conv_b, L0_attn_W_x, L0_attn_W_dt, L0_attn_b_dt, L0_attn_A_log, L0_attn_Dp, L0_attn_W_out, L0_attn_ln_w, L0_attn_ln_b, L0_xattn_W_Q, L0_xattn_W_K, L0_xattn_W_V, L0_xattn_W_O, L0_ffn_Wg, L0_ffn_W1, L0_ffn_b1, L0_ffn_W2, L0_ffn_b2, L1_attn_w_qkv, L1_attn_w_out, L1_attn_rel_emb, L1_ffn_ln_scale, L1_ffn_ln_bias, L1_ffn_attn_w, L1_ffn_attn_b, L1_ffn_gate_w, L1_ffn_w1, L1_ffn_b1, L1_ffn_w2, L1_ffn_b2, L1_ffn_next_w, L1_ffn_next_b, L2_attn_Wq, L2_attn_Wk, L2_attn_Wv, L2_attn_Wo, L2_xattn_Wq, L2_xattn_bq, L2_xattn_Wk, L2_xattn_bk, L2_xattn_Wv, L2_xattn_bv, L2_xattn_Wo, L2_ffn_Wg, L2_ffn_w1, L2_ffn_w2, L3_attn_wq, L3_attn_wk, L3_attn_wv, L3_attn_wo, L3_xattn_Wq, L3_xattn_bq, L3_xattn_Wk, L3_xattn_bk, L3_xattn_Wv, L3_xattn_bv, L3_xattn_Wo, L3_xattn_bo, L3_ffn_weights, L3_ffn_scale, L3_ffn_bias):
    import jax
    import jax.numpy as jnp

    def _L0_attn_ref(x, W_in, conv_w, conv_b, W_x, W_dt, b_dt, A_log, Dp, W_out, ln_w, ln_b):
        import jax, jax.numpy as jnp
        import numpy as np
        D_MODEL = 128
        NUM_LAYERS = 4
        D_STATE = 16
        D_CONV = 4
        EXPAND = 2
        D_INNER = EXPAND * D_MODEL
        DT_RANK = (D_MODEL + 15) // 16
        B, L = (4, 256)
        EPS = 1e-05

        def layer_norm(x, w, b):
            mu = jnp.mean(x, axis=-1, keepdims=True)
            var = jnp.mean(jnp.square(x - mu), axis=-1, keepdims=True)
            return (x - mu) * jax.lax.rsqrt(var + EPS) * w + b

        def mamba_block(x, Wi, cw, cb, Wx, Wdt, bdt, Alog, Dp, Wo):
            b, l, _ = x.shape
            xz = x @ Wi.T
            xs, z = jnp.split(xz, 2, axis=-1)
            xc = jnp.swapaxes(xs, 1, 2)
            xc = jax.lax.conv_general_dilated(xc, cw[:, None, :], (1,), [(D_CONV - 1, 0)], feature_group_count=D_INNER, dimension_numbers=('NCW', 'OIW', 'NCW'))
            u = jax.nn.silu(jnp.swapaxes(xc, 1, 2) + cb)
            xdbl = u @ Wx.T
            dt, Bc, Cc = jnp.split(xdbl, [DT_RANK, DT_RANK + D_STATE], axis=-1)
            dt = jax.nn.softplus(dt @ Wdt.T + bdt)
            A = -jnp.exp(Alog)

            def step(h, inp):
                dt_t, B_t, C_t, u_t = inp
                dA = jnp.exp(dt_t[:, :, None] * A)
                h = dA * h + dt_t[:, :, None] * B_t[:, None, :] * u_t[:, :, None]
                y = jnp.einsum('bds,bs->bd', h, C_t)
                return (h, y)
            h0 = jnp.zeros((b, D_INNER, D_STATE), x.dtype)
            xs_t = (jnp.swapaxes(dt, 0, 1), jnp.swapaxes(Bc, 0, 1), jnp.swapaxes(Cc, 0, 1), jnp.swapaxes(u, 0, 1))
            _, ys = jax.lax.scan(step, h0, xs_t)
            y = jnp.swapaxes(ys, 0, 1) + u * Dp
            y = y * jax.nn.silu(z)
            return y @ Wo.T
        for i in range(NUM_LAYERS):
            x = mamba_block(layer_norm(x, ln_w[i], ln_b[i]), W_in[i], conv_w[i], conv_b[i], W_x[i], W_dt[i], b_dt[i], A_log[i], Dp[i], W_out[i]) + x
        return x

    def _L0_xattn_ref(Q, K, V, mask, W_Q, W_K, W_V, W_O):
        import jax, jax.numpy as jnp
        import numpy as np
        import math
        D_MODEL = 128
        H = 16
        D_K = D_MODEL // H
        B, S1, _ = Q.shape
        S2 = K.shape[1]
        q = (Q @ W_Q).reshape(B, S1, H, D_K).transpose(0, 2, 1, 3)
        k = (K @ W_K).reshape(B, S2, H, D_K).transpose(0, 2, 1, 3)
        v = (V @ W_V).reshape(B, S2, H, D_K).transpose(0, 2, 1, 3)
        scores = jnp.einsum('bhqd,bhkd->bhqk', q, k) / math.sqrt(D_K)
        scores = jnp.where(mask[:, None, :, :] == 0, jnp.float32(-1000000000.0), scores)
        attn = jax.nn.softmax(scores, axis=-1)
        out = jnp.einsum('bhqk,bhkd->bhqd', attn, v)
        out = out.transpose(0, 2, 1, 3).reshape(B, S1, D_MODEL)
        return out @ W_O

    def _L0_ffn_ref(x, Wg, W1, b1, W2, b2):
        import jax, jax.numpy as jnp
        import numpy as np
        E = 8
        K = 2
        CAP_RATIO = 1.05
        B, S, D = x.shape
        T = B * S
        xf = x.reshape(T, D)
        gates = jax.nn.softmax(xf @ Wg.T, axis=-1)
        topw, topi = jax.lax.top_k(gates, K)
        C = int(round(K * T * CAP_RATIO / E))
        e_ord = topi.T.reshape(-1)
        tok_ord = jnp.tile(jnp.arange(T), K)
        oh = jax.nn.one_hot(e_ord, E, dtype=jnp.int32)
        cnt = jnp.take_along_axis(jnp.cumsum(oh, 0) - oh, e_ord[:, None], 1)[:, 0]
        within = cnt < C
        pos = jnp.where(within, cnt, C)
        x_disp = xf[tok_ord]
        buf = jnp.zeros((E, C + 1, D), xf.dtype).at[e_ord, pos].add(x_disp)[:, :C]
        h = jax.nn.gelu(jnp.einsum('ecd,edh->ech', buf, W1) + b1[:, None, :], approximate=False)
        y = jnp.einsum('ech,ehd->ecd', h, W2) + b2[:, None, :]
        y_ord = y[e_ord, jnp.minimum(pos, C - 1)] * within[:, None].astype(y.dtype)
        y_tk = y_ord.reshape(K, T, D).transpose(1, 0, 2)
        cw = topw * within.reshape(K, T).T.astype(topw.dtype)
        out = jnp.einsum('tk,tkd->td', cw, y_tk)
        return out.reshape(B, S, D)

    def _L1_attn_ref(x, w_qkv, w_out, rel_emb):
        import jax, jax.numpy as jnp
        import numpy as np
        import math
        NUM_HEADS = 16
        MAX_REL = 64
        LOCAL_WINDOW = 32
        B, L, D = x.shape
        H = NUM_HEADS
        hd = D // H
        qkv = (x @ w_qkv.T).reshape(B, L, 3, H, hd)
        q = jnp.transpose(qkv[:, :, 0], (0, 2, 1, 3))
        k = jnp.transpose(qkv[:, :, 1], (0, 2, 1, 3))
        v = jnp.transpose(qkv[:, :, 2], (0, 2, 1, 3))
        content = jnp.einsum('bhid,bhjd->bhij', q, k)
        qE = jnp.einsum('bhld,rd->bhlr', q, rel_emb)
        idx = jnp.arange(L)
        rel_idx = jnp.clip(idx[None, :] - idx[:, None], -MAX_REL, MAX_REL) + MAX_REL
        rel_scores = jnp.take_along_axis(qE, rel_idx[None, None, :, :], axis=3)
        scores = (content + rel_scores) / math.sqrt(hd)
        i = idx[:, None]
        j = idx[None, :]
        mask = (j > i) | (i - j >= LOCAL_WINDOW)
        scores = jnp.where(mask[None, None], -jnp.inf, scores)
        attn = jax.nn.softmax(scores, axis=-1)
        out = jnp.einsum('bhij,bhjd->bhid', attn, v)
        out = jnp.transpose(out, (0, 2, 1, 3)).reshape(B, L, D)
        return out @ w_out.T

    def _L1_xattn_ref(x, w1, v1, w2):
        import jax, jax.numpy as jnp
        import numpy as np
        E, TPE, H, F = (64, 64, 128, 128)
        h1 = jnp.einsum('eth,efh->etf', x, w1)
        h2 = jnp.einsum('eth,efh->etf', x, v1)
        g = jax.nn.gelu(h1, approximate=False) * h2
        return jnp.einsum('etf,efh->eth', g, w2)

    def _L1_ffn_ref(x, ln_scale, ln_bias, attn_w, attn_b, gate_w, w1, b1, w2, b2, next_w, next_b):
        import jax, jax.numpy as jnp
        import numpy as np
        MICRO_BATCHES = 2
        TOP_K = 2
        NUM_EXPERTS = 8
        B, S, D = (4, 512, 128)
        H = 4 * D
        b, s, d = x.shape
        flat = x.reshape(b * s, d)
        mu = jnp.mean(flat, axis=-1, keepdims=True)
        var = jnp.mean((flat - mu) ** 2, axis=-1, keepdims=True)
        xn = (flat - mu) * jax.lax.rsqrt(var + 1e-05) * ln_scale + ln_bias
        x_attn = xn @ attn_w.T + attn_b + flat
        logits = x_attn @ gate_w.T
        _vals, _idx = jax.lax.top_k(logits, TOP_K)
        e = w1.shape[0]
        n = b * s // (MICRO_BATCHES * e)
        xe = x_attn.reshape(MICRO_BATCHES, e, n, d)
        h = jax.nn.gelu(jnp.einsum('mend,edh->menh', xe, w1) + b1[None, :, None, :], approximate=False)
        eo = jnp.einsum('menh,ehd->mend', h, w2) + b2[None, :, None, :]
        eo = eo.reshape(b * s, d)
        out = jax.nn.gelu(eo @ next_w.T + next_b, approximate=False)
        return out.reshape(b, s, d)

    def _L2_attn_ref(x, Wq, Wk, Wv, Wo):
        import jax, jax.numpy as jnp
        import numpy as np
        B, S, DIM = (2, 1024, 128)
        NH, NKV, HD = (16, 4, 64)
        GROUPS = NH // NKV
        CHUNK = 128
        THETA = 10000.0

        def _slopes(h):
            return jnp.asarray([2.0 ** (-8.0 / h * (i + 1)) for i in range(h)], dtype=jnp.float32)

        def _rope_tables(s, d):
            inv = 1.0 / THETA ** (np.arange(0, d, 2, dtype=np.float64) / d)
            freqs = np.outer(np.arange(s, dtype=np.float64), inv)
            emb = np.concatenate([freqs, freqs], axis=-1)
            return (jnp.asarray(np.cos(emb), jnp.float32), jnp.asarray(np.sin(emb), jnp.float32))

        def _apply_rope(x, cos, sin):
            x1, x2 = jnp.split(x, 2, axis=-1)
            rot = jnp.concatenate([-x2, x1], axis=-1)
            return x * cos + rot * sin

        def _lightning_attn(q, k, v, slopes, chunk):
            b, h, s, d = q.shape
            nc = s // chunk
            t = jnp.arange(chunk, dtype=jnp.float32)
            sl = slopes[:, None, None]
            mask = jnp.where(t[:, None] >= t[None, :], jnp.exp(-sl * (t[:, None] - t[None, :])), 0.0)
            q_dec = jnp.exp(-slopes[:, None] * (t + 1.0))[..., None]
            k_dec = jnp.exp(-slopes[:, None] * (chunk - 1.0 - t))[..., None]
            blk_dec = jnp.exp(-slopes * chunk)[None, :, None, None]

            def to_chunks(x):
                return x.reshape(b, h, nc, chunk, d).transpose(2, 0, 1, 3, 4)
            qc, kc, vc = (to_chunks(q), to_chunks(k), to_chunks(v))

            def step(kv, inp):
                qi, ki, vi = inp
                scores = jnp.einsum('bhtd,bhsd->bhts', qi, ki) * mask
                o = jnp.einsum('bhts,bhsd->bhtd', scores, vi) + jnp.einsum('bhtd,bhde->bhte', qi * q_dec, kv)
                kv = blk_dec * kv + jnp.einsum('bhtd,bhte->bhde', ki * k_dec, vi)
                return (kv, o)
            kv0 = jnp.zeros((b, h, d, d), q.dtype)
            _, outs = jax.lax.scan(step, kv0, (qc, kc, vc))
            return outs.transpose(1, 2, 0, 3, 4).reshape(b, h, s, d)
        b, s, _ = x.shape
        q = (x @ Wq.T).reshape(b, s, NH, HD).transpose(0, 2, 1, 3)
        k = (x @ Wk.T).reshape(b, s, NKV, HD).transpose(0, 2, 1, 3)
        v = (x @ Wv.T).reshape(b, s, NKV, HD).transpose(0, 2, 1, 3)
        cos, sin = _rope_tables(s, HD)
        q = _apply_rope(q, cos, sin)
        k = _apply_rope(k, cos, sin)
        k = jnp.repeat(k, GROUPS, axis=1)
        v = jnp.repeat(v, GROUPS, axis=1)
        out = _lightning_attn(q, k, v, _slopes(NH), CHUNK)
        out = out.transpose(0, 2, 1, 3).reshape(b, s, NH * HD)
        return out @ Wo.T

    def _L2_xattn_ref(xq, xk, xv, Wq, bq, Wk, bk, Wv, bv, Wo):
        import jax, jax.numpy as jnp
        import numpy as np
        EMBED = 128
        HEADS = 16
        HEAD_DIM = EMBED // HEADS
        B, N, _ = xq.shape
        M = xk.shape[1]
        scale = HEAD_DIM ** (-0.5)
        q = (xq @ Wq.T + bq).reshape(B, N, HEADS, HEAD_DIM).transpose(0, 2, 1, 3)
        k = (xk @ Wk.T + bk).reshape(B, M, HEADS, HEAD_DIM).transpose(0, 2, 1, 3)
        v = (xv @ Wv.T + bv).reshape(B, M, HEADS, HEAD_DIM).transpose(0, 2, 1, 3)
        scores = jnp.einsum('bhnd,bhmd->bhnm', q, k) * scale
        weights = jax.nn.softmax(scores, axis=-1)
        out = jnp.einsum('bhnm,bhmd->bhnd', weights, v)
        out = out.transpose(0, 2, 1, 3).reshape(B, N, EMBED)
        return out @ Wo.T

    def _L2_ffn_ref(x, Wg, w1, w2):
        import jax, jax.numpy as jnp
        import numpy as np
        B, T, D = (1, 256, 128)
        E, DFF = (8, 512)

        def _gating(logits):
            S, num_e = logits.shape
            gates = jax.nn.softmax(logits.astype(jnp.float32), axis=1)
            idx1 = jnp.argmax(gates, axis=1)
            mask1 = jax.nn.one_hot(idx1, num_e, dtype=jnp.int32)
            logits_ex1 = jnp.where(mask1.astype(bool), -jnp.inf, logits)
            idx2 = jnp.argmax(logits_ex1, axis=1)
            mask2 = jax.nn.one_hot(idx2, num_e, dtype=jnp.int32)
            loc1 = jnp.cumsum(mask1, axis=0) - 1
            loc2 = jnp.cumsum(mask2, axis=0) - 1 + jnp.sum(mask1, axis=0, keepdims=True)
            loc1_s = jnp.sum(loc1 * mask1, axis=1)
            loc2_s = jnp.sum(loc2 * mask2, axis=1)
            g1 = jnp.sum(gates * mask1, axis=1)
            g2 = jnp.sum(gates * mask2, axis=1)
            denom = jnp.maximum(g1 + g2, jnp.finfo(jnp.float32).eps)
            g1, g2 = (g1 / denom, g2 / denom)
            cap = S
            loc1_sc = jax.nn.one_hot(loc1_s, cap, dtype=jnp.float32)
            loc2_sc = jax.nn.one_hot(loc2_s, cap, dtype=jnp.float32)
            combine = (g1[:, None] * mask1)[:, :, None] * loc1_sc[:, None, :] + (g2[:, None] * mask2)[:, :, None] * loc2_sc[:, None, :]
            dispatch_mask = combine != 0
            return (combine.astype(logits.dtype), dispatch_mask)
        d_model = x.shape[2]
        xs = x.reshape(-1, d_model)
        logits = xs @ Wg
        combine, dispatch_mask = _gating(logits)
        dispatched = jnp.einsum('sec,sm->ecm', dispatch_mask.astype(jnp.float32), xs)
        expert_out = jax.nn.relu(dispatched @ w1) @ w2
        out = jnp.einsum('sec,ecm->sm', combine, expert_out)
        return out.reshape(x.shape)

    def _L3_attn_ref(x, wq, wk, wv, wo):
        import math
        import jax, jax.numpy as jnp
        import numpy as np
        B, T, D_MODEL = (4, 128, 128)
        N_HEADS = 16
        HEAD_DIM = D_MODEL // N_HEADS
        TOP_K = 64

        def _scatter_last(base, idx, vals):
            d = base.shape[-1]
            k = idx.shape[-1]
            fb = base.reshape(-1, d)
            fi = idx.reshape(-1, k)
            fv = vals.reshape(-1, k)
            rows = jnp.arange(fb.shape[0])[:, None]
            return fb.at[rows, fi].set(fv).reshape(base.shape)

        def _sparsify_last_dim_topk(x, keep_k):
            if keep_k >= x.shape[-1]:
                return x
            _, idx = jax.lax.top_k(jnp.abs(x), keep_k)
            vals = jnp.take_along_axis(x, idx, axis=-1)
            return _scatter_last(jnp.zeros_like(x), idx, vals)

        def _forward(x, wq, wk, wv, wo):
            Bx, Tx, C = x.shape
            k_keep = min(TOP_K, Tx)
            feature_keep = min(HEAD_DIM, max(1, math.ceil(HEAD_DIM * (k_keep / Tx))))

            def proj(w):
                y = jnp.einsum('btc,dc->btd', x, w)
                return y.reshape(Bx, Tx, N_HEADS, HEAD_DIM).transpose(0, 2, 1, 3)
            q = _sparsify_last_dim_topk(proj(wq), feature_keep)
            k = _sparsify_last_dim_topk(proj(wk), feature_keep)
            v = _sparsify_last_dim_topk(proj(wv), feature_keep)
            scores = jnp.einsum('bhqd,bhkd->bhqk', q, k) / math.sqrt(HEAD_DIM)
            causal = jnp.triu(jnp.ones((Tx, Tx), dtype=bool), k=1)
            neg_inf = jnp.float32(-jnp.inf)
            scores = jnp.where(causal[None, None], neg_inf, scores)
            topk_vals, topk_idx = jax.lax.top_k(scores, k_keep)
            sparse_scores = _scatter_last(jnp.full_like(scores, neg_inf), topk_idx, topk_vals)
            attn = jax.nn.softmax(sparse_scores, axis=-1)
            out = jnp.einsum('bhqk,bhkd->bhqd', attn, v)
            out = out.transpose(0, 2, 1, 3).reshape(Bx, Tx, C)
            return jnp.einsum('btc,dc->btd', out, wo)
        return _forward(x, wq, wk, wv, wo)

    def _L3_xattn_ref(query_states, key_value_states, Wq, bq, Wk, bk, Wv, bv, Wo, bo):
        import jax, jax.numpy as jnp
        import numpy as np
        HIDDEN = 128
        NUM_HEADS = 16
        HEAD_DIM = HIDDEN // NUM_HEADS
        SCALE = 1.0 / float(np.sqrt(HEAD_DIM))
        B, SQ, _ = query_states.shape
        _, SKV, _ = key_value_states.shape
        q = query_states @ Wq.T + bq
        k = key_value_states @ Wk.T + bk
        v = key_value_states @ Wv.T + bv
        q = q.reshape(B, SQ, NUM_HEADS, HEAD_DIM).transpose(0, 2, 1, 3) * SCALE
        k = k.reshape(B, SKV, NUM_HEADS, HEAD_DIM).transpose(0, 2, 1, 3)
        v = v.reshape(B, SKV, NUM_HEADS, HEAD_DIM).transpose(0, 2, 1, 3)
        scores = jnp.einsum('bhqd,bhkd->bhqk', q, k)
        attn = jax.nn.softmax(scores, axis=-1)
        ctx = jnp.einsum('bhqk,bhkd->bhqd', attn, v)
        ctx = ctx.transpose(0, 2, 1, 3).reshape(B, SQ, HIDDEN)
        return ctx @ Wo.T + bo

    def _L3_ffn_ref(x, weights, scale, bias):
        import jax, jax.numpy as jnp
        import numpy as np
        MAX_VAL = 100.0
        w = (weights >= 0.0).astype(x.dtype) * 2.0 - 1.0
        y = jnp.einsum('bsi,oi->bso', x, w)
        y = y * scale + bias
        y = jnp.clip(y, -MAX_VAL, MAX_VAL)
        return y
    x = _layernorm(x + _L0_attn_ref(x, L0_attn_W_in, L0_attn_conv_w, L0_attn_conv_b, L0_attn_W_x, L0_attn_W_dt, L0_attn_b_dt, L0_attn_A_log, L0_attn_Dp, L0_attn_W_out, L0_attn_ln_w, L0_attn_ln_b), axis=-1)
    x = _layernorm(x + _L0_xattn_ref(x, ctx_1024, ctx_1024, mask_BxSxS2_if1, L0_xattn_W_Q, L0_xattn_W_K, L0_xattn_W_V, L0_xattn_W_O), axis=-1)
    x = _layernorm(x + _L0_ffn_ref(x, L0_ffn_Wg, L0_ffn_W1, L0_ffn_b1, L0_ffn_W2, L0_ffn_b2), axis=-1)
    x = _layernorm(x + _L1_attn_ref(x, L1_attn_w_qkv, L1_attn_w_out, L1_attn_rel_emb), axis=-1)
    x = _layernorm(x + _L1_xattn_ref(x, ctx_1024, ctx_1024, ctx_1024), axis=-1)
    x = _layernorm(x + _L1_ffn_ref(x, L1_ffn_ln_scale, L1_ffn_ln_bias, L1_ffn_attn_w, L1_ffn_attn_b, L1_ffn_gate_w, L1_ffn_w1, L1_ffn_b1, L1_ffn_w2, L1_ffn_b2, L1_ffn_next_w, L1_ffn_next_b), axis=-1)
    x = _layernorm(x + _L2_attn_ref(x, L2_attn_Wq, L2_attn_Wk, L2_attn_Wv, L2_attn_Wo), axis=-1)
    x = _layernorm(x + _L2_xattn_ref(x, ctx_1024, ctx_1024, L2_xattn_Wq, L2_xattn_bq, L2_xattn_Wk, L2_xattn_bk, L2_xattn_Wv, L2_xattn_bv, L2_xattn_Wo), axis=-1)
    x = _layernorm(x + _L2_ffn_ref(x, L2_ffn_Wg, L2_ffn_w1, L2_ffn_w2), axis=-1)
    x = _layernorm(x + _L3_attn_ref(x, L3_attn_wq, L3_attn_wk, L3_attn_wv, L3_attn_wo), axis=-1)
    x = _layernorm(x + _L3_xattn_ref(x, ctx_1024, L3_xattn_Wq, L3_xattn_bq, L3_xattn_Wk, L3_xattn_bk, L3_xattn_Wv, L3_xattn_bv, L3_xattn_Wo, L3_xattn_bo), axis=-1)
    x = _layernorm(x + _L3_ffn_ref(x, L3_ffn_weights, L3_ffn_scale, L3_ffn_bias), axis=-1)
    return x

_drawn_inputs = setup_inputs


def setup_inputs(seed=0):
    import zlib

    import numpy as np

    out = dict(_drawn_inputs(seed))
    spreads = {'L0_attn_conv_b': (0.0, 0.8),
     'L0_attn_b_dt': (-4.599999904632568, 0.6),
     'L0_attn_Dp': (1.0, 0.6),
     'L0_attn_ln_w': (1.0, 0.6),
     'L0_attn_ln_b': (0.0, 0.8),
     'L0_ffn_b1': (0.0, 0.8),
     'L0_ffn_b2': (0.0, 0.316),
     'L1_ffn_ln_scale': (1.0, 0.6),
     'L1_ffn_ln_bias': (0.0, 0.8),
     'L1_ffn_attn_b': (0.0, 0.8),
     'L1_ffn_b1': (0.0, 0.8),
     'L1_ffn_b2': (0.0, 0.427),
     'L1_ffn_next_b': (0.0, 0.268),
     'L2_xattn_bq': (0.0, 0.329),
     'L2_xattn_bk': (0.0, 2.0),
     'L2_xattn_bv': (0.0, 0.1),
     'L3_xattn_bq': (0.0, 2.0),
     'L3_xattn_bk': (0.0, 2.0),
     'L3_xattn_bv': (0.0, 0.333),
     'L3_xattn_bo': (0.0, 0.1),
     'L3_ffn_scale': (1.0, 0.2)}
    factors = {'L0_attn_W_in': 8.0,
     'L0_attn_conv_w': 8.0,
     'L0_attn_W_x': 8.0,
     'L0_attn_W_dt': 8.0,
     'L0_attn_A_log': 8.0,
     'L0_attn_W_out': 8.0,
     'L0_ffn_W1': 4.566,
     'L0_ffn_W2': 4.064,
     'L1_ffn_attn_w': 8.0,
     'L1_ffn_w1': 6.56,
     'L1_ffn_w2': 5.765,
     'L1_ffn_next_w': 2.836,
     'L2_ffn_Wg': 64.0,
     'L3_attn_wq': 36.491,
     'L3_attn_wk': 33.544,
     'L3_xattn_Wq': 8.0,
     'L3_xattn_Wk': 8.0}
    for name, (base, spread) in spreads.items():
        noise = np.random.default_rng([zlib.crc32(name.encode()), seed]).standard_normal(out[name].shape)
        drawn = base * np.exp(spread * noise) if base else spread * noise
        out[name] = jnp.asarray(drawn.astype(out[name].dtype))
    for name, factor in factors.items():
        out[name] = (out[name] * factor).astype(out[name].dtype)
    return out
```

```python
import concourse.bass as bass
from concourse import mybir
from contextlib import ExitStack

F32 = mybir.dt.float32
I32 = mybir.dt.int32
BF16 = mybir.dt.bfloat16
ALU = mybir.AluOpType
ACT = mybir.ActivationFunctionType
AX = mybir.AxisListType

P = 128
B = 4
S = 512
TB = S // P
NT = B * TB
EPS = 1e-5
H = 16
HD = P // H
SK = 77
STAGES = range(12)
FIRST_SEM = 110


class Chain:

    def __init__(self, eng, sem):
        self.eng, self.sem, self.n = eng, sem, 0

    def __call__(self, ins):
        self.n += 1
        ins.then_inc(self.sem, 1)
        self.eng.wait_ge(self.sem, self.n)

    def mark(self, ins):
        self.n += 1
        ins.then_inc(self.sem, 1)
        return self.n

    def wait_for(self, n):
        self.eng.wait_ge(self.sem, n)


def semaphores(nc, ctx, names):
    names = names.split()
    handles = [ctx.enter_context(nc.semaphore(n, num=FIRST_SEM + i)) for i, n in enumerate(names)]
    return dict(zip(names, handles), numbers=range(FIRST_SEM, FIRST_SEM + len(names)))


def layer_norm_stats(v, chain, src, st, mv, tiles, s_var):
    for t in range(tiles):
        ins = v.bn_stats(st[:, t, :], src[:, t, :])
    chain(ins)
    for t in range(tiles):
        ins = v.bn_aggr(mv[:, t, :], st[:, t, :])
    ins.then_inc(s_var, 1)


def mamba(nc, env):
    DI, NS, R, K = 256, 16, 8, 4
    NF = DI // P
    X = env.X
    cols, at = {}, 0
    NX = 3 * 2 * NS
    for name, n in (("wi", 2 * DI), ("wx", NF * (R + 2 * NS)), ("wo", NF * P), ("pc", NF * (K + 3 + NS)), ("ln", 2)):
        cols[name] = (at, at + n)
        at += n
    with ExitStack() as ctx:
        sb = lambda n, s, t=F32: ctx.enter_context(nc.sbuf_tensor(n, s, t))
        wl = sb("mamba_w", [P, at])
        wdt = sb("mamba_wdt", [R, DI])
        sel32 = sb("state_selector_f32", [NX, 2 * NS, P])
        sel = sb("state_selector", [NX, 2 * NS, P], BF16)
        wx3 = sb("wx_three_times", [P, NF, NX])
        X0 = sb("x_before_mamba", [P, NT, P])
        xh = sb("x_normed", [P, NT, P])
        st = sb("bn_stats", [P, NT, 6])
        mv = sb("mean_var", [P, NT, 2])
        sd = sb("std", [P, NT])
        rs = sb("rstd", [P, NT])
        xn = sb("xn_t", [P, B, S])
        xp = sb("xs_padded", [P, 2, NF, K - 1 + S])
        sz = sb("silu_z", [P, B, NF, S])
        cv = sb("conv", [P, 2, NF, S])
        u = sb("u", [P, B, NF, S])
        xd = sb("dt_low_rank", [R, B, S])
        bc = sb("b_c_rows", [NX, 2, S])
        bcp = sb("b_c_part", [NX, S], BF16)
        bc3 = sb("b_c_parts", [NX, B, S], BF16)
        dt = sb("dt", [P, B, NF, S])
        dtu = sb("dtu", [P, B, NF, S])
        an = sb("a_neg", [P, NF, NS])
        dA = sb("dA", [P, 4, S])
        dBu = sb("dBu", [P, 3, S])
        hs = sb("h_states", [P, 4, S])
        cs = sb("c_copy", [P, 2, S])
        hc = cv[:, :, :, :].rearrange("p a f s -> p (a f) s")
        yt = sb("y_t", [P, NF, S])
        ps = env.banks
        s = semaphores(nc, ctx, "m_w m_var m_sd m_vc m_xh m_xt m_xn m_pj m_pje m_cv m_u m_xd m_xde m_dtp m_v m_e m_l m_dt "
                          "m_wx m_bcx m_bce m_bcs m_ae m_a m_bc m_da m_dbu m_cs m_hs m_hc m_yt m_o m_sel m_xa m_ga m_ra")
        wi = wl[:, cols["wi"][0]:cols["wi"][1]]
        wx = wl[:, cols["wx"][0]:cols["wx"][1]].rearrange("p (f n) -> p f n", f=NF)
        wo = wl[:, cols["wo"][0]:cols["wo"][1]].rearrange("p (f n) -> p f n", f=NF)
        pc = wl[:, cols["pc"][0]:cols["pc"][1]].rearrange("p (f n) -> p f n", f=NF)
        lnw, lnb = (wl[:, cols["ln"][0] + i:cols["ln"][0] + i + 1] for i in range(2))
        CB, BDT, DP, AL = K, K + 1, K + 2, K + 3
        psB, psC = ps[0:2], ps[2:4]
        psY = lambda b, f: ps[4 + 2 * (b % 2) + f]

        with nc.Block() as block:
            @block.sync
            def _(sp_):
                sp_.dma_start(sel32[:, :, :], env.d["mamba_sel"]).then_inc(s["m_sel"], 16)
                sp_.wait_ge(s["m_sel"], 16)

            @block.vector
            def _(v):
                v.tensor_copy(X0[:, :, :], X[:, :, :])
                v.memset(xp[:, :, :, :], 0.0)
                v.wait_ge(s["m_sel"], 16)
                v.tensor_copy(sel[:, :, :], sel32[:, :, :])
        nc.all_engine_barrier(sems_to_clear=s["numbers"])

        with nc.Fori(0, env.mamba_layers) as layer:
            with nc.Block() as block:
                @block.sync
                def _(sp_):
                    sp_.dma_start(wl[:, :], env.d["mamba_w"][bass.ds(layer, 1), :, :].rearrange("o p n -> p (o n)"))\
                        .then_inc(s["m_w"], 16)
                    sp_.dma_start(wdt[:, :], env.d["mamba_wdt"][bass.ds(layer, 1), :, :].rearrange("o p n -> p (o n)"))\
                        .then_inc(s["m_w"], 16)

                @block.vector
                def _(v):
                    chain = Chain(v, s["m_vc"])
                    layer_norm_stats(v, chain, X, st, mv, NT, s["m_var"])
                    v.wait_ge(s["m_sd"], 1)
                    chain(v.reciprocal(rs[:, :], sd[:, :]))
                    for t in range(NT):
                        v.tensor_scalar(xh[:, t, :], X[:, t, :], mv[:, t, 0:1], rs[:, t:t + 1],
                                        ALU.subtract, ALU.mult).then_inc(s["m_xh"], 1)
                    v.wait_ge(s["m_w"], 32)
                    for b in range(B):
                        for f in range(NF):
                            v.wait_ge(s["m_xa"], NF * b + f + 1)
                            if b >= 2:
                                v.wait_ge(s["m_u"], NF * (b - 2) + f + 1)
                            c = cv[:, b % 2, f, :]
                            chain(v.tensor_scalar(c, xp[:, b % 2, f, 0:S], pc[:, f, 0:1], pc[:, f, CB:CB + 1],
                                                  ALU.mult, ALU.add))
                            for k in range(1, K):
                                ins = v.scalar_tensor_tensor(out=c, in0=xp[:, b % 2, f, k:k + S],
                                                             scalar=pc[:, f, k:k + 1], in1=c,
                                                             op0=ALU.mult, op1=ALU.add)
                                if k < K - 1:
                                    chain(ins)
                            ins.then_inc(s["m_cv"], 1)
                        v.wait_ge(s["m_bce"], b + 1)
                        x = bc[:, b % 2, :]
                        T = 2 * NS
                        for k in range(3):
                            chain(v.tensor_copy(bcp[:, :], x))
                            chain(v.tensor_copy(bc3[k * T:(k + 1) * T, b, :], bcp[k * T:(k + 1) * T, :]))
                            if k < 2:
                                chain(v.tensor_tensor(x, x, bcp[:, :], ALU.subtract))
                        v.sem_inc(s["m_bcs"], 1)
                    v.wait_ge(s["m_ae"], 1)
                    v.tensor_scalar(an[:, :, :], an[:, :, :], -1.0, None, ALU.mult).then_inc(s["m_a"], 1)

                    v.wait_ge(s["m_u"], NF * B)
                    for i in range(B * NF):
                        b, f = divmod(i, NF)
                        v.wait_ge(s["m_dtp"], i + 1)
                        chain(v.tensor_scalar(dt[:, b, f, :], ps[i % 4][:, :], pc[:, f, BDT:BDT + 1], None, ALU.add))
                        v.scalar_tensor_tensor(out=dtu[:, b, f, :], in0=dt[:, b, f, :], scalar=-1.0,
                                               in1=dt[:, b, f, :], op0=ALU.mult, op1=ALU.max).then_inc(s["m_v"], 1)

                    def softplus_out(i):
                        b, f = divmod(i, NF)
                        v.wait_ge(s["m_l"], i + 1)
                        chain(v.scalar_tensor_tensor(out=dt[:, b, f, :], in0=dt[:, b, f, :], scalar=0.0,
                                                     in1=dtu[:, b, f, :], op0=ALU.max, op1=ALU.add))
                        v.tensor_tensor(dtu[:, b, f, :], dt[:, b, f, :], u[:, b, f, :], ALU.mult).then_inc(s["m_dt"], 1)

                    for i in range(NF):
                        softplus_out(i)

                    def gate(b):
                        for f in range(NF):
                            v.wait_ge(s["m_ga"], NF * (NS * b + NS - 1) + f + 1)
                            if b >= 1:
                                v.wait_ge(s["m_o"], b)
                            chain(v.scalar_tensor_tensor(out=yt[:, f, :], in0=u[:, b, f, :], scalar=pc[:, f, DP:DP + 1],
                                                         in1=psY(b, f)[:, :], op0=ALU.mult, op1=ALU.add))
                            v.tensor_tensor(yt[:, f, :], yt[:, f, :], sz[:, b, f, :], ALU.mult).then_inc(s["m_yt"], 1)

                    def residual(b):
                        v.wait_ge(s["m_o"], b + 1)
                        v.tensor_tensor(X[:, TB * b:TB * b + TB, :], X[:, TB * b:TB * b + TB, :],
                                        psY(b, 0)[:, :].rearrange("p (c n) -> p c n", c=TB), ALU.add)\
                            .then_inc(s["m_ra"], 1)

                    def input_term(i):
                        j, f = divmod(i, NF)
                        b, n = divmod(j, NS)
                        v.wait_ge(s["m_bc"], j + 1)
                        if i >= 3:
                            v.wait_ge(s["m_hs"], i - 2)
                        v.tensor_tensor(dBu[:, i % 3, :], psB[n % 2][:, :], dtu[:, b, f, :], ALU.mult)\
                            .then_inc(s["m_dbu"], 1)

                    def scan(i):
                        v.wait_ge(s["m_dbu"], i + 1)
                        v.wait_ge(s["m_da"], i + 1)
                        if i >= 4:
                            v.wait_ge(s["m_hc"], i - 3)
                        v.tensor_tensor_scan(hs[:, i % 4, :], dA[:, i % 4, :], dBu[:, i % 3, :], 0.0,
                                             ALU.mult, ALU.add).then_inc(s["m_hs"], 1)

                    for i in range(B * NS * NF):
                        j, f = divmod(i, NF)
                        b, n = divmod(j, NS)
                        if f == 0 and n == 8 and b + 1 < B:
                            softplus_out(NF * b + NF)
                            softplus_out(NF * b + NF + 1)
                            v.wait_ge(s["m_dt"], NF * (b + 2))
                        if i == 0:
                            v.wait_ge(s["m_dt"], NF)
                        input_term(i)
                        if i >= 1:
                            scan(i - 1)
                        if f == 1 and b >= 1 and n == 2:
                            gate(b - 1)
                        if f == 1 and b >= 1 and n == 6:
                            residual(b - 1)
                    scan(B * NS * NF - 1)
                    gate(B - 1)
                    residual(B - 1)

                @block.gpsimd
                def _(g):
                    for i in range(B * NS * NF):
                        g.wait_ge(s["m_hs"], i + 1)
                        g.wait_ge(s["m_cs"], i // NF + 1)
                        if i >= 4:
                            g.wait_ge(s["m_ga"], i - 3)
                        g.tensor_tensor(hc[:, i % 4, :], hs[:, i % 4, :], cs[:, (i // NF) % 2, :], ALU.mult)\
                            .then_inc(s["m_hc"], 1)

                @block.scalar
                def _(a):
                    a.wait_ge(s["m_var"], 1)
                    a.activation(sd[:, :], mv[:, :, 1], ACT.Sqrt, bias=env.eps[:, 0:1]).then_inc(s["m_sd"], 1)
                    a.wait_ge(s["m_w"], 32)
                    for x in range(3):
                        ins = a.activation(wx3[:, :, 2 * NS * x:2 * NS * (x + 1)], wx[:, :, R:], ACT.Copy)
                    ins.then_inc(s["m_wx"], 1)

                    def normed(b):
                        a.wait_ge(s["m_xt"], b + 1)
                        a.activation(xn[:, b, :], ps[4 + b % 2][:, :], ACT.Identity, scale=lnw, bias=lnb)\
                            .then_inc(s["m_xn"], 1)

                    normed(0)
                    for b in range(B):
                        if b + 1 < B:
                            normed(b + 1)
                        for m in range(4):
                            a.wait_ge(s["m_pj"], 4 * b + m + 1)
                            if m < NF:
                                if b >= 2:
                                    a.wait_ge(s["m_cv"], NF * (b - 2) + m + 1)
                                a.activation(xp[:, b % 2, m, K - 1:K - 1 + S], ps[m][:, :], ACT.Copy)\
                                    .then_inc(s["m_xa"], 1)
                            else:
                                a.activation(sz[:, b, m - NF, :], ps[m][:, :], ACT.Silu).then_inc(s["m_pje"], 1)
                        for f in range(NF):
                            a.wait_ge(s["m_cv"], NF * b + f + 1)
                            a.activation(u[:, b, f, :], cv[:, b % 2, f, :], ACT.Silu).then_inc(s["m_u"], 1)
                        a.wait_ge(s["m_xd"], b + 1)
                        a.activation(xd[:, b, :], ps[6][0:R, :], ACT.Copy).then_inc(s["m_xde"], 1)
                        if b >= 2:
                            a.wait_ge(s["m_bcs"], b - 1)
                        a.activation(bc[:, b % 2, :], ps[7][0:NX, :], ACT.Copy).then_inc(s["m_bce"], 1)
                    a.activation(an[:, :, :], pc[:, :, AL:AL + NS], ACT.Exp).then_inc(s["m_ae"], 1)
                    for i in range(B * NF):
                        a.wait_ge(s["m_v"], i + 1)
                        x = dtu[:, i // NF, i % NF, :]
                        a.activation(x, x, ACT.Exp, scale=-1.0).then_inc(s["m_e"], 1)
                    for i in range(B * NF):
                        a.wait_ge(s["m_e"], i + 1)
                        x = dtu[:, i // NF, i % NF, :]
                        a.activation(x, x, ACT.Ln, bias=env.one[:, 0:1]).then_inc(s["m_l"], 1)
                    a.wait_ge(s["m_a"], 1)
                    for j in range(B * NS):
                        b, n = divmod(j, NS)
                        for f in range(NF):
                            i = j * NF + f
                            a.wait_ge(s["m_dt"], NF * b + f + 1)
                            if i >= 4:
                                a.wait_ge(s["m_hs"], i - 3)
                            a.activation(dA[:, i % 4, :], dt[:, b, f, :], ACT.Exp, scale=an[:, f, n:n + 1])\
                                .then_inc(s["m_da"], 1)
                        a.wait_ge(s["m_bc"], j + 1)
                        if j >= 2:
                            a.wait_ge(s["m_hc"], NF * (j - 1))
                        a.activation(cs[:, j % 2, :], psC[j % 2][:, :], ACT.Copy).then_inc(s["m_cs"], 1)

                @block.tensor
                def _(t):
                    t.wait_ge(s["m_w"], 32)

                    def turn(b):
                        if b >= 2:
                            t.wait_ge(s["m_xn"], b - 1)
                        for c in range(TB):
                            t.wait_ge(s["m_xh"], TB * b + c + 1)
                            ins = t.transpose(ps[4 + b % 2][:, c * P:(c + 1) * P], xh[:, TB * b + c, :], env.ident[:, :])
                        ins.then_inc(s["m_xt"], 1)

                    def project(b):
                        t.wait_ge(s["m_xn"], b + 1)
                        if b >= 1:
                            t.wait_ge(s["m_xa"], NF * b)
                            t.wait_ge(s["m_pje"], NF * b)
                        for m in range(4):
                            t.matmul(ps[m][:, :], wi[:, m * P:(m + 1) * P], xn[:, b, :],
                                     start=True, stop=True).then_inc(s["m_pj"], 1)

                    def x_dbl(b):
                        if b >= 1:
                            t.wait_ge(s["m_xde"], b)
                            t.wait_ge(s["m_bce"], b)
                        t.wait_ge(s["m_wx"], 1)
                        for f in range(NF):
                            t.wait_ge(s["m_u"], NF * b + f + 1)
                            t.matmul(ps[6][0:R, :], wx[:, f, 0:R], u[:, b, f, :], start=(f == 0), stop=(f == NF - 1))
                            ins = t.matmul(ps[7][0:NX, :], wx3[:, f, :], u[:, b, f, :], start=(f == 0), stop=(f == NF - 1))
                        ins.then_inc(s["m_xd"], 1)

                    turn(0)
                    turn(1)
                    for b in range(B):
                        project(b)
                        if b + 2 < B:
                            turn(b + 2)
                        if b >= 1:
                            x_dbl(b - 1)
                    x_dbl(B - 1)
                    t.wait_ge(s["m_pje"], NF * B)
                    t.wait_ge(s["m_xa"], NF * B)
                    for i in range(B * NF):
                        b, f = divmod(i, NF)
                        t.wait_ge(s["m_xde"], b + 1)
                        if i >= 4:
                            t.wait_ge(s["m_v"], i - 3)
                        t.matmul(ps[i % 4][:, :], wdt[:, f * P:(f + 1) * P], xd[0:R, b, :],
                                 start=True, stop=True).then_inc(s["m_dtp"], 1)
                    t.wait_ge(s["m_v"], B * NF)

                    def spread(j):
                        b, n = divmod(j, NS)
                        if j >= 2:
                            t.wait_ge(s["m_dbu"], NF * (j - 1))
                            t.wait_ge(s["m_cs"], j - 1)
                        t.matmul(psB[j % 2][:, :], sel[:, n, :], bc3[:, b, :], start=True, stop=True)
                        t.matmul(psC[j % 2][:, :], sel[:, NS + n, :], bc3[:, b, :], start=True, stop=True)\
                            .then_inc(s["m_bc"], 1)

                    def gather(i):
                        b, r = divmod(i, NF * NS)
                        n, f = divmod(r, NF)
                        t.wait_ge(s["m_hc"], i + 1)
                        if n == 0 and b >= 2:
                            t.wait_ge(s["m_ra"], b - 1)
                        t.matmul(psY(b, f)[:, :], env.ident[:, :], hc[:, i % 4, :], start=(n == 0), stop=(n == NS - 1))\
                            .then_inc(s["m_ga"], 1)

                    def out(b):
                        for c in range(TB):
                            for f in range(NF):
                                t.wait_ge(s["m_yt"], NF * b + f + 1)
                                ins = t.matmul(psY(b, 0)[:, c * P:(c + 1) * P], yt[:, f, c * P:(c + 1) * P],
                                               wo[:, f, :], start=(f == 0), stop=(f == NF - 1))
                        ins.then_inc(s["m_o"], 1)

                    t.wait_ge(s["m_bcs"], B)
                    spread(0)
                    for b in range(B):
                        for n in range(NS):
                            j = b * NS + n
                            if j + 1 < B * NS:
                                spread(j + 1)
                            for f in range(NF if j else 0):
                                gather(NF * (j - 1) + f)
                            if b >= 1 and n == 4:
                                out(b - 1)
                    for f in range(NF):
                        gather(NF * (B * NS - 1) + f)
                    out(B - 1)
            nc.all_engine_barrier(sems_to_clear=s["numbers"])

        with nc.Block() as block:
            finish_layer_norm(block, X, X0, xh, st, mv, sd, rs, NT, env, s["m_vc"], s["m_var"], s["m_sd"], s["m_v"])
        nc.all_engine_barrier(sems_to_clear=s["numbers"])


def finish_layer_norm(block, X, Y, R, st, mv, sd, rs, tiles, env, s_chain, s_var, s_sd, s_done):
    @block.vector
    def _(v):
        chain = Chain(v, s_chain)
        chain(v.tensor_tensor(R[:, :, :], X[:, :, :], Y[:, :, :], ALU.add))
        layer_norm_stats(v, chain, R, st, mv, tiles, s_var)
        v.wait_ge(s_sd, 1)
        chain(v.reciprocal(rs[:, :], sd[:, :]))
        for t in range(tiles):
            v.tensor_scalar(X[:, t, :], R[:, t, :], mv[:, t, 0:1], rs[:, t:t + 1], ALU.subtract, ALU.mult)\
                .then_inc(s_done, 1)

    @block.scalar
    def _(a):
        a.wait_ge(s_var, 1)
        a.activation(sd[:, :], mv[:, :, 1], ACT.Sqrt, bias=env.eps[:, 0:1]).then_inc(s_sd, 1)


def normalise(v, chain, sm, w, y, X):
    if len(y.shape) == 2:
        y = y[:, :].rearrange("p (c n) -> p c n", c=TB)
    chain(v.tensor_tensor(w.R[:, :, :], X[:, :, :], y[:, :, :], ALU.add))
    layer_norm_stats(v, chain, w.R, w.st, w.mv, TB, sm["var"])
    v.wait_ge(sm["sd"], 1)
    chain(v.reciprocal(w.rs[:, :], w.sd[:, :]))
    for c in range(TB):
        v.tensor_scalar(X[:, c, :], w.R[:, c, :], w.mv[:, c, 0:1], w.rs[:, c:c + 1],
                        ALU.subtract, ALU.mult).then_inc(sm["xn"], 1)


def turn_tokens(t, sm, X, bank, ident):
    for c in range(TB):
        t.wait_ge(sm["xn"], c + 1)
        ins = t.transpose(bank[:, c * P:(c + 1) * P], X[:, c, :], ident[:, :])
    ins.then_inc(sm["tr"], 1)


def std_and_turn(a, sm, w, XT, bank, eps):
    a.wait_ge(sm["var"], 1)
    a.activation(w.sd[:, :], w.mv[:, :, 1], ACT.Sqrt, bias=eps[:, 0:1]).then_inc(sm["sd"], 1)
    a.wait_ge(sm["tr"], 1)
    a.activation(XT[:, :], bank[:, :], ACT.Copy)


LN_SEMS = "var sd xn tr chain "


class Batch:

    def __init__(self, nc, ctx, banks, tag):
        sb = lambda n, s: ctx.enter_context(nc.sbuf_tensor(tag + n, s, F32))
        self.X = sb("tokens", [P, TB, P])
        self.XT = sb("t", [P, S])
        self.ctxT = sb("ctx_t", [P, SK])
        self.ctx = sb("ctx", [SK, P])
        self.R = sb("residual", [P, TB, P])
        self.st = sb("bn_stats", [P, TB, 6])
        self.mv = sb("mean_var", [P, TB, 2])
        self.sd = sb("std", [P, TB])
        self.rs = sb("rstd", [P, TB])
        self.ps = banks


def enter_batch(nc, env, w, b):
    with ExitStack() as ctx:
        s = semaphores(nc, ctx, "ctx_loaded copied turned")
        with nc.Block() as block:
            @block.sync
            def _(sp):
                sp.dma_start(w.ctxT[:, :], env.d["ctx_t"][bass.ds(b, 1), :, :].rearrange("o p n -> p (o n)")).then_inc(s["ctx_loaded"], 16)
                sp.dma_start(w.ctx[:, :], env.d["ctx"][bass.ds(b, 1), :, :].rearrange("o p n -> p (o n)")).then_inc(s["ctx_loaded"], 16)
                sp.wait_ge(s["ctx_loaded"], 32)

            @block.vector
            def _(v):
                v.tensor_copy(w.X[:, :, :], env.X[:, bass.ds(b * TB, TB), :]).then_inc(s["copied"], 1)

            @block.tensor
            def _(t):
                t.wait_ge(s["copied"], 1)
                for c in range(TB):
                    ins = t.transpose(w.ps[0][:, c * P:(c + 1) * P], w.X[:, c, :], env.ident[:, :])
                ins.then_inc(s["turned"], 1)

            @block.scalar
            def _(a):
                a.wait_ge(s["turned"], 1)
                a.activation(w.XT[:, :], w.ps[0][:, :], ACT.Copy)
        nc.all_engine_barrier(sems_to_clear=s["numbers"])


def leave_batch(nc, env, w, b):
    with nc.Block() as block:
        @block.vector
        def _(v):
            v.tensor_copy(env.X[:, bass.ds(b * TB, TB), :], w.X[:, :, :])


def cross_attention(nc, env, w, pre, b, scale, masked, biased, out_bias):
    wt = env.weights[pre]
    cols = env.columns.get(pre)
    rows = env.rows.get(pre)
    GH = (0, 6, 12, 16)
    NG = len(GH) - 1
    X, XT, ps = w.X, w.XT, w.ps
    with ExitStack() as ctx:
        sb = lambda n, s, t=F32: ctx.enter_context(nc.sbuf_tensor(pre + n, s, t))
        kt = sb("k_t", [P, SK])
        kb = sb("k_by_head", [P, H, SK])
        vv = sb("v", [SK, P])
        qt = sb("q_t", [P, S])
        D = sb("scores", [P, 2, H, SK])
        mx = sb("max", [P, 2, H])
        zs = sb("sum", [P, 2, H])
        pt = sb("p_t", [SK, H, P])
        o = sb("o", [P, 2, P])
        ot = sb("o_t", [P, 2, P])
        if masked:
            mi = sb("mask_int", [P, TB, SK], I32)
            mf = sb("mask", [P, TB, SK])
            pen = sb("penalty", [P, TB, SK])
        s = semaphores(nc, ctx, LN_SEMS + "proj kt q vv kb sc dd ex pt pte pv on ot ote y mk")
        psS, psT, psV, psO, psY = ps[0:3], ps[3:5], ps[5], ps[6], ps[7]
        with nc.Block() as block:
            @block.sync
            def _(sp):
                if masked:
                    src = env.d["mask"][bass.ds(b, 1), :, :].rearrange("o (c p) n -> p (o c) n", p=P)
                    sp.dma_start(mi[:, :, :], src).then_inc(s["mk"], 16)
                    sp.wait_ge(s["mk"], 16)

            @block.tensor
            def _(t):
                t.matmul(psS[0][:, 0:SK], wt[:, 1, :], w.ctxT[:, :], start=True, stop=True).then_inc(s["proj"], 1)
                t.matmul(psS[1][:, :], wt[:, 0, :], XT[:, :], start=True, stop=True).then_inc(s["proj"], 1)
                ins = t.matmul(psS[2][0:SK, 0:P], w.ctxT[:, :], wt[:, 2, :], start=True, stop=not biased)
                if biased:
                    ins = t.matmul(psS[2][0:SK, 0:P], env.one_row[0:1, 0:SK], rows[0:1, 0, :], start=False, stop=True)
                ins.then_inc(s["proj"], 1)

                def scores(c):
                    t.wait_ge(s["kb"], 1)
                    t.wait_ge(s["q"], 1)
                    t.wait_ge(s["vv"], 1)
                    if c >= 1:
                        t.wait_ge(s["dd"], NG * c)
                    for g in range(NG):
                        n = (GH[g + 1] - GH[g]) * SK
                        t.matmul(psS[g][:, 0:n], qt[:, c * P:(c + 1) * P],
                                 kb[:, GH[g]:GH[g + 1], :].rearrange("p h n -> p (h n)"),
                                 start=True, stop=True).then_inc(s["sc"], 1)

                def turn_and_weigh(c):
                    t.wait_ge(s["ex"], c + 1)
                    for q in range(4):
                        i = 4 * c + q
                        if i >= 2:
                            t.wait_ge(s["pte"], i - 1)
                        for k in range(4):
                            ins = t.transpose(psT[i % 2][0:SK, k * P:(k + 1) * P], D[:, c % 2, 4 * q + k, :],
                                              env.ident[:, :])
                        ins.then_inc(s["pt"], 1)
                    if c >= 1:
                        t.wait_ge(s["on"], c)
                    for h in range(H):
                        t.wait_ge(s["pte"], 4 * c + h // 4 + 1)
                        ins = t.matmul(psV[:, h * HD:(h + 1) * HD], pt[:, h, :], vv[:, h * HD:(h + 1) * HD],
                                       start=True, stop=True)
                    ins.then_inc(s["pv"], 1)

                def project(c):
                    t.wait_ge(s["on"], c + 1)
                    if c >= 1:
                        t.wait_ge(s["ote"], c)
                    t.transpose(psO[:, 0:P], o[:, c % 2, :], env.ident[:, :]).then_inc(s["ot"], 1)
                    t.wait_ge(s["ote"], c + 1)
                    ins = t.matmul(psY[:, c * P:(c + 1) * P], ot[:, c % 2, :], wt[:, 3, :], start=True, stop=not out_bias)
                    if out_bias:
                        ins = t.matmul(psY[:, c * P:(c + 1) * P], env.one_row[0:1, :], rows[0:1, 1, :],
                                       start=False, stop=True)
                    ins.then_inc(s["y"], 1)

                scores(0)
                for c in range(TB):
                    if c + 1 < TB:
                        scores(c + 1)
                    turn_and_weigh(c)
                    if c >= 1:
                        project(c - 1)
                project(TB - 1)
                turn_tokens(t, s, X, psS[0], env.ident)

            @block.scalar
            def _(a):
                a.wait_ge(s["proj"], 1)
                if biased:
                    a.activation(kt[:, :], psS[0][:, 0:SK], ACT.Identity, bias=cols[:, 1:2]).then_inc(s["kt"], 1)
                else:
                    a.activation(kt[:, :], psS[0][:, 0:SK], ACT.Copy).then_inc(s["kt"], 1)
                a.wait_ge(s["proj"], 2)
                if biased:
                    a.activation(qt[:, :], psS[1][:, :], ACT.Identity, bias=cols[:, 0:1]).then_inc(s["q"], 1)
                else:
                    a.activation(qt[:, :], psS[1][:, :], ACT.Copy).then_inc(s["q"], 1)
                a.wait_ge(s["proj"], 3)
                a.activation(vv[:, :], psS[2][0:SK, 0:P], ACT.Copy).then_inc(s["vv"], 1)

                def exps(c):
                    a.wait_ge(s["dd"], NG * (c + 1))
                    a.activation(D[:, c % 2, :, :], D[:, c % 2, :, :], ACT.Exp, scale=scale).then_inc(s["ex"], 1)

                def p_out(c):
                    for q in range(4):
                        i = 4 * c + q
                        a.wait_ge(s["pt"], i + 1)
                        if c >= 1:
                            a.wait_ge(s["pv"], c)
                        a.activation(pt[:, 4 * q:4 * q + 4, :],
                                     psT[i % 2][0:SK, :].rearrange("p (k n) -> p k n", k=4), ACT.Copy).then_inc(s["pte"], 1)

                def o_out(c):
                    a.wait_ge(s["ot"], c + 1)
                    if c >= 2:
                        a.wait_ge(s["y"], c - 1)
                    a.activation(ot[:, c % 2, :], psO[:, 0:P], ACT.Copy).then_inc(s["ote"], 1)

                for c in range(TB):
                    exps(c)
                    p_out(c)
                    if c >= 1:
                        o_out(c - 1)
                o_out(TB - 1)
                std_and_turn(a, s, w, XT, psS[0], env.eps)

            @block.vector
            def _(v):
                chain = Chain(v, s["chain"])
                v.wait_ge(s["kt"], 1)
                v.tensor_tensor(kb[:, :, :], kt[:, None, :].broadcast_to([P, H, SK]),
                                env.head_mask[:, :, None].broadcast_to([P, H, SK]), ALU.mult).then_inc(s["kb"], 1)
                if masked:
                    v.wait_ge(s["mk"], 16)
                    chain(v.tensor_scalar(mf[:, :, :], mi[:, :, :], 0.0, None, ALU.not_equal))
                    chain(v.tensor_scalar(pen[:, :, :], mf[:, :, :], -1.0, 1e9 / scale, ALU.add, ALU.mult))

                def shifted(c):
                    if c >= 2:
                        v.wait_ge(s["pt"], 4 * (c - 1))
                    for g in range(NG):
                        a0, a1 = GH[g], GH[g + 1]
                        src = psS[g][:, 0:(a1 - a0) * SK].rearrange("p (h n) -> p h n", n=SK)
                        d = D[:, c % 2, a0:a1, :]
                        v.wait_ge(s["sc"], NG * c + g + 1)
                        if masked:
                            m, q = (x[:, c:c + 1, :].broadcast_to([P, a1 - a0, SK]) for x in (mf, pen))
                            chain(v.tensor_tensor(d, src, m, ALU.mult))
                            chain(v.tensor_tensor(d, d, q, ALU.add))
                            src = d
                        chain(v.tensor_reduce(mx[:, c % 2, a0:a1], src, AX.X, ALU.max))
                        v.tensor_tensor(d, src, mx[:, c % 2, a0:a1, None].broadcast_to([P, a1 - a0, SK]),
                                        ALU.subtract).then_inc(s["dd"], 1)

                def weighed(c):
                    v.wait_ge(s["ex"], c + 1)
                    chain(v.tensor_reduce(zs[:, c % 2, :], D[:, c % 2, :, :], AX.X, ALU.add))
                    chain(v.reciprocal(zs[:, c % 2, :], zs[:, c % 2, :]))
                    v.wait_ge(s["pv"], c + 1)
                    if c >= 2:
                        v.wait_ge(s["ot"], c - 1)
                    v.tensor_tensor(o[:, c % 2, :].rearrange("p (h n) -> p h n", n=HD),
                                    psV[:, 0:P].rearrange("p (h n) -> p h n", n=HD),
                                    zs[:, c % 2, :, None].broadcast_to([P, H, HD]), ALU.mult).then_inc(s["on"], 1)

                shifted(0)
                for c in range(TB):
                    if c + 1 < TB:
                        shifted(c + 1)
                    weighed(c)
                v.wait_ge(s["y"], TB)
                normalise(v, chain, s, w, psY, X)
        nc.all_engine_barrier(sems_to_clear=s["numbers"])


def load_common(nc, env, ctx):
    d = env.d
    sb = lambda n, s: ctx.enter_context(nc.sbuf_tensor(n, s, F32))
    env.head_mask = sb("head_mask", [P, H])
    env.one_row = sb("one_row", [1, P])
    env.weights, env.columns, env.rows = {}, {}, {}
    loads = [(env.head_mask[:, :], d["head_mask"])]
    for pre in ("x0", "x2", "x3"):
        env.weights[pre] = sb(pre + "_w", [P, 4, P])
        loads.append((env.weights[pre][:, :, :], d[pre + "_w"]))
        if pre != "x0":
            env.columns[pre] = sb(pre + "_cols", [P, 2])
            loads.append((env.columns[pre][:, :], d[pre + "_cols"]))
            env.rows[pre] = sb(pre + "_rows", [1, 2, P])
            loads.append((env.rows[pre][:, :, :], d[pre + "_rows"]))
    return loads


def moe(nc, env):
    E, HID = 8, 512
    NH = HID // P
    C = int(round(2 * B * S * 1.05 / E))
    X, d = env.X, env.d
    with ExitStack() as ctx:
        sb = lambda n, s: ctx.enter_context(nc.sbuf_tensor(n, s, F32))
        XT = sb("moe_x_t", [P, NT, P])
        wg = sb("gate_w", [P, E])
        tri = sb("strictly_before", [P, P])
        ones = sb("all_ones", [P, P])
        desc = sb("descending", [P, E])
        lg = sb("gates", [P, NT, E])
        g2 = sb("gates_left", [P, NT, E])
        tmp = sb("gate_tmp", [P, NT, E])
        m = sb("gate_max", [P, 2, NT])
        z = sb("gate_z", [P, NT])
        oh = sb("one_hot", [P, 2, NT, E])
        tot = sb("tile_totals", [P, 2 * NT, E])
        run_ = sb("running_totals", [P, 2 * NT, E])
        cw = sb("combine_w", [P, E, NT])
        w1 = sb("moe_w1", [P, NH, P])
        w2 = sb("moe_w2", [P, NH, P])
        b1 = sb("moe_b1", [P, NH])
        b2 = sb("moe_b2", [1, P])
        hT = sb("moe_h_t", [P, 2, NH, S])
        acc = sb("moe_acc", [P, NT, P])
        st = sb("moe_bn", [P, NT, 6])
        mv = sb("moe_mv", [P, NT, 2])
        sd = sb("moe_sd", [P, NT])
        rs = sb("moe_rs", [P, NT])
        ps = env.banks
        s = semaphores(nc, ctx, "e_ld e_tr e_xt e_lg e_chain e_sub e_exp e_oh e_cnt e_w e_h e_he e_y e_acc e_var e_sd e_done")
        with nc.Block() as block:
            @block.sync
            def _(sp):
                for dst, src in ((wg[:, :], "moe_gate"), (tri[:, :], "tri"), (desc[:, :], "desc")):
                    sp.dma_start(dst, d[src]).then_inc(s["e_ld"], 16)

            @block.tensor
            def _(t):
                for b in range(B):
                    if b >= 2:
                        t.wait_ge(s["e_xt"], b - 1)
                    for c in range(TB):
                        ins = t.transpose(ps[b % 2][:, c * P:(c + 1) * P], X[:, TB * b + c, :], env.ident[:, :])
                    ins.then_inc(s["e_tr"], 1)
                t.wait_ge(s["e_ld"], 48)
                for c in range(NT):
                    t.wait_ge(s["e_xt"], c // TB + 1)
                    ins = t.matmul(ps[2][:, c * E:(c + 1) * E], XT[:, c, :], wg[:, :], start=True, stop=True)
                ins.then_inc(s["e_lg"], 1)
                t.wait_ge(s["e_oh"], 2)
                o = oh[:, :, :, :].rearrange("p k t e -> p (k t e)")
                t.matmul(ps[3][:, 0:2 * NT * E], tri[:, :], o, start=True, stop=True)
                t.matmul(ps[4][:, 0:2 * NT * E], ones[:, :], o, start=True, stop=True).then_inc(s["e_cnt"], 1)

            @block.scalar
            def _(a):
                for b in range(B):
                    a.wait_ge(s["e_tr"], b + 1)
                    a.activation(XT[:, TB * b:TB * b + TB, :], ps[b % 2][:, :].rearrange("p (c n) -> p c n", c=TB),
                                 ACT.Copy).then_inc(s["e_xt"], 1)
                a.wait_ge(s["e_sub"], 1)
                a.activation(lg[:, :, :], lg[:, :, :], ACT.Exp).then_inc(s["e_exp"], 1)

            @block.vector
            def _(v):
                chain = Chain(v, s["e_chain"])
                v.memset(ones[:, :], 1.0)
                v.memset(acc[:, :, :], 0.0)
                bc = lambda a: a[:, :, None].broadcast_to([P, NT, E])
                v.wait_ge(s["e_lg"], 1)
                L = ps[2][:, 0:NT * E].rearrange("p (t e) -> p t e", e=E)
                chain(v.tensor_reduce(z[:, :], L, AX.X, ALU.max))
                v.tensor_tensor(lg[:, :, :], L, bc(z[:, :]), ALU.subtract).then_inc(s["e_sub"], 1)
                v.wait_ge(s["e_exp"], 1)
                chain(v.tensor_reduce(z[:, :], lg[:, :, :], AX.X, ALU.add))
                chain(v.reciprocal(z[:, :], z[:, :]))
                chain(v.tensor_tensor(lg[:, :, :], lg[:, :, :], bc(z[:, :]), ALU.mult))
                v.wait_ge(s["e_ld"], 48)
                G = lg
                for k in range(2):
                    chain(v.tensor_reduce(m[:, k, :], G[:, :, :], AX.X, ALU.max))
                    chain(v.tensor_tensor(tmp[:, :, :], G[:, :, :], bc(m[:, k, :]), ALU.is_equal))
                    chain(v.tensor_tensor(tmp[:, :, :], tmp[:, :, :], desc[:, None, :].broadcast_to([P, NT, E]), ALU.mult))
                    chain(v.tensor_reduce(z[:, :], tmp[:, :, :], AX.X, ALU.max))
                    v.tensor_tensor(oh[:, k, :, :], tmp[:, :, :], bc(z[:, :]), ALU.is_equal).then_inc(s["e_oh"], 1)
                    if k == 0:
                        v.wait_ge(s["e_oh"], 1)
                        chain(v.scalar_tensor_tensor(out=g2[:, :, :], in0=oh[:, 0, :, :], scalar=-2.0, in1=lg[:, :, :],
                                                     op0=ALU.mult, op1=ALU.add))
                        G = g2
                v.wait_ge(s["e_cnt"], 1)
                chain(v.tensor_copy(tot[:, :, :], ps[4][:, 0:2 * NT * E].rearrange("p (t e) -> p t e", e=E)))
                for e in range(E):
                    ins = v.tensor_tensor_scan(run_[:, :, e], ones[:, 0:2 * NT], tot[:, :, e], 0.0, ALU.mult, ALU.add)
                chain(ins)
                chain(v.tensor_tensor(run_[:, :, :], run_[:, :, :], tot[:, :, :], ALU.subtract))
                chain(v.tensor_tensor(run_[:, :, :], run_[:, :, :],
                                      ps[3][:, 0:2 * NT * E].rearrange("p (t e) -> p t e", e=E), ALU.add))
                o = oh[:, :, :, :].rearrange("p k t e -> p (k t) e")
                chain(v.scalar_tensor_tensor(out=run_[:, :, :], in0=run_[:, :, :], scalar=float(C), in1=o,
                                             op0=ALU.is_lt, op1=ALU.mult))
                for k in range(2):
                    ins = v.tensor_tensor(tot[:, k * NT:(k + 1) * NT, :], run_[:, k * NT:(k + 1) * NT, :],
                                          bc(m[:, k, :]), ALU.mult)
                chain(ins)
                v.tensor_tensor(cw[:, :, :].rearrange("p e t -> p t e"), tot[:, 0:NT, :], tot[:, NT:2 * NT, :], ALU.add)
        nc.all_engine_barrier(sems_to_clear=s["numbers"])

        cwe = sb("combine_w_expert", [P, NT])
        with nc.Fori(0, E) as e:
            with nc.Block() as block:
                @block.sync
                def _(sp):
                    for dst, src in ((w1[:, :, :], "moe_w1"), (w2[:, :, :], "moe_w2")):
                        sp.dma_start(dst, d[src][bass.ds(e, 1), :, :, :].rearrange("o p a b -> p (o a) b")).then_inc(s["e_ld"], 16)
                    sp.dma_start(b1[:, :], d["moe_b1"][bass.ds(e, 1), :, :].rearrange("o p a -> p (o a)")).then_inc(s["e_ld"], 16)
                    sp.dma_start(b2[:, :], d["moe_b2"][bass.ds(e, 1), :]).then_inc(s["e_ld"], 16)

                @block.tensor
                def _(t):
                    t.wait_ge(s["e_ld"], 64)

                    def up(b):
                        for n in range(NH):
                            i = NH * b + n
                            if i >= 4:
                                t.wait_ge(s["e_he"], i - 3)
                            t.matmul(ps[i % 4][:, :], w1[:, n, :],
                                     XT[:, TB * b:TB * b + TB, :].rearrange("p c n -> p (c n)"),
                                     start=True, stop=True).then_inc(s["e_h"], 1)

                    def down(b):
                        if b >= 2:
                            t.wait_ge(s["e_acc"], TB * (b - 1))
                        for c in range(TB):
                            y = ps[4 + b % 2][:, c * P:(c + 1) * P]
                            for n in range(NH):
                                t.wait_ge(s["e_he"], NH * b + n + 1)
                                t.matmul(y, hT[:, b % 2, n, c * P:(c + 1) * P], w2[:, n, :], start=(n == 0), stop=False)
                            t.matmul(y, env.one_row[0:1, :], b2[0:1, :], start=False, stop=True).then_inc(s["e_y"], 1)

                    up(0)
                    for b in range(B):
                        if b + 1 < B:
                            up(b + 1)
                        down(b)

                @block.scalar
                def _(a):
                    a.wait_ge(s["e_ld"], 64)
                    for i in range(NH * B):
                        b, n = divmod(i, NH)
                        a.wait_ge(s["e_h"], i + 1)
                        if b >= 2:
                            a.wait_ge(s["e_y"], TB * (b - 1))
                        a.activation(hT[:, b % 2, n, :], ps[i % 4][:, :], ACT.Gelu, bias=b1[:, n:n + 1]).then_inc(s["e_he"], 1)

                @block.vector
                def _(v):
                    v.tensor_copy(cwe[:, :], cw[:, bass.ds(e, 1), :].rearrange("p o t -> p (o t)")).then_inc(s["e_w"], 1)
                    v.wait_ge(s["e_w"], 1)
                    for c in range(NT):
                        v.wait_ge(s["e_y"], TB * (c // TB + 1))
                        v.scalar_tensor_tensor(out=acc[:, c, :],
                                               in0=ps[4 + (c // TB) % 2][:, (c % TB) * P:(c % TB + 1) * P],
                                               scalar=cwe[:, c:c + 1], in1=acc[:, c, :],
                                               op0=ALU.mult, op1=ALU.add).then_inc(s["e_acc"], 1)
            nc.all_engine_barrier(sems_to_clear=s["numbers"])
        with nc.Block() as block:
            finish_layer_norm(block, X, acc, XT, st, mv, sd, rs, NT, env, s["e_chain"], s["e_var"], s["e_sd"], s["e_done"])
        nc.all_engine_barrier(sems_to_clear=s["numbers"])


def load_late(nc, env, ctx):
    d = env.d
    env.w = {}
    with ExitStack() as inner:
        s = semaphores(nc, inner, "late_loaded")
        with nc.Block() as block:
            @block.sync
            def _(sp):
                names = ("la_w", "la_e", "la_wo", "la_sel", "la_mask", "gm_w", "gm_cols", "gm_row", "lt_wq", "lt_wk",
                         "lt_wv", "lt_wo", "lt_rope", "lt_decay", "sm_gate", "sm_w1", "sm_w2", "sa_w", "sa_wo",
                         "sa_desc", "sa_causal", "sl_w", "sl_cols")
                for name in names:
                    shape = list(d[name].shape)
                    env.w[name] = ctx.enter_context(nc.sbuf_tensor(name, shape, F32))
                    at = tuple(slice(None) for _ in shape)
                    sp.dma_start(env.w[name][at], d[name]).then_inc(s["late_loaded"], 16)
                sp.wait_ge(s["late_loaded"], 16 * len(names))
        nc.all_engine_barrier(sems_to_clear=s["numbers"])
    sb = lambda n, s: ctx.enter_context(nc.sbuf_tensor(n, s, F32))
    env.gm1 = sb("gm_w1", [P, TB, 4, P])
    env.gm2 = sb("gm_w2", [P, TB, 4, P])
    env.gmb = sb("gm_b", [P, TB, 5])


def load_experts(sp, env, b, sem):
    d, group = env.d, b % 2
    for dst, src in ((env.gm1, "gm_w1"), (env.gm2, "gm_w2"), (env.gmb, "gm_b")):
        at = tuple(slice(None) for _ in dst.shape)
        n = d[src][(bass.ds(group, 1),) + at]
        n = n.rearrange("o p a b c -> p (o a) b c") if len(n.shape) == 5 else n.rearrange("o p a b -> p (o a) b")
        sp.dma_start(dst[at], n).then_inc(sem, 16)


def local_attention(nc, env, w, b):
    WIN = 32
    NG = WIN * H // P
    RG = WIN // NG
    X, XT, ps = w.X, w.XT, w.ps
    W, Ec, Wo, sel, msk = (env.w[n] for n in ("la_w", "la_e", "la_wo", "la_sel", "la_mask"))
    scale = HD ** -0.5
    with ExitStack() as ctx:
        sb = lambda n, s: ctx.enter_context(nc.sbuf_tensor("la_" + n, s, F32))
        qt = sb("q_t", [P, S])
        kp = sb("k_padded", [P, WIN + S])
        vp = sb("v_padded", [P, WIN + S])
        pr = sb("products", [P, 4, S])
        D = sb("weights", [P, TB, WIN, H])
        mx = sb("max", [P, TB, H])
        zs = sb("sum", [P, TB, H])
        pt = sb("weights_t", [P, NG, S])
        s = semaphores(nc, ctx, LN_SEMS + "proj q pad pr sc dd ex pn pt pte bc pv y ld")
        psS, psT, psB, psY = ps[0:4], ps[4:8], ps[0:3], ps[3]
        with nc.Block() as block:
            @block.sync
            def _(sp):
                load_experts(sp, env, b, s["ld"])
                sp.wait_ge(s["ld"], 48)

            @block.tensor
            def _(t):
                for m in range(3):
                    t.matmul(psT[m][:, :], W[:, m * P:(m + 1) * P], XT[:, :], start=True, stop=True).then_inc(s["proj"], 1)
                for r in range(WIN):
                    t.wait_ge(s["pr"], r + 1)
                    for c in range(TB):
                        ins = t.matmul(psS[c][:, r * H:(r + 1) * H], pr[:, r % 4, c * P:(c + 1) * P],
                                       env.head_mask[:, :], start=True, stop=True)
                    ins.then_inc(s["sc"], 1)
                t.wait_ge(s["q"], 3)
                for c in range(TB):
                    t.wait_ge(s["pn"], c + 1)
                    for g in range(NG):
                        ins = t.transpose(psT[g][:, c * P:(c + 1) * P],
                                          D[:, c, g * RG:(g + 1) * RG, :].rearrange("p r h -> p (r h)"), env.ident[:, :])
                ins.then_inc(s["pt"], 1)
                for r in range(WIN + 2):
                    if r < WIN:
                        t.wait_ge(s["pte"], r // RG + 1)
                        if r >= 3:
                            t.wait_ge(s["pv"], r - 2)
                        t.matmul(psB[r % 3][:, :], sel[:, r % RG, :], pt[:, r // RG, :], start=True, stop=True)\
                            .then_inc(s["bc"], 1)
                    if r >= 2:
                        t.wait_ge(s["pv"], r - 1)
                        for c in range(TB):
                            ins = t.matmul(psY[:, c * P:(c + 1) * P], pr[:, (r - 2) % 4, c * P:(c + 1) * P], Wo[:, :],
                                           start=(r == 2 and c == 0), stop=(r == WIN + 1), skip_group_check=True)
                        ins.then_inc(s["y"], 1)
                turn_tokens(t, s, X, ps[0], env.ident)

            @block.scalar
            def _(a):
                for m, dst in enumerate((qt[:, :], kp[:, WIN:], vp[:, WIN:])):
                    a.wait_ge(s["proj"], m + 1)
                    a.activation(dst, psT[m][:, :], ACT.Copy).then_inc(s["q"], 1)
                for c in range(TB):
                    a.wait_ge(s["dd"], c + 1)
                    a.activation(D[:, c, :, :], D[:, c, :, :], ACT.Exp, scale=scale).then_inc(s["ex"], 1)
                a.wait_ge(s["pt"], 1)
                for g in range(NG):
                    a.activation(pt[:, g, :], psT[g][:, :], ACT.Copy).then_inc(s["pte"], 1)
                std_and_turn(a, s, w, XT, ps[0], env.eps)

            @block.vector
            def _(v):
                chain = Chain(v, s["chain"])
                v.memset(kp[:, 0:WIN], 0.0)
                chain(v.memset(vp[:, 0:WIN], 0.0))
                v.wait_ge(s["q"], 2)
                for r in range(WIN):
                    if r >= 4:
                        v.wait_ge(s["sc"], r - 3)
                    v.scalar_tensor_tensor(out=pr[:, r % 4, :], in0=kp[:, r + 1:r + 1 + S], scalar=Ec[:, r:r + 1],
                                           in1=qt[:, :], op0=ALU.add, op1=ALU.mult).then_inc(s["pr"], 1)
                v.wait_ge(s["sc"], WIN)
                for c in range(TB):
                    src = psS[c][:, :].rearrange("p (r h) -> p r h", h=H)
                    if c == 0:
                        chain(v.tensor_tensor(D[:, 0, :, :], src, msk[:, :, None].broadcast_to([P, WIN, H]), ALU.add))
                        src = D[:, 0, :, :]
                    chain(v.tensor_reduce(mx[:, c, :], src.rearrange("p r h -> p h r"), AX.X, ALU.max))
                    v.tensor_tensor(D[:, c, :, :], src, mx[:, c, None, :].broadcast_to([P, WIN, H]), ALU.subtract)\
                        .then_inc(s["dd"], 1)
                for c in range(TB):
                    v.wait_ge(s["ex"], c + 1)
                    chain(v.tensor_reduce(zs[:, c, :], D[:, c, :, :].rearrange("p r h -> p h r"), AX.X, ALU.add))
                    chain(v.reciprocal(zs[:, c, :], zs[:, c, :]))
                    v.tensor_tensor(D[:, c, :, :], D[:, c, :, :], zs[:, c, None, :].broadcast_to([P, WIN, H]),
                                    ALU.mult).then_inc(s["pn"], 1)
                v.wait_ge(s["q"], 3)
                for r in range(WIN):
                    v.wait_ge(s["bc"], r + 1)
                    if r >= 4:
                        v.wait_ge(s["y"], r - 3)
                    v.tensor_tensor(pr[:, r % 4, :], psB[r % 3][:, :], vp[:, r + 1:r + 1 + S], ALU.mult).then_inc(s["pv"], 1)
                v.wait_ge(s["y"], WIN)
                normalise(v, chain, s, w, psY, X)
        nc.all_engine_barrier(sems_to_clear=s["numbers"])


def context_mlp(nc, env, w, b):
    X, XT, ps = w.X, w.XT, w.ps
    with ExitStack() as ctx:
        g = ctx.enter_context(nc.sbuf_tensor("cm_gelu", [SK, S], F32))
        s = semaphores(nc, ctx, LN_SEMS + "h g gh y")
        with nc.Block() as block:
            @block.tensor
            def _(t):
                t.matmul(ps[1][0:SK, :], w.ctxT[:, :], XT[:, :], start=True, stop=True).then_inc(s["h"], 1)
                t.wait_ge(s["gh"], 1)
                for c in range(TB):
                    ins = t.matmul(ps[2][:, c * P:(c + 1) * P], g[:, c * P:(c + 1) * P], w.ctx[:, :], start=True, stop=True)
                ins.then_inc(s["y"], 1)
                turn_tokens(t, s, X, ps[0], env.ident)

            @block.scalar
            def _(a):
                a.wait_ge(s["h"], 1)
                a.activation(g[:, :], ps[1][0:SK, :], ACT.Gelu).then_inc(s["g"], 1)
                std_and_turn(a, s, w, XT, ps[0], env.eps)

            @block.vector
            def _(v):
                chain = Chain(v, s["chain"])
                v.wait_ge(s["g"], 1)
                v.tensor_tensor(g[:, :], ps[1][0:SK, :], g[:, :], ALU.mult).then_inc(s["gh"], 1)
                v.wait_ge(s["y"], 1)
                normalise(v, chain, s, w, ps[2], X)
        nc.all_engine_barrier(sems_to_clear=s["numbers"])


def grouped_mlp(nc, env, w, b):
    NH = 4
    X, XT, ps = w.X, w.XT, w.ps
    W, cols, row = env.w["gm_w"], env.w["gm_cols"], env.w["gm_row"]
    with ExitStack() as ctx:
        sb = lambda n, s: ctx.enter_context(nc.sbuf_tensor("gm_" + n, s, F32))
        xn = sb("xn_t", [P, S])
        xa = sb("x_attn_t", [P, S])
        hT = sb("h_t", [P, TB, NH, P])
        eo = sb("eo_t", [P, TB, P])
        y = sb("y", [P, TB, P])
        s = semaphores(nc, ctx, LN_SEMS + "var0 sd0 xh xt xnt at xa h he e ee y ye")
        psE, psN = ps[6], ps[7]
        with nc.Block() as block:
            @block.tensor
            def _(t):
                for c in range(TB):
                    t.wait_ge(s["xh"], c + 1)
                    ins = t.transpose(ps[0][:, c * P:(c + 1) * P], w.R[:, c, :], env.ident[:, :])
                ins.then_inc(s["xt"], 1)
                t.wait_ge(s["xnt"], 1)
                t.matmul(ps[1][:, :], W[:, 0, :], xn[:, :], start=True, stop=True).then_inc(s["at"], 1)
                t.wait_ge(s["xa"], 1)
                for c in range(TB):
                    for n in range(NH):
                        ins = t.matmul(ps[2 + c][:, n * P:(n + 1) * P], env.gm1[:, c, n, :], xa[:, c * P:(c + 1) * P],
                                       start=True, stop=True)
                    ins.then_inc(s["h"], 1)
                for c in range(TB):
                    for n in range(NH):
                        t.wait_ge(s["he"], NH * c + n + 1)
                        ins = t.matmul(psE[:, c * P:(c + 1) * P], env.gm2[:, c, n, :], hT[:, c, n, :],
                                       start=(n == 0), stop=(n == NH - 1))
                ins.then_inc(s["e"], 1)
                for c in range(TB):
                    t.wait_ge(s["ee"], c + 1)
                    t.matmul(psN[:, c * P:(c + 1) * P], eo[:, c, :], W[:, 1, :], start=True, stop=False)
                    ins = t.matmul(psN[:, c * P:(c + 1) * P], env.one_row[0:1, :], row[0:1, :], start=False, stop=True)
                ins.then_inc(s["y"], 1)
                turn_tokens(t, s, X, ps[0], env.ident)

            @block.scalar
            def _(a):
                a.wait_ge(s["var0"], 1)
                a.activation(w.sd[:, :], w.mv[:, :, 1], ACT.Sqrt, bias=env.eps[:, 0:1]).then_inc(s["sd0"], 1)
                a.wait_ge(s["xt"], 1)
                a.activation(xn[:, :], ps[0][:, :], ACT.Identity, scale=cols[:, 0:1], bias=cols[:, 1:2]).then_inc(s["xnt"], 1)
                for c in range(TB):
                    a.wait_ge(s["h"], c + 1)
                    for n in range(NH):
                        a.activation(hT[:, c, n, :], ps[2 + c][:, n * P:(n + 1) * P], ACT.Gelu,
                                     bias=env.gmb[:, c, n:n + 1]).then_inc(s["he"], 1)
                a.wait_ge(s["y"], 1)
                a.activation(y[:, :, :], psN[:, :].rearrange("p (c n) -> p c n", c=TB), ACT.Gelu).then_inc(s["ye"], 1)
                std_and_turn(a, s, w, XT, ps[0], env.eps)

            @block.vector
            def _(v):
                chain = Chain(v, s["chain"])
                layer_norm_stats(v, chain, X, w.st, w.mv, TB, s["var0"])
                v.wait_ge(s["sd0"], 1)
                chain(v.reciprocal(w.rs[:, :], w.sd[:, :]))
                for c in range(TB):
                    v.tensor_scalar(w.R[:, c, :], X[:, c, :], w.mv[:, c, 0:1], w.rs[:, c:c + 1],
                                    ALU.subtract, ALU.mult).then_inc(s["xh"], 1)
                v.wait_ge(s["at"], 1)
                v.scalar_tensor_tensor(out=xa[:, :], in0=ps[1][:, :], scalar=cols[:, 2:3], in1=XT[:, :],
                                       op0=ALU.add, op1=ALU.add).then_inc(s["xa"], 1)
                v.wait_ge(s["e"], 1)
                for c in range(TB):
                    v.tensor_scalar(eo[:, c, :], psE[:, c * P:(c + 1) * P], env.gmb[:, c, NH:NH + 1], None, ALU.add)\
                        .then_inc(s["ee"], 1)
                v.wait_ge(s["ye"], 1)
                normalise(v, chain, s, w, y, X)
        nc.all_engine_barrier(sems_to_clear=s["numbers"])


def lightning(nc, env, w, b):
    HQ, KV, W2 = 16, 4, 64
    NQ, NK = HQ * W2 // P, KV * W2 // P
    X, XT, ps = w.X, w.XT, w.ps
    wq, wk, wv, wo, rope, decay = (env.w["lt_" + n] for n in ("wq", "wk", "wv", "wo", "rope", "decay"))
    with ExitStack() as ctx:
        sb = lambda n, s: ctx.enter_context(nc.sbuf_tensor("lt_" + n, s, F32))
        qk = sb("q_k_t", [P, NQ + NK, S])
        tmp = sb("rope_tmp", [P, 2, 2, S])
        vv = sb("v", [P, TB, KV * W2])
        pd = sb("decayed", [P, 4, S])
        ot = sb("o_t", [P, 2, S])
        s = semaphores(nc, ctx, LN_SEMS + "vp ve pj r1 qk sc pd av oe y")
        NC_ = NQ + NK
        pair = lambda i: (ps[2 * (i % 2)], ps[2 * (i % 2) + 1])
        psO, psY = ps[4:6], ps[7]
        items = [(m, r, j) for m in range(NQ) for r in range(2) for j in range(TB)]
        with nc.Block() as block:
            @block.tensor
            def _(t):
                for c in range(TB):
                    ins = t.matmul(ps[4 + c // 2][:, (c % 2) * 256:(c % 2 + 1) * 256], XT[:, c * P:(c + 1) * P], wv[:, :],
                                   start=True, stop=True)
                ins.then_inc(s["vp"], 1)
                for i in range(NC_):
                    if i >= 2:
                        t.wait_ge(s["r1"], 2 * (i - 1))
                    wt, m = (wk, i) if i < NK else (wq, i - NK)
                    for x in range(2):
                        t.matmul(pair(i)[x][:, :], wt[:, x, m, :], XT[:, :], start=True, stop=True).then_inc(s["pj"], 1)
                t.wait_ge(s["r1"], 2 * NC_)
                t.wait_ge(s["ve"], 2)

                def score(i):
                    m, r, j = items[i]
                    if i >= 4:
                        t.wait_ge(s["pd"], i - 3)
                    t.wait_ge(s["qk"], NK + m + 1)
                    rows = slice(W2 * r, W2 * r + W2)
                    t.matmul(ps[i % 4][:, j * P:S], qk[rows, m // 4, j * P:(j + 1) * P], qk[rows, NK + m, j * P:S],
                             start=True, stop=True).then_inc(s["sc"], 1)

                def weigh(i):
                    m, r, j = items[i]
                    t.wait_ge(s["pd"], i + 1)
                    if m >= 2 and r == 0 and j == 0:
                        t.wait_ge(s["oe"], m - 1)
                    kv = 2 * (m // 4) + r
                    t.matmul(psO[m % 2][W2 * r:W2 * r + W2, j * P:S], vv[:, j, kv * W2:(kv + 1) * W2], pd[:, i % 4, j * P:S],
                             start=(j == 0), stop=(j == TB - 1), skip_group_check=True).then_inc(s["av"], 1)

                def out(m):
                    t.wait_ge(s["oe"], m + 1)
                    for c in range(TB):
                        ins = t.matmul(psY[:, c * P:(c + 1) * P], ot[:, m % 2, c * P:(c + 1) * P], wo[:, m, :],
                                       start=(m == 0 and c == 0), stop=(m == NQ - 1), skip_group_check=True)
                    ins.then_inc(s["y"], 1)

                N = len(items)
                for i in range(N + 2):
                    if i < N:
                        score(i)
                    if i >= 2:
                        weigh(i - 2)
                    if i % 8 == 3 and i >= 11:
                        out((i - 11) // 8)
                out(NQ - 1)
                turn_tokens(t, s, X, ps[0], env.ident)

            @block.scalar
            def _(a):
                a.wait_ge(s["vp"], 1)
                for x in range(2):
                    a.activation(vv[:, 2 * x:2 * x + 2, :], ps[4 + x][:, :].rearrange("p (c n) -> p c n", c=2), ACT.Copy)\
                        .then_inc(s["ve"], 1)
                for m in range(NQ):
                    a.wait_ge(s["av"], 8 * (m + 1))
                    if m >= 2:
                        a.wait_ge(s["y"], m - 1)
                    a.activation(ot[:, m % 2, :], psO[m % 2][:, :], ACT.Copy).then_inc(s["oe"], 1)
                std_and_turn(a, s, w, XT, ps[0], env.eps)

            @block.gpsimd
            def _(g):
                for i in range(NC_):
                    g.wait_ge(s["r1"], 2 * (i + 1))
                    g.tensor_tensor(qk[:, i, :], tmp[:, i % 2, 0, :], tmp[:, i % 2, 1, :], ALU.add).then_inc(s["qk"], 1)

            @block.vector
            def _(v):
                chain = Chain(v, s["chain"])
                for i in range(NC_):
                    if i >= 2:
                        v.wait_ge(s["qk"], i - 1)
                    for x in range(2):
                        v.wait_ge(s["pj"], 2 * i + x + 1)
                        v.tensor_tensor(tmp[:, i % 2, x, :], pair(i)[x][:, :], rope[:, x, :], ALU.mult).then_inc(s["r1"], 1)
                for i, (m, r, j) in enumerate(items):
                    h = 8 * (m // 4) + 4 * r + m % 4
                    v.wait_ge(s["sc"], i + 1)
                    if i >= 4:
                        v.wait_ge(s["av"], i - 3)
                    v.tensor_tensor(pd[:, i % 4, j * P:S], ps[i % 4][:, j * P:S], decay[:, h, 0:S - j * P], ALU.mult)\
                        .then_inc(s["pd"], 1)
                v.wait_ge(s["y"], NQ)
                normalise(v, chain, s, w, psY, X)
        nc.all_engine_barrier(sems_to_clear=s["numbers"])


def shared_moe(nc, env, w, b):
    E, NH = 8, 4
    X, XT, ps = w.X, w.XT, w.ps
    wg, w1, w2 = env.w["sm_gate"], env.w["sm_w1"], env.w["sm_w2"]
    with ExitStack() as ctx:
        sb = lambda n, s: ctx.enter_context(nc.sbuf_tensor("sm_" + n, s, F32))
        lg = sb("gates", [P, TB, E])
        top = sb("top", [P, TB, E])
        z = sb("z", [P, TB])
        dn = sb("denom", [P, TB])
        hT = sb("h_t", [P, NH, S])
        y = sb("y", [P, TB, P])
        s = semaphores(nc, ctx, LN_SEMS + "lg sub ex h he y")
        with nc.Block() as block:
            @block.tensor
            def _(t):
                for c in range(TB):
                    ins = t.matmul(ps[1][:, c * E:(c + 1) * E], XT[:, c * P:(c + 1) * P], wg[:, :], start=True, stop=True)
                ins.then_inc(s["lg"], 1)
                for n in range(NH):
                    t.matmul(ps[2 + n][:, :], w1[:, n, :], XT[:, :], start=True, stop=True).then_inc(s["h"], 1)
                for c in range(TB):
                    for n in range(NH):
                        t.wait_ge(s["he"], n + 1)
                        ins = t.matmul(ps[6][:, c * P:(c + 1) * P], hT[:, n, c * P:(c + 1) * P], w2[:, n, :],
                                       start=(n == 0), stop=(n == NH - 1))
                ins.then_inc(s["y"], 1)
                turn_tokens(t, s, X, ps[0], env.ident)

            @block.scalar
            def _(a):
                a.wait_ge(s["sub"], 1)
                a.activation(lg[:, :, :], lg[:, :, :], ACT.Exp).then_inc(s["ex"], 1)
                for n in range(NH):
                    a.wait_ge(s["h"], n + 1)
                    a.activation(hT[:, n, :], ps[2 + n][:, :], ACT.Relu).then_inc(s["he"], 1)
                std_and_turn(a, s, w, XT, ps[0], env.eps)

            @block.vector
            def _(v):
                chain = Chain(v, s["chain"])
                bc = lambda a: a[:, :, None].broadcast_to([P, TB, E])
                v.wait_ge(s["lg"], 1)
                L = ps[1][:, 0:TB * E].rearrange("p (t e) -> p t e", e=E)
                chain(v.tensor_reduce(z[:, :], L, AX.X, ALU.max))
                v.tensor_tensor(lg[:, :, :], L, bc(z[:, :]), ALU.subtract).then_inc(s["sub"], 1)
                v.wait_ge(s["ex"], 1)
                chain(v.tensor_reduce(z[:, :], lg[:, :, :], AX.X, ALU.add))
                chain(v.reciprocal(z[:, :], z[:, :]))
                chain(v.tensor_tensor(lg[:, :, :], lg[:, :, :], bc(z[:, :]), ALU.mult))
                for c in range(TB):
                    ins = v.max(top[:, c, :], lg[:, c, :])
                chain(ins)
                chain(v.tensor_tensor(dn[:, :], top[:, :, 0], top[:, :, 1], ALU.add))
                chain(v.tensor_scalar(dn[:, :], dn[:, :], 1.1920929e-07, None, ALU.max))
                chain(v.reciprocal(dn[:, :], dn[:, :]))
                chain(v.tensor_tensor(top[:, :, 0:2], top[:, :, 0:2], dn[:, :, None].broadcast_to([P, TB, 2]), ALU.mult))
                chain(v.tensor_tensor(z[:, :], top[:, :, 0], top[:, :, 1], ALU.add))
                v.wait_ge(s["y"], 1)
                for c in range(TB):
                    ins = v.tensor_scalar(y[:, c, :], ps[6][:, c * P:(c + 1) * P], z[:, c:c + 1], None, ALU.mult)
                chain(ins)
                normalise(v, chain, s, w, y, X)
        nc.all_engine_barrier(sems_to_clear=s["numbers"])


def sparse_attention(nc, env, w, b):
    KEEP = 64
    MASKED, TAKEN = -1e30, -3e38
    G3 = 3 * H
    X, XT, ps = w.X, w.XT, w.ps
    W, Wo, desc, causal = (env.w["sa_" + n] for n in ("w", "wo", "desc", "causal"))
    scale = HD ** -0.5
    with ExitStack() as ctx:
        sb = lambda n, s: ctx.enter_context(nc.sbuf_tensor("sa_" + n, s, F32))
        qkv = sb("qkv", [P, TB, 3 * P])
        ab = sb("abs", [P, 2, 3 * P])
        m = sb("feature_max", [P, 2, G3])
        qt = sb("q_t", [P, S])
        kt = sb("k_t", [P, S])
        kh = sb("k_by_head", [P, H, S])
        sc = sb("scores", [P, 4, S])
        left = sb("left", [P, 2, S])
        m8 = sb("max8", [P, 2, 8])
        top = sb("top", [P, 4])
        pe = sb("exp", [P, 4, S])
        zs = sb("sum", [P, TB, H])
        pt = sb("p_t", [P, 2, S])
        o = sb("o", [P, P])
        ot = sb("o_t", [P, P])
        s = semaphores(nc, ctx, LN_SEMS + "pj pje keep tk tke kh sc cp dg tp ex pk pt pte pv on ott ote y")
        psS, psT, psV, psO, psY = ps[0:2], ps[2:4], ps[4:6], ps[6], ps[7]
        items = [(c, h) for c in range(TB) for h in range(H)]
        N = len(items)
        with nc.Block() as block:
            @block.tensor
            def _(t):
                for c in range(TB):
                    t.matmul(ps[c][:, 0:3 * P], XT[:, c * P:(c + 1) * P], W[:, :], start=True, stop=True).then_inc(s["pj"], 1)
                for c in range(TB):
                    t.wait_ge(s["keep"], c + 1)
                    for x in range(2):
                        ins = t.transpose(ps[4 + x][:, c * P:(c + 1) * P], qkv[:, c, x * P:(x + 1) * P], env.ident[:, :])
                ins.then_inc(s["tk"], 1)
                t.wait_ge(s["tke"], 2)
                t.wait_ge(s["pje"], TB)

                def score(i):
                    c, h = items[i]
                    t.wait_ge(s["kh"], h + 1)
                    if i >= 2:
                        t.wait_ge(s["dg"], i - 1)
                    if i - 2 >= H:
                        t.wait_ge(s["cp"], i - 1 - H)
                    n = (c + 1) * P
                    t.matmul(psS[i % 2][:, 0:n], qt[:, c * P:n], kh[:, h, 0:n], start=True, stop=True).then_inc(s["sc"], 1)

                def turn(i):
                    c, h = items[i]
                    t.wait_ge(s["pk"], i + 1)
                    if i >= 2:
                        t.wait_ge(s["pte"], i - 1)
                    for j in range(c + 1):
                        ins = t.transpose(psT[i % 2][:, j * P:(j + 1) * P], pe[:, i % 4, j * P:(j + 1) * P], env.ident[:, :])
                    ins.then_inc(s["pt"], 1)

                def weigh(i):
                    c, h = items[i]
                    t.wait_ge(s["pte"], i + 1)
                    if h == 0 and c >= 2:
                        t.wait_ge(s["on"], c - 1)
                    for j in range(c + 1):
                        ins = t.matmul(psV[c % 2][:, h * HD:(h + 1) * HD], pt[:, i % 2, j * P:(j + 1) * P],
                                       qkv[:, j, 2 * P + h * HD:2 * P + (h + 1) * HD], start=(j == 0), stop=(j == c))
                    ins.then_inc(s["pv"], 1)

                def project(c):
                    t.wait_ge(s["on"], c + 1)
                    t.transpose(psO[:, 0:P], o[:, :], env.ident[:, :]).then_inc(s["ott"], 1)
                    t.wait_ge(s["ote"], c + 1)
                    t.matmul(psY[:, c * P:(c + 1) * P], ot[:, :], Wo[:, :], start=True, stop=True).then_inc(s["y"], 1)

                for i in range(0, N + 4, 2):
                    for k in (i, i + 1):
                        if k < N:
                            score(k)
                    for step in (turn, weigh):
                        for k in (i - 4, i - 3):
                            if k >= 0:
                                step(k)
                    if i - 4 >= 0 and items[i - 4][1] == 8 and items[i - 4][0] >= 1:
                        project(items[i - 4][0] - 1)
                project(TB - 1)
                turn_tokens(t, s, X, ps[0], env.ident)

            @block.scalar
            def _(a):
                for c in range(TB):
                    a.wait_ge(s["pj"], c + 1)
                    a.activation(qkv[:, c, :], ps[c][:, 0:3 * P], ACT.Copy).then_inc(s["pje"], 1)
                a.wait_ge(s["tk"], 1)
                for x, dst in enumerate((qt, kt)):
                    a.activation(dst[:, :], ps[4 + x][:, :], ACT.Copy).then_inc(s["tke"], 1)

                def early(i):
                    c, h = items[i]
                    if i >= 4:
                        a.wait_ge(s["ex"], i - 3)
                        a.wait_ge(s["pk"], i - 3)
                    a.wait_ge(s["sc"], i + 1)
                    if c >= 1:
                        a.wait_ge(s["dg"], i + 1)
                        a.activation(sc[:, i % 4, 0:c * P], psS[i % 2][:, 0:c * P], ACT.Copy).then_inc(s["cp"], 1)

                def exps(i):
                    c, h = items[i]
                    n = (c + 1) * P
                    a.wait_ge(s["tp"], i + 1)
                    if i >= 4:
                        a.wait_ge(s["pt"], i - 3)
                    a.activation(pe[:, i % 4, 0:n], sc[:, i % 4, 0:n], ACT.Exp, scale=scale,
                                 bias=top[:, i % 4:i % 4 + 1]).then_inc(s["ex"], 1)

                def turned(i):
                    c, h = items[i]
                    n = (c + 1) * P
                    a.wait_ge(s["pt"], i + 1)
                    if i >= 2:
                        a.wait_ge(s["pv"], i - 1)
                    a.activation(pt[:, i % 2, 0:n], psT[i % 2][:, 0:n], ACT.Copy).then_inc(s["pte"], 1)

                def o_out(c):
                    a.wait_ge(s["ott"], c + 1)
                    if c >= 1:
                        a.wait_ge(s["y"], c)
                    a.activation(ot[:, :], psO[:, 0:P], ACT.Copy).then_inc(s["ote"], 1)

                for i in range(0, N + 4, 2):
                    for k in (i, i + 1):
                        if k < N:
                            early(k)
                    for step, lag in ((exps, 2), (turned, 4)):
                        for k in (i - lag, i + 1 - lag):
                            if 0 <= k < N:
                                step(k)
                    if i - 4 >= 0 and items[i - 4][1] == 8 and items[i - 4][0] >= 1:
                        o_out(items[i - 4][0] - 1)
                o_out(TB - 1)
                std_and_turn(a, s, w, XT, ps[0], env.eps)

            @block.gpsimd
            def _(g):
                g.wait_ge(s["tke"], 2)
                for h in range(H):
                    g.tensor_scalar(kh[:, h, :], kt[:, :], env.head_mask[:, h:h + 1], None, ALU.mult).then_inc(s["kh"], 1)

            @block.vector
            def _(v):
                chain = Chain(v, s["chain"])
                for c in range(TB):
                    v.wait_ge(s["pje"], c + 1)
                    x = qkv[:, c, :].rearrange("p (g n) -> p g n", n=HD)
                    y = ab[:, c % 2, :].rearrange("p (g n) -> p g n", n=HD)
                    bc = m[:, c % 2, :, None].broadcast_to([P, G3, HD])
                    chain(v.scalar_tensor_tensor(out=ab[:, c % 2, :], in0=qkv[:, c, :], scalar=-1.0, in1=qkv[:, c, :],
                                                 op0=ALU.mult, op1=ALU.max))
                    chain(v.tensor_reduce(m[:, c % 2, :], y, AX.X, ALU.max))
                    chain(v.tensor_tensor(y, y, bc, ALU.is_equal))
                    chain(v.tensor_tensor(y, y, desc[:, None, :].broadcast_to([P, G3, HD]), ALU.mult))
                    chain(v.tensor_reduce(m[:, c % 2, :], y, AX.X, ALU.max))
                    chain(v.tensor_tensor(y, y, bc, ALU.is_equal))
                    v.tensor_tensor(x, x, y, ALU.mult).then_inc(s["keep"], 1)

                def finish(c):
                    chain(v.reciprocal(zs[:, c, :], zs[:, c, :]))
                    v.wait_ge(s["pv"], H * (c + 1))
                    if c >= 1:
                        v.wait_ge(s["ott"], c)
                    v.tensor_tensor(o[:, :].rearrange("p (h n) -> p h n", n=HD),
                                    psV[c % 2][:, 0:P].rearrange("p (h n) -> p h n", n=HD),
                                    zs[:, c, :, None].broadcast_to([P, H, HD]), ALU.mult).then_inc(s["on"], 1)

                def masked(i):
                    c, h = items[i]
                    v.wait_ge(s["sc"], i + 1)
                    if i >= 4:
                        v.wait_ge(s["ex"], i - 3)
                    v.tensor_tensor(sc[:, i % 4, c * P:(c + 1) * P], psS[i % 2][:, c * P:(c + 1) * P], causal[:, :],
                                    ALU.add).then_inc(s["dg"], 1)

                def largest(i, j):
                    src = sc
                    for r in range(KEEP // 8):
                        found = []
                        for k in (i, j):
                            n = (items[k][0] + 1) * P
                            if r:
                                chain.wait_for(taken[k - i])
                            found.append(chain.mark(v.max(m8[:, k % 2, :], src[:, k % (4 if r == 0 else 2), 0:n])))
                        for k in (i, j):
                            chain.wait_for(found[k - i])
                            if r == 0:
                                v.tensor_scalar(top[:, k % 4:k % 4 + 1], m8[:, k % 2, 0:1], -scale, None, ALU.mult)\
                                    .then_inc(s["tp"], 1)
                        taken = []
                        for k in (i, j):
                            n = (items[k][0] + 1) * P
                            taken.append(chain.mark(v.match_replace(left[:, k % 2, 0:n], m8[:, k % 2, :],
                                                                    src[:, k % (4 if r == 0 else 2), 0:n], TAKEN)))
                        src = left
                    return taken

                masked(0)
                masked(1)
                for i in range(0, N, 2):
                    for k in (i + 2, i + 3):
                        if k < N:
                            masked(k)
                    v.wait_ge(s["dg"], i + 2)
                    if items[i][0] >= 1:
                        v.wait_ge(s["cp"], i + 2 - H)
                    taken = largest(i, i + 1)
                    for k in (i, i + 1):
                        c, h = items[k]
                        n = (c + 1) * P
                        chain.wait_for(taken[k - i])
                        v.wait_ge(s["ex"], k + 1)
                        v.scalar_tensor_tensor(out=pe[:, k % 4, 0:n], in0=left[:, k % 2, 0:n], scalar=TAKEN,
                                               in1=pe[:, k % 4, 0:n], op0=ALU.is_equal, op1=ALU.mult,
                                               accum_out=zs[:, c, h:h + 1]).then_inc(s["pk"], 1)
                    if items[i][1] == 6 and items[i][0] >= 1:
                        finish(items[i][0] - 1)
                v.wait_ge(s["pk"], N)
                finish(TB - 1)
                v.wait_ge(s["y"], TB)
                normalise(v, chain, s, w, psY, X)
        nc.all_engine_barrier(sems_to_clear=s["numbers"])


def sign_linear(nc, env, w, b):
    LIMIT = 100.0
    X, XT, ps = w.X, w.XT, w.ps
    W, cols = env.w["sl_w"], env.w["sl_cols"]
    with ExitStack() as ctx:
        sb = lambda n, s: ctx.enter_context(nc.sbuf_tensor("sl_" + n, s, F32))
        sg = sb("signs", [P, P])
        yt = sb("y_t", [P, S])
        s = semaphores(nc, ctx, LN_SEMS + "sg yt cl y")
        with nc.Block() as block:
            @block.tensor
            def _(t):
                t.wait_ge(s["sg"], 1)
                t.matmul(ps[1][:, :], sg[:, :], XT[:, :], start=True, stop=True).then_inc(s["yt"], 1)
                t.wait_ge(s["cl"], 1)
                for c in range(TB):
                    ins = t.transpose(ps[2][:, c * P:(c + 1) * P], yt[:, c * P:(c + 1) * P], env.ident[:, :])
                ins.then_inc(s["y"], 1)
                turn_tokens(t, s, X, ps[0], env.ident)

            @block.scalar
            def _(a):
                std_and_turn(a, s, w, XT, ps[0], env.eps)

            @block.vector
            def _(v):
                chain = Chain(v, s["chain"])
                chain(v.tensor_scalar(sg[:, :], W[:, :], 0.0, 2.0, ALU.is_ge, ALU.mult))
                v.tensor_scalar(sg[:, :], sg[:, :], -1.0, None, ALU.add).then_inc(s["sg"], 1)
                v.wait_ge(s["yt"], 1)
                chain(v.tensor_scalar(yt[:, :], ps[1][:, :], cols[:, 0:1], cols[:, 1:2], ALU.mult, ALU.add))
                v.tensor_scalar(yt[:, :], yt[:, :], -LIMIT, LIMIT, ALU.max, ALU.min).then_inc(s["cl"], 1)
                v.wait_ge(s["y"], 1)
                normalise(v, chain, s, w, ps[2], X)
        nc.all_engine_barrier(sems_to_clear=s["numbers"])


def late_layouts(np, i):
    f32 = np.float32
    o = {}
    WIN, RG = 32, 8
    o["la_w"] = i["L1_attn_w_qkv"].T
    o["la_e"] = np.tile(i["L1_attn_rel_emb"][64 - WIN + 1:65].T, (H, 1))
    o["la_wo"] = i["L1_attn_w_out"].T
    sel = np.zeros((RG, H, RG, H, HD), f32)
    for r in range(RG):
        for h in range(H):
            sel[r, h, r, h, :] = 1.0
    o["la_sel"] = sel.reshape(P, RG, P)
    t, r = np.arange(P)[:, None], np.arange(WIN)[None]
    o["la_mask"] = np.where(t + r < WIN - 1, -1e30, 0.0).astype(f32)
    o["gm_w"] = np.stack([i["L1_ffn_attn_w"].T, i["L1_ffn_next_w"].T], 1)
    o["gm_cols"] = np.stack([i["L1_ffn_ln_scale"], i["L1_ffn_ln_bias"], i["L1_ffn_attn_b"]], 1)
    o["gm_row"] = i["L1_ffn_next_b"][None]
    two = lambda a: a.reshape((2, 4) + a.shape[1:])
    o["gm_w1"] = two(i["L1_ffn_w1"].reshape(8, P, 4, P)).transpose(0, 2, 1, 3, 4)
    o["gm_w2"] = two(i["L1_ffn_w2"].reshape(8, 4, P, P)).transpose(0, 3, 1, 2, 4)
    gb = np.concatenate([i["L1_ffn_b1"].reshape(8, 4, P), i["L1_ffn_b2"][:, None]], 1)
    o["gm_b"] = two(gb).transpose(0, 3, 1, 2)
    order = [8 * (m // 4) + 4 * r + m % 4 for m in range(8) for r in range(2)]
    swap = (np.arange(64) + 32) % 64
    wq = i["L2_attn_Wq"].reshape(16, 64, P)[order]
    wk = i["L2_attn_Wk"].reshape(4, 64, P)
    chunks = lambda a: np.stack([a.reshape(-1, P, P).transpose(2, 0, 1), a[:, swap].reshape(-1, P, P).transpose(2, 0, 1)], 1)
    o["lt_wq"], o["lt_wk"] = chunks(wq), chunks(wk)
    o["lt_wv"] = i["L2_attn_Wv"].T
    o["lt_wo"] = i["L2_attn_Wo"].T.reshape(16, 64, P)[order].reshape(8, P, P).transpose(1, 0, 2)
    inv = 1.0 / 10000.0 ** (np.arange(0, 64, 2, dtype=np.float64) / 64)
    freqs = np.outer(np.arange(S, dtype=np.float64), inv)
    emb = np.concatenate([freqs, freqs], -1).T
    sign = np.where(np.arange(64) < 32, -1.0, 1.0)[:, None]
    o["lt_rope"] = np.stack([np.tile(np.cos(emb), (2, 1)), np.tile(np.sin(emb) * sign, (2, 1))], 1).astype(f32)
    slope = 2.0 ** (-8.0 / 16 * (np.arange(16) + 1))
    lag = np.arange(S)[None] - np.arange(P)[:, None]
    o["lt_decay"] = np.where(lag[:, None] >= 0, np.exp(-slope[None, :, None] * np.maximum(lag, 0)[:, None]), 0.0).astype(f32)
    o["sm_gate"] = i["L2_ffn_Wg"]
    o["sm_w1"] = i["L2_ffn_w1"].reshape(P, 4, P)
    o["sm_w2"] = i["L2_ffn_w2"].reshape(4, P, P).transpose(1, 0, 2)
    o["sa_w"] = np.concatenate([i["L3_attn_wq"].T, i["L3_attn_wk"].T, i["L3_attn_wv"].T], 1)
    o["sa_wo"] = i["L3_attn_wo"].T
    o["sa_desc"] = np.tile(np.arange(8, 0, -1, dtype=f32), (P, 1))
    o["sa_causal"] = np.where(np.arange(P)[None] > np.arange(P)[:, None], -1e30, 0.0).astype(f32)
    o["sl_w"] = i["L3_ffn_weights"].T
    o["sl_cols"] = np.stack([i["L3_ffn_scale"], i["L3_ffn_bias"]], 1)
    return o


class Env:
    pass


def program(nc, d, out):
    env = Env()
    env.d = d
    env.mamba_layers = 4
    with ExitStack() as ctx:
        sb = lambda n, s: ctx.enter_context(nc.sbuf_tensor(n, s, F32))
        env.banks = [ctx.enter_context(nc.psum_tensor(f"bank{i}", [P, S], F32)) for i in range(8)]
        env.X = sb("x_tokens", [P, NT, P])
        env.ident = sb("identity", [P, P])
        env.eps = sb("eps", [P, 1])
        env.one = sb("ones", [P, 1])
        loads = [(env.X[:, :, :], d["x"].rearrange("b (c p) n -> p (b c) n", p=P)), (env.ident[:, :], d["ident"])]
        loads += load_common(nc, env, ctx)
        inputs_loaded, output_stored = (ctx.enter_context(nc.semaphore(n)) for n in ("inputs_loaded", "output_stored"))
        with nc.Block() as block:
            @block.sync
            def _(sp):
                for dst, src in loads:
                    sp.dma_start(dst, src).then_inc(inputs_loaded, 16)
                sp.wait_ge(inputs_loaded, 16 * len(loads))

            @block.vector
            def _(v):
                v.memset(env.eps[:, :], EPS)
                v.memset(env.one[:, :], 1.0)
                v.memset(env.one_row[:, :], 1.0)
        if 0 in STAGES:
            mamba(nc, env)
        if 1 in STAGES:
            with ExitStack() as inner:
                w = Batch(nc, inner, env.banks, "early_")
                with nc.Fori(0, B) as b:
                    enter_batch(nc, env, w, b)
                    cross_attention(nc, env, w, "x0", b, HD ** -0.5, True, False, False)
                    leave_batch(nc, env, w, b)
        if 2 in STAGES:
            moe(nc, env)
        if max(STAGES) >= 3:
            with ExitStack() as inner:
                w = Batch(nc, inner, env.banks, "late_")
                load_late(nc, env, inner)
                with nc.Fori(0, B) as b:
                    enter_batch(nc, env, w, b)
                    if 3 in STAGES:
                        local_attention(nc, env, w, b)
                    if 4 in STAGES:
                        context_mlp(nc, env, w, b)
                    if 5 in STAGES:
                        grouped_mlp(nc, env, w, b)
                    if 6 in STAGES:
                        lightning(nc, env, w, b)
                    if 7 in STAGES:
                        cross_attention(nc, env, w, "x2", b, HD ** -0.5, False, True, False)
                    if 8 in STAGES:
                        shared_moe(nc, env, w, b)
                    if 9 in STAGES:
                        sparse_attention(nc, env, w, b)
                    if 10 in STAGES:
                        cross_attention(nc, env, w, "x3", b, HD ** -0.5, False, True, True)
                    if 11 in STAGES:
                        sign_linear(nc, env, w, b)
                    leave_batch(nc, env, w, b)
        with nc.Block() as block:
            @block.sync
            def _(sp):
                sp.dma_start(out.rearrange("b (c p) n -> p (b c) n", p=P), env.X[:, :, :]).then_inc(output_stored, 16)
                sp.wait_ge(output_stored, 16)


def layouts(np, i):
    L, DI, NS, R, NF = 4, 256, 16, 8, 2
    halves = lambda a: np.moveaxis(a.reshape(L, NF, P, -1), 1, 2)
    pc = np.concatenate([i["L0_attn_conv_w"], i["L0_attn_conv_b"][..., None], i["L0_attn_b_dt"][..., None],
                         i["L0_attn_Dp"][..., None], i["L0_attn_A_log"]], -1)
    flat = lambda a: a.reshape(L, P, -1)
    f32 = np.float32
    o = {
        "x": i["x"],
        "ident": np.eye(P, dtype=f32),
        "mamba_w": np.concatenate([i["L0_attn_W_in"].transpose(0, 2, 1),
                                   flat(halves(i["L0_attn_W_x"].transpose(0, 2, 1))),
                                   flat(halves(i["L0_attn_W_out"].transpose(0, 2, 1))),
                                   flat(halves(pc)),
                                   i["L0_attn_ln_w"][..., None], i["L0_attn_ln_b"][..., None]], -1),
        "mamba_wdt": i["L0_attn_W_dt"].transpose(0, 2, 1),
        "ctx": i["ctx_1024"],
        "ctx_t": i["ctx_1024"].transpose(0, 2, 1),
        "mask": i["mask_BxSxS2_if1"],
        "head_mask": np.repeat(np.eye(H, dtype=f32), HD, axis=0),
        "x0_w": np.stack([i["L0_xattn_W_Q"], i["L0_xattn_W_K"], i["L0_xattn_W_V"], i["L0_xattn_W_O"]], 1),
        "tri": np.triu(np.ones((P, P), f32), 1),
        "desc": np.tile(np.arange(8, 0, -1, dtype=f32), (P, 1)),
        "moe_gate": i["L0_ffn_Wg"].T,
        "moe_w1": i["L0_ffn_W1"].reshape(8, P, 4, P),
        "moe_w2": i["L0_ffn_W2"].reshape(8, 4, P, P).transpose(0, 2, 1, 3),
        "moe_b1": i["L0_ffn_b1"].reshape(8, 4, P).transpose(0, 2, 1),
        "moe_b2": i["L0_ffn_b2"],
    }
    for pre, name in (("x2", "L2_xattn_"), ("x3", "L3_xattn_")):
        o[pre + "_w"] = np.stack([i[name + n].T for n in ("Wq", "Wk", "Wv", "Wo")], 1)
        o[pre + "_cols"] = np.stack([i[name + "bq"], i[name + "bk"]], 1)
        o[pre + "_rows"] = np.stack([i[name + "bv"], i[name + ("bo" if pre == "x3" else "bv")]])[None]
    sel = np.zeros((3, 2 * NS, 2 * NS, P), f32)
    for n in range(2 * NS):
        sel[:, n, n, :] = 1.0
    sel = sel.reshape(6 * NS, 2 * NS, P)
    o["mamba_sel"] = sel
    o.update(late_layouts(np, i))
    return o


def kernel(**inputs):
    import numpy as np
    import concourse.bacc as bacc
    from concourse.bass_utils import run_bass_kernel_spmd as run

    nc = bacc.Bacc("TRN2", target_bir_lowering=False, num_devices=1)
    arrays, d = {}, {}
    for name, a in layouts(np, inputs).items():
        a = np.ascontiguousarray(a)
        arrays["in_" + name] = a
        d[name] = nc.dram_tensor("in_" + name, a.shape, mybir.dt.from_np(a.dtype), kind="ExternalInput").ap()
    out = nc.dram_tensor("out", (B, S, P), F32, kind="ExternalOutput").ap()
    program(nc, d, out)
    return run(nc, [arrays], core_ids=[0]).results[0]["out"]
```

```python
import concourse.bass as bass
from concourse import mybir
from contextlib import ExitStack

F32 = mybir.dt.float32
I32 = mybir.dt.int32
BF16 = mybir.dt.bfloat16
ALU = mybir.AluOpType
ACT = mybir.ActivationFunctionType
AX = mybir.AxisListType

P = 128
B = 4
S = 512
TB = S // P
NT = B * TB
EPS = 1e-5
H = 16
HD = P // H
SK = 77
STAGES = range(12)
FIRST_SEM = 110


class Chain:

    def __init__(self, eng, sem):
        self.eng, self.sem, self.n = eng, sem, 0

    def __call__(self, ins):
        self.n += 1
        ins.then_inc(self.sem, 1)
        self.eng.wait_ge(self.sem, self.n)

    def mark(self, ins):
        self.n += 1
        ins.then_inc(self.sem, 1)
        return self.n

    def wait_for(self, n):
        self.eng.wait_ge(self.sem, n)


def semaphores(nc, ctx, names):
    names = names.split()
    handles = [ctx.enter_context(nc.semaphore(n, num=FIRST_SEM + i)) for i, n in enumerate(names)]
    return dict(zip(names, handles), numbers=range(FIRST_SEM, FIRST_SEM + len(names)))


def layer_norm_stats(v, chain, src, st, mv, tiles, s_var):
    for t in range(tiles):
        ins = v.bn_stats(st[:, t, :], src[:, t, :])
    chain(ins)
    for t in range(tiles):
        ins = v.bn_aggr(mv[:, t, :], st[:, t, :])
    ins.then_inc(s_var, 1)


def mamba(nc, env):
    DI, NS, R, K = 256, 16, 8, 4
    NF = DI // P
    X = env.X
    cols, at = {}, 0
    NX = 3 * 2 * NS
    for name, n in (("wi", 2 * DI), ("wx", NF * (R + 2 * NS)), ("wo", NF * P), ("pc", NF * (K + 3 + NS)), ("ln", 2)):
        cols[name] = (at, at + n)
        at += n
    with ExitStack() as ctx:
        sb = lambda n, s, t=F32: ctx.enter_context(nc.sbuf_tensor(n, s, t))
        wl = sb("mamba_w", [P, at])
        wdt = sb("mamba_wdt", [R, DI])
        sel32 = sb("state_selector_f32", [NX, 2 * NS, P])
        sel = sb("state_selector", [NX, 2 * NS, P], BF16)
        wx3 = sb("wx_three_times", [P, NF, NX])
        X0 = sb("x_before_mamba", [P, NT, P])
        xh = sb("x_normed", [P, NT, P])
        st = sb("bn_stats", [P, NT, 6])
        mv = sb("mean_var", [P, NT, 2])
        sd = sb("std", [P, NT])
        rs = sb("rstd", [P, NT])
        xn = sb("xn_t", [P, B, S])
        xp = sb("xs_padded", [P, 2, NF, K - 1 + S])
        sz = sb("silu_z", [P, B, NF, S])
        cv = sb("conv", [P, 2, NF, S])
        u = sb("u", [P, B, NF, S])
        xd = sb("dt_low_rank", [R, B, S])
        bc = sb("b_c_rows", [NX, 2, S])
        bcp = sb("b_c_part", [NX, S], BF16)
        bc3 = sb("b_c_parts", [NX, B, S], BF16)
        dt = sb("dt", [P, B, NF, S])
        dtu = sb("dtu", [P, B, NF, S])
        an = sb("a_neg", [P, NF, NS])
        dA = sb("dA", [P, 4, S])
        dBu = sb("dBu", [P, 3, S])
        hs = sb("h_states", [P, 4, S])
        cs = sb("c_copy", [P, 2, S])
        hc = cv[:, :, :, :].rearrange("p a f s -> p (a f) s")
        yt = sb("y_t", [P, NF, S])
        ps = env.banks
        s = semaphores(nc, ctx, "m_w m_var m_sd m_vc m_xh m_xt m_xn m_pj m_pje m_cv m_u m_xd m_xde m_dtp m_v m_e m_l m_dt "
                          "m_wx m_bcx m_bce m_bcs m_ae m_a m_bc m_da m_dbu m_cs m_hs m_hc m_yt m_o m_sel m_xa m_ga m_ra")
        wi = wl[:, cols["wi"][0]:cols["wi"][1]]
        wx = wl[:, cols["wx"][0]:cols["wx"][1]].rearrange("p (f n) -> p f n", f=NF)
        wo = wl[:, cols["wo"][0]:cols["wo"][1]].rearrange("p (f n) -> p f n", f=NF)
        pc = wl[:, cols["pc"][0]:cols["pc"][1]].rearrange("p (f n) -> p f n", f=NF)
        lnw, lnb = (wl[:, cols["ln"][0] + i:cols["ln"][0] + i + 1] for i in range(2))
        CB, BDT, DP, AL = K, K + 1, K + 2, K + 3
        psB, psC = ps[0:2], ps[2:4]
        psY = lambda b, f: ps[4 + 2 * (b % 2) + f]

        with nc.Block() as block:
            @block.sync
            def _(sp_):
                sp_.dma_start(sel32[:, :, :], env.d["mamba_sel"]).then_inc(s["m_sel"], 16)
                sp_.wait_ge(s["m_sel"], 16)

            @block.vector
            def _(v):
                v.tensor_copy(X0[:, :, :], X[:, :, :])
                v.memset(xp[:, :, :, :], 0.0)
                v.wait_ge(s["m_sel"], 16)
                v.tensor_copy(sel[:, :, :], sel32[:, :, :])
        nc.all_engine_barrier(sems_to_clear=s["numbers"])

        with nc.Fori(0, env.mamba_layers) as layer:
            with nc.Block() as block:
                @block.sync
                def _(sp_):
                    sp_.dma_start(wl[:, :], env.d["mamba_w"][bass.ds(layer, 1), :, :].rearrange("o p n -> p (o n)"))\
                        .then_inc(s["m_w"], 16)
                    sp_.dma_start(wdt[:, :], env.d["mamba_wdt"][bass.ds(layer, 1), :, :].rearrange("o p n -> p (o n)"))\
                        .then_inc(s["m_w"], 16)

                @block.vector
                def _(v):
                    chain = Chain(v, s["m_vc"])
                    layer_norm_stats(v, chain, X, st, mv, NT, s["m_var"])
                    v.wait_ge(s["m_sd"], 1)
                    chain(v.reciprocal(rs[:, :], sd[:, :]))
                    for t in range(NT):
                        v.tensor_scalar(xh[:, t, :], X[:, t, :], mv[:, t, 0:1], rs[:, t:t + 1],
                                        ALU.subtract, ALU.mult).then_inc(s["m_xh"], 1)
                    v.wait_ge(s["m_w"], 32)
                    for b in range(B):
                        for f in range(NF):
                            v.wait_ge(s["m_xa"], NF * b + f + 1)
                            if b >= 2:
                                v.wait_ge(s["m_u"], NF * (b - 2) + f + 1)
                            c = cv[:, b % 2, f, :]
                            chain(v.tensor_scalar(c, xp[:, b % 2, f, 0:S], pc[:, f, 0:1], pc[:, f, CB:CB + 1],
                                                  ALU.mult, ALU.add))
                            for k in range(1, K):
                                ins = v.scalar_tensor_tensor(out=c, in0=xp[:, b % 2, f, k:k + S],
                                                             scalar=pc[:, f, k:k + 1], in1=c,
                                                             op0=ALU.mult, op1=ALU.add)
                                if k < K - 1:
                                    chain(ins)
                            ins.then_inc(s["m_cv"], 1)
                        v.wait_ge(s["m_bce"], b + 1)
                        x = bc[:, b % 2, :]
                        T = 2 * NS
                        for k in range(3):
                            chain(v.tensor_copy(bcp[:, :], x))
                            chain(v.tensor_copy(bc3[k * T:(k + 1) * T, b, :], bcp[k * T:(k + 1) * T, :]))
                            if k < 2:
                                chain(v.tensor_tensor(x, x, bcp[:, :], ALU.subtract))
                        v.sem_inc(s["m_bcs"], 1)
                    v.wait_ge(s["m_ae"], 1)
                    v.tensor_scalar(an[:, :, :], an[:, :, :], -1.0, None, ALU.mult).then_inc(s["m_a"], 1)

                    v.wait_ge(s["m_u"], NF * B)
                    for i in range(B * NF):
                        b, f = divmod(i, NF)
                        v.wait_ge(s["m_dtp"], i + 1)
                        chain(v.tensor_scalar(dt[:, b, f, :], ps[i % 4][:, :], pc[:, f, BDT:BDT + 1], None, ALU.add))
                        v.scalar_tensor_tensor(out=dtu[:, b, f, :], in0=dt[:, b, f, :], scalar=-1.0,
                                               in1=dt[:, b, f, :], op0=ALU.mult, op1=ALU.max).then_inc(s["m_v"], 1)

                    def softplus_out(i):
                        b, f = divmod(i, NF)
                        v.wait_ge(s["m_l"], i + 1)
                        chain(v.scalar_tensor_tensor(out=dt[:, b, f, :], in0=dt[:, b, f, :], scalar=0.0,
                                                     in1=dtu[:, b, f, :], op0=ALU.max, op1=ALU.add))
                        v.tensor_tensor(dtu[:, b, f, :], dt[:, b, f, :], u[:, b, f, :], ALU.mult).then_inc(s["m_dt"], 1)

                    for i in range(NF):
                        softplus_out(i)

                    def gate(b):
                        for f in range(NF):
                            v.wait_ge(s["m_ga"], NF * (NS * b + NS - 1) + f + 1)
                            if b >= 1:
                                v.wait_ge(s["m_o"], b)
                            chain(v.scalar_tensor_tensor(out=yt[:, f, :], in0=u[:, b, f, :], scalar=pc[:, f, DP:DP + 1],
                                                         in1=psY(b, f)[:, :], op0=ALU.mult, op1=ALU.add))
                            v.tensor_tensor(yt[:, f, :], yt[:, f, :], sz[:, b, f, :], ALU.mult).then_inc(s["m_yt"], 1)

                    def residual(b):
                        v.wait_ge(s["m_o"], b + 1)
                        v.tensor_tensor(X[:, TB * b:TB * b + TB, :], X[:, TB * b:TB * b + TB, :],
                                        psY(b, 0)[:, :].rearrange("p (c n) -> p c n", c=TB), ALU.add)\
                            .then_inc(s["m_ra"], 1)

                    def input_term(i):
                        j, f = divmod(i, NF)
                        b, n = divmod(j, NS)
                        v.wait_ge(s["m_bc"], j + 1)
                        if i >= 3:
                            v.wait_ge(s["m_hs"], i - 2)
                        v.tensor_tensor(dBu[:, i % 3, :], psB[n % 2][:, :], dtu[:, b, f, :], ALU.mult)\
                            .then_inc(s["m_dbu"], 1)

                    def scan(i):
                        v.wait_ge(s["m_dbu"], i + 1)
                        v.wait_ge(s["m_da"], i + 1)
                        if i >= 4:
                            v.wait_ge(s["m_hc"], i - 3)
                        v.tensor_tensor_scan(hs[:, i % 4, :], dA[:, i % 4, :], dBu[:, i % 3, :], 0.0,
                                             ALU.mult, ALU.add).then_inc(s["m_hs"], 1)

                    for i in range(B * NS * NF):
                        j, f = divmod(i, NF)
                        b, n = divmod(j, NS)
                        if f == 0 and n == 8 and b + 1 < B:
                            softplus_out(NF * b + NF)
                            softplus_out(NF * b + NF + 1)
                            v.wait_ge(s["m_dt"], NF * (b + 2))
                        if i == 0:
                            v.wait_ge(s["m_dt"], NF)
                        input_term(i)
                        if i >= 1:
                            scan(i - 1)
                        if f == 1 and b >= 1 and n == 2:
                            gate(b - 1)
                        if f == 1 and b >= 1 and n == 6:
                            residual(b - 1)
                    scan(B * NS * NF - 1)
                    gate(B - 1)
                    residual(B - 1)

                @block.gpsimd
                def _(g):
                    for i in range(B * NS * NF):
                        g.wait_ge(s["m_hs"], i + 1)
                        g.wait_ge(s["m_cs"], i // NF + 1)
                        if i >= 4:
                            g.wait_ge(s["m_ga"], i - 3)
                        g.tensor_tensor(hc[:, i % 4, :], hs[:, i % 4, :], cs[:, (i // NF) % 2, :], ALU.mult)\
                            .then_inc(s["m_hc"], 1)

                @block.scalar
                def _(a):
                    a.wait_ge(s["m_var"], 1)
                    a.activation(sd[:, :], mv[:, :, 1], ACT.Sqrt, bias=env.eps[:, 0:1]).then_inc(s["m_sd"], 1)
                    a.wait_ge(s["m_w"], 32)
                    for x in range(3):
                        ins = a.activation(wx3[:, :, 2 * NS * x:2 * NS * (x + 1)], wx[:, :, R:], ACT.Copy)
                    ins.then_inc(s["m_wx"], 1)

                    def normed(b):
                        a.wait_ge(s["m_xt"], b + 1)
                        a.activation(xn[:, b, :], ps[4 + b % 2][:, :], ACT.Identity, scale=lnw, bias=lnb)\
                            .then_inc(s["m_xn"], 1)

                    normed(0)
                    for b in range(B):
                        if b + 1 < B:
                            normed(b + 1)
                        for m in range(4):
                            a.wait_ge(s["m_pj"], 4 * b + m + 1)
                            if m < NF:
                                if b >= 2:
                                    a.wait_ge(s["m_cv"], NF * (b - 2) + m + 1)
                                a.activation(xp[:, b % 2, m, K - 1:K - 1 + S], ps[m][:, :], ACT.Copy)\
                                    .then_inc(s["m_xa"], 1)
                            else:
                                a.activation(sz[:, b, m - NF, :], ps[m][:, :], ACT.Silu).then_inc(s["m_pje"], 1)
                        for f in range(NF):
                            a.wait_ge(s["m_cv"], NF * b + f + 1)
                            a.activation(u[:, b, f, :], cv[:, b % 2, f, :], ACT.Silu).then_inc(s["m_u"], 1)
                        a.wait_ge(s["m_xd"], b + 1)
                        a.activation(xd[:, b, :], ps[6][0:R, :], ACT.Copy).then_inc(s["m_xde"], 1)
                        if b >= 2:
                            a.wait_ge(s["m_bcs"], b - 1)
                        a.activation(bc[:, b % 2, :], ps[7][0:NX, :], ACT.Copy).then_inc(s["m_bce"], 1)
                    a.activation(an[:, :, :], pc[:, :, AL:AL + NS], ACT.Exp).then_inc(s["m_ae"], 1)
                    for i in range(B * NF):
                        a.wait_ge(s["m_v"], i + 1)
                        x = dtu[:, i // NF, i % NF, :]
                        a.activation(x, x, ACT.Exp, scale=-1.0).then_inc(s["m_e"], 1)
                    for i in range(B * NF):
                        a.wait_ge(s["m_e"], i + 1)
                        x = dtu[:, i // NF, i % NF, :]
                        a.activation(x, x, ACT.Ln, bias=env.one[:, 0:1]).then_inc(s["m_l"], 1)
                    a.wait_ge(s["m_a"], 1)
                    for j in range(B * NS):
                        b, n = divmod(j, NS)
                        for f in range(NF):
                            i = j * NF + f
                            a.wait_ge(s["m_dt"], NF * b + f + 1)
                            if i >= 4:
                                a.wait_ge(s["m_hs"], i - 3)
                            a.activation(dA[:, i % 4, :], dt[:, b, f, :], ACT.Exp, scale=an[:, f, n:n + 1])\
                                .then_inc(s["m_da"], 1)
                        a.wait_ge(s["m_bc"], j + 1)
                        if j >= 2:
                            a.wait_ge(s["m_hc"], NF * (j - 1))
                        a.activation(cs[:, j % 2, :], psC[j % 2][:, :], ACT.Copy).then_inc(s["m_cs"], 1)

                @block.tensor
                def _(t):
                    t.wait_ge(s["m_w"], 32)

                    def turn(b):
                        if b >= 2:
                            t.wait_ge(s["m_xn"], b - 1)
                        for c in range(TB):
                            t.wait_ge(s["m_xh"], TB * b + c + 1)
                            ins = t.transpose(ps[4 + b % 2][:, c * P:(c + 1) * P], xh[:, TB * b + c, :], env.ident[:, :])
                        ins.then_inc(s["m_xt"], 1)

                    def project(b):
                        t.wait_ge(s["m_xn"], b + 1)
                        if b >= 1:
                            t.wait_ge(s["m_xa"], NF * b)
                            t.wait_ge(s["m_pje"], NF * b)
                        for m in range(4):
                            t.matmul(ps[m][:, :], wi[:, m * P:(m + 1) * P], xn[:, b, :],
                                     start=True, stop=True).then_inc(s["m_pj"], 1)

                    def x_dbl(b):
                        if b >= 1:
                            t.wait_ge(s["m_xde"], b)
                            t.wait_ge(s["m_bce"], b)
                        t.wait_ge(s["m_wx"], 1)
                        for f in range(NF):
                            t.wait_ge(s["m_u"], NF * b + f + 1)
                            t.matmul(ps[6][0:R, :], wx[:, f, 0:R], u[:, b, f, :], start=(f == 0), stop=(f == NF - 1))
                            ins = t.matmul(ps[7][0:NX, :], wx3[:, f, :], u[:, b, f, :], start=(f == 0), stop=(f == NF - 1))
                        ins.then_inc(s["m_xd"], 1)

                    turn(0)
                    turn(1)
                    for b in range(B):
                        project(b)
                        if b + 2 < B:
                            turn(b + 2)
                        if b >= 1:
                            x_dbl(b - 1)
                    x_dbl(B - 1)
                    t.wait_ge(s["m_pje"], NF * B)
                    t.wait_ge(s["m_xa"], NF * B)
                    for i in range(B * NF):
                        b, f = divmod(i, NF)
                        t.wait_ge(s["m_xde"], b + 1)
                        if i >= 4:
                            t.wait_ge(s["m_v"], i - 3)
                        t.matmul(ps[i % 4][:, :], wdt[:, f * P:(f + 1) * P], xd[0:R, b, :],
                                 start=True, stop=True).then_inc(s["m_dtp"], 1)
                    t.wait_ge(s["m_v"], B * NF)

                    def spread(j):
                        b, n = divmod(j, NS)
                        if j >= 2:
                            t.wait_ge(s["m_dbu"], NF * (j - 1))
                            t.wait_ge(s["m_cs"], j - 1)
                        t.matmul(psB[j % 2][:, :], sel[:, n, :], bc3[:, b, :], start=True, stop=True)
                        t.matmul(psC[j % 2][:, :], sel[:, NS + n, :], bc3[:, b, :], start=True, stop=True)\
                            .then_inc(s["m_bc"], 1)

                    def gather(i):
                        b, r = divmod(i, NF * NS)
                        n, f = divmod(r, NF)
                        t.wait_ge(s["m_hc"], i + 1)
                        if n == 0 and b >= 2:
                            t.wait_ge(s["m_ra"], b - 1)
                        t.matmul(psY(b, f)[:, :], env.ident[:, :], hc[:, i % 4, :], start=(n == 0), stop=(n == NS - 1))\
                            .then_inc(s["m_ga"], 1)

                    def out(b):
                        for c in range(TB):
                            for f in range(NF):
                                t.wait_ge(s["m_yt"], NF * b + f + 1)
                                ins = t.matmul(psY(b, 0)[:, c * P:(c + 1) * P], yt[:, f, c * P:(c + 1) * P],
                                               wo[:, f, :], start=(f == 0), stop=(f == NF - 1))
                        ins.then_inc(s["m_o"], 1)

                    t.wait_ge(s["m_bcs"], B)
                    spread(0)
                    for b in range(B):
                        for n in range(NS):
                            j = b * NS + n
                            if j + 1 < B * NS:
                                spread(j + 1)
                            for f in range(NF if j else 0):
                                gather(NF * (j - 1) + f)
                            if b >= 1 and n == 4:
                                out(b - 1)
                    for f in range(NF):
                        gather(NF * (B * NS - 1) + f)
                    out(B - 1)
            nc.all_engine_barrier(sems_to_clear=s["numbers"])

        with nc.Block() as block:
            finish_layer_norm(block, X, X0, xh, st, mv, sd, rs, NT, env, s["m_vc"], s["m_var"], s["m_sd"], s["m_v"])
        nc.all_engine_barrier(sems_to_clear=s["numbers"])


def finish_layer_norm(block, X, Y, R, st, mv, sd, rs, tiles, env, s_chain, s_var, s_sd, s_done):
    @block.vector
    def _(v):
        chain = Chain(v, s_chain)
        chain(v.tensor_tensor(R[:, :, :], X[:, :, :], Y[:, :, :], ALU.add))
        layer_norm_stats(v, chain, R, st, mv, tiles, s_var)
        v.wait_ge(s_sd, 1)
        chain(v.reciprocal(rs[:, :], sd[:, :]))
        for t in range(tiles):
            v.tensor_scalar(X[:, t, :], R[:, t, :], mv[:, t, 0:1], rs[:, t:t + 1], ALU.subtract, ALU.mult)\
                .then_inc(s_done, 1)

    @block.scalar
    def _(a):
        a.wait_ge(s_var, 1)
        a.activation(sd[:, :], mv[:, :, 1], ACT.Sqrt, bias=env.eps[:, 0:1]).then_inc(s_sd, 1)


def normalise(v, chain, sm, w, y, X):
    if len(y.shape) == 2:
        y = y[:, :].rearrange("p (c n) -> p c n", c=TB)
    chain(v.tensor_tensor(w.R[:, :, :], X[:, :, :], y[:, :, :], ALU.add))
    found = [chain.mark(v.bn_stats(w.st[:, c, :], w.R[:, c, :])) for c in range(TB)]
    for c in range(TB):
        chain.wait_for(found[c])
        ins = v.bn_aggr(w.mv[:, c, :], w.st[:, c, :])
    ins.then_inc(sm["var"], 1)
    v.wait_ge(sm["sd"], 1)
    chain(v.reciprocal(w.rs[:, :], w.sd[:, :]))
    for c in range(TB):
        v.tensor_scalar(X[:, c, :], w.R[:, c, :], w.mv[:, c, 0:1], w.rs[:, c:c + 1],
                        ALU.subtract, ALU.mult).then_inc(sm["xn"], 1)


def turn_tokens(t, sm, X, banks, ident):
    for c in range(TB):
        t.wait_ge(sm["xn"], c + 1)
        ins = t.transpose(banks[c // 2][:, (c % 2) * P:(c % 2 + 1) * P], X[:, c, :], ident[:, :])
        if c % 2:
            ins.then_inc(sm["tr"], 1)


def std_and_turn(a, sm, w, XT, banks, eps, following):
    a.activation(w.scrap[:, 0:1], eps[:, 0:1], ACT.Sqrt)
    a.wait_ge(sm["var"], 1)
    a.activation(w.sd[:, :], w.mv[:, :, 1], ACT.Sqrt, bias=eps[:, 0:1]).then_inc(sm["sd"], 1)
    a.activation(w.scrap[:, 1:2], eps[:, 0:1], following)
    for i in range(2):
        a.wait_ge(sm["tr"], i + 1)
        a.activation(XT[:, 2 * i * P:2 * (i + 1) * P], banks[i][:, 0:2 * P], ACT.Copy)


LN_SEMS = "var sd xn tr chain "


class Batch:

    def __init__(self, nc, ctx, banks, tag):
        sb = lambda n, s: ctx.enter_context(nc.sbuf_tensor(tag + n, s, F32))
        self.X = sb("tokens", [P, TB, P])
        self.XT = sb("t", [P, S])
        self.ctxT = sb("ctx_t", [P, SK])
        self.ctx = sb("ctx", [SK, P])
        self.R = sb("residual", [P, TB, P])
        self.st = sb("bn_stats", [P, TB, 6])
        self.mv = sb("mean_var", [P, TB, 2])
        self.sd = sb("std", [P, TB])
        self.rs = sb("rstd", [P, TB])
        self.scrap = sb("scrap", [P, 2])
        self.ps = banks


def enter_batch(nc, env, w, b):
    with ExitStack() as ctx:
        s = semaphores(nc, ctx, "ctx_loaded copied turned")
        with nc.Block() as block:
            @block.sync
            def _(sp):
                sp.dma_start(w.ctxT[:, :], env.d["ctx_t"][bass.ds(b, 1), :, :].rearrange("o p n -> p (o n)")).then_inc(s["ctx_loaded"], 16)
                sp.dma_start(w.ctx[:, :], env.d["ctx"][bass.ds(b, 1), :, :].rearrange("o p n -> p (o n)")).then_inc(s["ctx_loaded"], 16)
                sp.wait_ge(s["ctx_loaded"], 32)

            @block.vector
            def _(v):
                v.tensor_copy(w.X[:, :, :], env.X[:, bass.ds(b * TB, TB), :]).then_inc(s["copied"], 1)

            @block.tensor
            def _(t):
                t.wait_ge(s["copied"], 1)
                for c in range(TB):
                    ins = t.transpose(w.ps[0][:, c * P:(c + 1) * P], w.X[:, c, :], env.ident[:, :])
                ins.then_inc(s["turned"], 1)

            @block.scalar
            def _(a):
                a.wait_ge(s["turned"], 1)
                a.activation(w.XT[:, :], w.ps[0][:, :], ACT.Copy)
        nc.all_engine_barrier(sems_to_clear=s["numbers"])


def leave_batch(nc, env, w, b):
    with nc.Block() as block:
        @block.vector
        def _(v):
            v.tensor_copy(env.X[:, bass.ds(b * TB, TB), :], w.X[:, :, :])


def cross_attention(nc, env, w, pre, b, scale, masked, biased, out_bias):
    wt = env.weights[pre]
    cols = env.columns.get(pre)
    rows = env.rows.get(pre)
    GH = (0, 6, 12, 16)
    NG = len(GH) - 1
    X, XT, ps = w.X, w.XT, w.ps
    with ExitStack() as ctx:
        sb = lambda n, s, t=F32: ctx.enter_context(nc.sbuf_tensor(pre + n, s, t))
        kt = sb("k_t", [P, SK])
        kb = sb("k_by_head", [P, H, SK])
        vv = sb("v", [SK, P])
        qt = sb("q_t", [P, S])
        D = sb("scores", [P, 2, H, SK])
        mx = sb("max", [P, 2, H])
        zs = sb("sum", [P, 2, H])
        pt = sb("p_t", [SK, H, P])
        o = sb("o", [P, 2, P])
        ot = sb("o_t", [P, 2, P])
        if masked:
            mi = sb("mask_int", [P, TB, SK], I32)
            mf = sb("mask", [P, TB, SK])
            pen = sb("penalty", [P, TB, SK])
        s = semaphores(nc, ctx, LN_SEMS + "proj kt q vv kb sc dd ex pt pte pv on ot ote y mk")
        psS, psT, psV, psO, psY = ps[0:3], ps[3:5], ps[5], ps[6], ps[7]
        with nc.Block() as block:
            @block.sync
            def _(sp):
                if masked:
                    src = env.d["mask"][bass.ds(b, 1), :, :].rearrange("o (c p) n -> p (o c) n", p=P)
                    sp.dma_start(mi[:, :, :], src).then_inc(s["mk"], 16)
                    sp.wait_ge(s["mk"], 16)

            @block.tensor
            def _(t):
                t.matmul(psS[0][:, 0:SK], wt[:, 1, :], w.ctxT[:, :], start=True, stop=True).then_inc(s["proj"], 1)
                t.matmul(psS[1][:, :], wt[:, 0, :], XT[:, :], start=True, stop=True).then_inc(s["proj"], 1)
                ins = t.matmul(psS[2][0:SK, 0:P], w.ctxT[:, :], wt[:, 2, :], start=True, stop=not biased)
                if biased:
                    ins = t.matmul(psS[2][0:SK, 0:P], env.one_row[0:1, 0:SK], rows[0:1, 0, :], start=False, stop=True)
                ins.then_inc(s["proj"], 1)

                def scores(c):
                    t.wait_ge(s["kb"], 1)
                    t.wait_ge(s["q"], 1)
                    t.wait_ge(s["vv"], 1)
                    if c >= 1:
                        t.wait_ge(s["dd"], NG * c)
                    for g in range(NG):
                        n = (GH[g + 1] - GH[g]) * SK
                        t.matmul(psS[g][:, 0:n], qt[:, c * P:(c + 1) * P],
                                 kb[:, GH[g]:GH[g + 1], :].rearrange("p h n -> p (h n)"),
                                 start=True, stop=True).then_inc(s["sc"], 1)

                def turn_and_weigh(c):
                    t.wait_ge(s["ex"], c + 1)
                    for q in range(4):
                        i = 4 * c + q
                        if i >= 2:
                            t.wait_ge(s["pte"], i - 1)
                        for k in range(4):
                            ins = t.transpose(psT[i % 2][0:SK, k * P:(k + 1) * P], D[:, c % 2, 4 * q + k, :],
                                              env.ident[:, :])
                        ins.then_inc(s["pt"], 1)
                    if c >= 1:
                        t.wait_ge(s["on"], c)
                    for h in range(H):
                        t.wait_ge(s["pte"], 4 * c + h // 4 + 1)
                        ins = t.matmul(psV[:, h * HD:(h + 1) * HD], pt[:, h, :], vv[:, h * HD:(h + 1) * HD],
                                       start=True, stop=True)
                    ins.then_inc(s["pv"], 1)

                def project(c):
                    t.wait_ge(s["on"], c + 1)
                    if c >= 1:
                        t.wait_ge(s["ote"], c)
                    t.transpose(psO[:, 0:P], o[:, c % 2, :], env.ident[:, :]).then_inc(s["ot"], 1)
                    t.wait_ge(s["ote"], c + 1)
                    ins = t.matmul(psY[:, c * P:(c + 1) * P], ot[:, c % 2, :], wt[:, 3, :], start=True, stop=not out_bias)
                    if out_bias:
                        ins = t.matmul(psY[:, c * P:(c + 1) * P], env.one_row[0:1, :], rows[0:1, 1, :],
                                       start=False, stop=True)
                    ins.then_inc(s["y"], 1)

                scores(0)
                for c in range(TB):
                    if c + 1 < TB:
                        scores(c + 1)
                    turn_and_weigh(c)
                    if c >= 1:
                        project(c - 1)
                project(TB - 1)
                turn_tokens(t, s, X, ps[0:2], env.ident)

            @block.scalar
            def _(a):
                a.wait_ge(s["proj"], 1)
                if biased:
                    a.activation(kt[:, :], psS[0][:, 0:SK], ACT.Identity, bias=cols[:, 1:2]).then_inc(s["kt"], 1)
                else:
                    a.activation(kt[:, :], psS[0][:, 0:SK], ACT.Copy).then_inc(s["kt"], 1)
                a.wait_ge(s["proj"], 2)
                if biased:
                    a.activation(qt[:, :], psS[1][:, :], ACT.Identity, bias=cols[:, 0:1]).then_inc(s["q"], 1)
                else:
                    a.activation(qt[:, :], psS[1][:, :], ACT.Copy).then_inc(s["q"], 1)
                a.wait_ge(s["proj"], 3)
                a.activation(vv[:, :], psS[2][0:SK, 0:P], ACT.Copy).then_inc(s["vv"], 1)

                def exps(c):
                    a.wait_ge(s["dd"], NG * (c + 1))
                    a.activation(D[:, c % 2, :, :], D[:, c % 2, :, :], ACT.Exp, scale=scale).then_inc(s["ex"], 1)

                def p_out(c):
                    for q in range(4):
                        i = 4 * c + q
                        a.wait_ge(s["pt"], i + 1)
                        if c >= 1:
                            a.wait_ge(s["pv"], c)
                        a.activation(pt[:, 4 * q:4 * q + 4, :],
                                     psT[i % 2][0:SK, :].rearrange("p (k n) -> p k n", k=4), ACT.Copy).then_inc(s["pte"], 1)

                def o_out(c):
                    a.wait_ge(s["ot"], c + 1)
                    if c >= 2:
                        a.wait_ge(s["y"], c - 1)
                    a.activation(ot[:, c % 2, :], psO[:, 0:P], ACT.Copy).then_inc(s["ote"], 1)

                for c in range(TB):
                    exps(c)
                    p_out(c)
                    if c >= 1:
                        o_out(c - 1)
                o_out(TB - 1)
                std_and_turn(a, s, w, XT, ps[0:2], env.eps, ACT.Exp if pre == "x2" else ACT.Copy)

            @block.vector
            def _(v):
                chain = Chain(v, s["chain"])
                v.wait_ge(s["kt"], 1)
                v.tensor_tensor(kb[:, :, :], kt[:, None, :].broadcast_to([P, H, SK]),
                                env.head_mask[:, :, None].broadcast_to([P, H, SK]), ALU.mult).then_inc(s["kb"], 1)
                if masked:
                    v.wait_ge(s["mk"], 16)
                    chain(v.tensor_scalar(mf[:, :, :], mi[:, :, :], 0.0, None, ALU.not_equal))
                    chain(v.tensor_scalar(pen[:, :, :], mf[:, :, :], -1.0, 1e9 / scale, ALU.add, ALU.mult))

                def shifted(c):
                    if c >= 2:
                        v.wait_ge(s["pt"], 4 * (c - 1))
                    for g in range(NG):
                        a0, a1 = GH[g], GH[g + 1]
                        src = psS[g][:, 0:(a1 - a0) * SK].rearrange("p (h n) -> p h n", n=SK)
                        d = D[:, c % 2, a0:a1, :]
                        v.wait_ge(s["sc"], NG * c + g + 1)
                        if masked:
                            m, q = (x[:, c:c + 1, :].broadcast_to([P, a1 - a0, SK]) for x in (mf, pen))
                            chain(v.tensor_tensor(d, src, m, ALU.mult))
                            chain(v.tensor_tensor(d, d, q, ALU.add))
                            src = d
                        chain(v.tensor_reduce(mx[:, c % 2, a0:a1], src, AX.X, ALU.max))
                        v.tensor_tensor(d, src, mx[:, c % 2, a0:a1, None].broadcast_to([P, a1 - a0, SK]),
                                        ALU.subtract).then_inc(s["dd"], 1)

                def weighed(c):
                    v.wait_ge(s["ex"], c + 1)
                    chain(v.tensor_reduce(zs[:, c % 2, :], D[:, c % 2, :, :], AX.X, ALU.add))
                    chain(v.reciprocal(zs[:, c % 2, :], zs[:, c % 2, :]))
                    v.wait_ge(s["pv"], c + 1)
                    if c >= 2:
                        v.wait_ge(s["ot"], c - 1)
                    v.tensor_tensor(o[:, c % 2, :].rearrange("p (h n) -> p h n", n=HD),
                                    psV[:, 0:P].rearrange("p (h n) -> p h n", n=HD),
                                    zs[:, c % 2, :, None].broadcast_to([P, H, HD]), ALU.mult).then_inc(s["on"], 1)

                shifted(0)
                for c in range(TB):
                    if c + 1 < TB:
                        shifted(c + 1)
                    weighed(c)
                v.wait_ge(s["y"], TB)
                normalise(v, chain, s, w, psY, X)
        nc.all_engine_barrier(sems_to_clear=s["numbers"])


def load_common(nc, env, ctx):
    d = env.d
    sb = lambda n, s: ctx.enter_context(nc.sbuf_tensor(n, s, F32))
    env.head_mask = sb("head_mask", [P, H])
    env.one_row = sb("one_row", [1, P])
    env.weights, env.columns, env.rows = {}, {}, {}
    loads = [(env.head_mask[:, :], d["head_mask"])]
    for pre in ("x0", "x2", "x3"):
        env.weights[pre] = sb(pre + "_w", [P, 4, P])
        loads.append((env.weights[pre][:, :, :], d[pre + "_w"]))
        if pre != "x0":
            env.columns[pre] = sb(pre + "_cols", [P, 2])
            loads.append((env.columns[pre][:, :], d[pre + "_cols"]))
            env.rows[pre] = sb(pre + "_rows", [1, 2, P])
            loads.append((env.rows[pre][:, :, :], d[pre + "_rows"]))
    return loads


def moe(nc, env):
    E, HID = 8, 512
    NH = HID // P
    C = int(round(2 * B * S * 1.05 / E))
    X, d = env.X, env.d
    with ExitStack() as ctx:
        sb = lambda n, s: ctx.enter_context(nc.sbuf_tensor(n, s, F32))
        XT = sb("moe_x_t", [P, NT, P])
        wg = sb("gate_w", [P, E])
        tri = sb("strictly_before", [P, P])
        ones = sb("all_ones", [P, P])
        desc = sb("descending", [P, E])
        lg = sb("gates", [P, NT, E])
        g2 = sb("gates_left", [P, NT, E])
        tmp = sb("gate_tmp", [P, NT, E])
        m = sb("gate_max", [P, 2, NT])
        z = sb("gate_z", [P, NT])
        oh = sb("one_hot", [P, 2, NT, E])
        tot = sb("tile_totals", [P, 2 * NT, E])
        run_ = sb("running_totals", [P, 2 * NT, E])
        cw = sb("combine_w", [P, E, NT])
        w1 = sb("moe_w1", [P, NH, P])
        w2 = sb("moe_w2", [P, NH, P])
        b1 = sb("moe_b1", [P, NH])
        b2 = sb("moe_b2", [1, P])
        hT = sb("moe_h_t", [P, 2, NH, S])
        acc = sb("moe_acc", [P, NT, P])
        st = sb("moe_bn", [P, NT, 6])
        mv = sb("moe_mv", [P, NT, 2])
        sd = sb("moe_sd", [P, NT])
        rs = sb("moe_rs", [P, NT])
        ps = env.banks
        s = semaphores(nc, ctx, "e_ld e_tr e_xt e_lg e_chain e_sub e_exp e_oh e_cnt e_w e_h e_he e_y e_acc e_var e_sd e_done")
        with nc.Block() as block:
            @block.sync
            def _(sp):
                for dst, src in ((wg[:, :], "moe_gate"), (tri[:, :], "tri"), (desc[:, :], "desc")):
                    sp.dma_start(dst, d[src]).then_inc(s["e_ld"], 16)

            @block.tensor
            def _(t):
                for b in range(B):
                    if b >= 2:
                        t.wait_ge(s["e_xt"], b - 1)
                    for c in range(TB):
                        ins = t.transpose(ps[b % 2][:, c * P:(c + 1) * P], X[:, TB * b + c, :], env.ident[:, :])
                    ins.then_inc(s["e_tr"], 1)
                t.wait_ge(s["e_ld"], 48)
                for c in range(NT):
                    t.wait_ge(s["e_xt"], c // TB + 1)
                    ins = t.matmul(ps[2][:, c * E:(c + 1) * E], XT[:, c, :], wg[:, :], start=True, stop=True)
                ins.then_inc(s["e_lg"], 1)
                t.wait_ge(s["e_oh"], 2)
                o = oh[:, :, :, :].rearrange("p k t e -> p (k t e)")
                t.matmul(ps[3][:, 0:2 * NT * E], tri[:, :], o, start=True, stop=True)
                t.matmul(ps[4][:, 0:2 * NT * E], ones[:, :], o, start=True, stop=True).then_inc(s["e_cnt"], 1)

            @block.scalar
            def _(a):
                for b in range(B):
                    a.wait_ge(s["e_tr"], b + 1)
                    a.activation(XT[:, TB * b:TB * b + TB, :], ps[b % 2][:, :].rearrange("p (c n) -> p c n", c=TB),
                                 ACT.Copy).then_inc(s["e_xt"], 1)
                a.wait_ge(s["e_sub"], 1)
                a.activation(lg[:, :, :], lg[:, :, :], ACT.Exp).then_inc(s["e_exp"], 1)

            @block.vector
            def _(v):
                chain = Chain(v, s["e_chain"])
                v.memset(ones[:, :], 1.0)
                v.memset(acc[:, :, :], 0.0)
                bc = lambda a: a[:, :, None].broadcast_to([P, NT, E])
                v.wait_ge(s["e_lg"], 1)
                L = ps[2][:, 0:NT * E].rearrange("p (t e) -> p t e", e=E)
                chain(v.tensor_reduce(z[:, :], L, AX.X, ALU.max))
                v.tensor_tensor(lg[:, :, :], L, bc(z[:, :]), ALU.subtract).then_inc(s["e_sub"], 1)
                v.wait_ge(s["e_exp"], 1)
                chain(v.tensor_reduce(z[:, :], lg[:, :, :], AX.X, ALU.add))
                chain(v.reciprocal(z[:, :], z[:, :]))
                chain(v.tensor_tensor(lg[:, :, :], lg[:, :, :], bc(z[:, :]), ALU.mult))
                v.wait_ge(s["e_ld"], 48)
                G = lg
                for k in range(2):
                    chain(v.tensor_reduce(m[:, k, :], G[:, :, :], AX.X, ALU.max))
                    chain(v.tensor_tensor(tmp[:, :, :], G[:, :, :], bc(m[:, k, :]), ALU.is_equal))
                    chain(v.tensor_tensor(tmp[:, :, :], tmp[:, :, :], desc[:, None, :].broadcast_to([P, NT, E]), ALU.mult))
                    chain(v.tensor_reduce(z[:, :], tmp[:, :, :], AX.X, ALU.max))
                    v.tensor_tensor(oh[:, k, :, :], tmp[:, :, :], bc(z[:, :]), ALU.is_equal).then_inc(s["e_oh"], 1)
                    if k == 0:
                        v.wait_ge(s["e_oh"], 1)
                        chain(v.scalar_tensor_tensor(out=g2[:, :, :], in0=oh[:, 0, :, :], scalar=-2.0, in1=lg[:, :, :],
                                                     op0=ALU.mult, op1=ALU.add))
                        G = g2
                v.wait_ge(s["e_cnt"], 1)
                chain(v.tensor_copy(tot[:, :, :], ps[4][:, 0:2 * NT * E].rearrange("p (t e) -> p t e", e=E)))
                for e in range(E):
                    ins = v.tensor_tensor_scan(run_[:, :, e], ones[:, 0:2 * NT], tot[:, :, e], 0.0, ALU.mult, ALU.add)
                chain(ins)
                chain(v.tensor_tensor(run_[:, :, :], run_[:, :, :], tot[:, :, :], ALU.subtract))
                chain(v.tensor_tensor(run_[:, :, :], run_[:, :, :],
                                      ps[3][:, 0:2 * NT * E].rearrange("p (t e) -> p t e", e=E), ALU.add))
                o = oh[:, :, :, :].rearrange("p k t e -> p (k t) e")
                chain(v.scalar_tensor_tensor(out=run_[:, :, :], in0=run_[:, :, :], scalar=float(C), in1=o,
                                             op0=ALU.is_lt, op1=ALU.mult))
                for k in range(2):
                    ins = v.tensor_tensor(tot[:, k * NT:(k + 1) * NT, :], run_[:, k * NT:(k + 1) * NT, :],
                                          bc(m[:, k, :]), ALU.mult)
                chain(ins)
                v.tensor_tensor(cw[:, :, :].rearrange("p e t -> p t e"), tot[:, 0:NT, :], tot[:, NT:2 * NT, :], ALU.add)
        nc.all_engine_barrier(sems_to_clear=s["numbers"])

        cwe = sb("combine_w_expert", [P, NT])
        with nc.Fori(0, E) as e:
            with nc.Block() as block:
                @block.sync
                def _(sp):
                    for dst, src in ((w1[:, :, :], "moe_w1"), (w2[:, :, :], "moe_w2")):
                        sp.dma_start(dst, d[src][bass.ds(e, 1), :, :, :].rearrange("o p a b -> p (o a) b")).then_inc(s["e_ld"], 16)
                    sp.dma_start(b1[:, :], d["moe_b1"][bass.ds(e, 1), :, :].rearrange("o p a -> p (o a)")).then_inc(s["e_ld"], 16)
                    sp.dma_start(b2[:, :], d["moe_b2"][bass.ds(e, 1), :]).then_inc(s["e_ld"], 16)

                @block.tensor
                def _(t):
                    t.wait_ge(s["e_ld"], 64)

                    def up(b):
                        for n in range(NH):
                            i = NH * b + n
                            if i >= 4:
                                t.wait_ge(s["e_he"], i - 3)
                            t.matmul(ps[i % 4][:, :], w1[:, n, :],
                                     XT[:, TB * b:TB * b + TB, :].rearrange("p c n -> p (c n)"),
                                     start=True, stop=True).then_inc(s["e_h"], 1)

                    def down(b):
                        if b >= 2:
                            t.wait_ge(s["e_acc"], TB * (b - 1))
                        for c in range(TB):
                            y = ps[4 + b % 2][:, c * P:(c + 1) * P]
                            for n in range(NH):
                                t.wait_ge(s["e_he"], NH * b + n + 1)
                                t.matmul(y, hT[:, b % 2, n, c * P:(c + 1) * P], w2[:, n, :], start=(n == 0), stop=False)
                            t.matmul(y, env.one_row[0:1, :], b2[0:1, :], start=False, stop=True).then_inc(s["e_y"], 1)

                    up(0)
                    for b in range(B):
                        if b + 1 < B:
                            up(b + 1)
                        down(b)

                @block.scalar
                def _(a):
                    a.wait_ge(s["e_ld"], 64)
                    for i in range(NH * B):
                        b, n = divmod(i, NH)
                        a.wait_ge(s["e_h"], i + 1)
                        if b >= 2:
                            a.wait_ge(s["e_y"], TB * (b - 1))
                        a.activation(hT[:, b % 2, n, :], ps[i % 4][:, :], ACT.Gelu, bias=b1[:, n:n + 1]).then_inc(s["e_he"], 1)

                @block.vector
                def _(v):
                    v.tensor_copy(cwe[:, :], cw[:, bass.ds(e, 1), :].rearrange("p o t -> p (o t)")).then_inc(s["e_w"], 1)
                    v.wait_ge(s["e_w"], 1)
                    for c in range(NT):
                        v.wait_ge(s["e_y"], TB * (c // TB + 1))
                        v.scalar_tensor_tensor(out=acc[:, c, :],
                                               in0=ps[4 + (c // TB) % 2][:, (c % TB) * P:(c % TB + 1) * P],
                                               scalar=cwe[:, c:c + 1], in1=acc[:, c, :],
                                               op0=ALU.mult, op1=ALU.add).then_inc(s["e_acc"], 1)
            nc.all_engine_barrier(sems_to_clear=s["numbers"])
        with nc.Block() as block:
            finish_layer_norm(block, X, acc, XT, st, mv, sd, rs, NT, env, s["e_chain"], s["e_var"], s["e_sd"], s["e_done"])
        nc.all_engine_barrier(sems_to_clear=s["numbers"])


def load_late(nc, env, ctx):
    d = env.d
    env.w = {}
    with ExitStack() as inner:
        s = semaphores(nc, inner, "late_loaded")
        with nc.Block() as block:
            @block.sync
            def _(sp):
                names = ("la_w", "la_e", "la_wo", "la_mask", "gm_w", "gm_cols", "gm_row",
                         "sm_gate", "sm_w1", "sm_w2", "sa_w", "sa_wo", "sa_desc", "sl_w", "sl_cols")
                for name in names:
                    shape = list(d[name].shape)
                    env.w[name] = ctx.enter_context(nc.sbuf_tensor(name, shape, F32))
                    at = tuple(slice(None) for _ in shape)
                    sp.dma_start(env.w[name][at], d[name]).then_inc(s["late_loaded"], 16)
                sp.wait_ge(s["late_loaded"], 16 * len(names))
        nc.all_engine_barrier(sems_to_clear=s["numbers"])
    env.sa_counting = ctx.enter_context(nc.sbuf_tensor("sa_counting16", [P, 5, P], BF16))
    env.la_sel16 = ctx.enter_context(nc.sbuf_tensor("la_sel16", [6 * H, 2, P], BF16))
    with ExitStack() as inner:
        sel = inner.enter_context(nc.sbuf_tensor("la_sel", [6 * H, 2, P], F32))
        counting = inner.enter_context(nc.sbuf_tensor("sa_counting", [P, 5, P], F32))
        s = semaphores(nc, inner, "counting_loaded")
        with nc.Block() as block:
            @block.sync
            def _(sp):
                sp.dma_start(counting[:, :, :], d["sa_counting"]).then_inc(s["counting_loaded"], 16)
                sp.dma_start(sel[:, :, :], d["la_sel"]).then_inc(s["counting_loaded"], 16)

            @block.vector
            def _(v):
                v.wait_ge(s["counting_loaded"], 32)
                v.tensor_copy(env.la_sel16[:, :, :], sel[:, :, :])
                v.tensor_copy(env.sa_counting[:, :, :], counting[:, :, :])
        nc.all_engine_barrier(sems_to_clear=s["numbers"])


def load_experts(sp, env, b, sem):
    d, group = env.d, b % 2
    for dst, src in ((env.gm1, "gm_w1"), (env.gm2, "gm_w2"), (env.gmb, "gm_b")):
        at = tuple(slice(None) for _ in dst.shape)
        n = d[src][(bass.ds(group, 1),) + at]
        n = n.rearrange("o p a b c -> p (o a) b c") if len(n.shape) == 5 else n.rearrange("o p a b -> p (o a) b")
        sp.dma_start(dst[at], n).then_inc(sem, 16)


LIGHTNING_CONSTANTS = ("lt_decay", "lt_rope", "lt_wq", "lt_wk", "lt_wv", "lt_wo")


def place_early_weights(nc, env, ctx):
    sb = lambda n, s: ctx.enter_context(nc.sbuf_tensor(n, s, F32))
    env.gm1 = sb("gm_w1", [P, TB, 4, P])
    env.gm2 = sb("gm_w2", [P, TB, 4, P])
    env.gmb = sb("gm_b", [P, TB, 5])
    for name in LIGHTNING_CONSTANTS:
        env.w[name] = ctx.enter_context(nc.sbuf_tensor(name, list(env.d[name].shape), F32))


def local_attention(nc, env, w, b):
    WIN = 32
    RG = P // H
    NG = WIN // RG
    TG = 2
    NT2 = WIN // TG
    TR = 3 * TG * H
    X, XT, ps = w.X, w.XT, w.ps
    W, Ec, Wo, msk = (env.w[n] for n in ("la_w", "la_e", "la_wo", "la_mask"))
    sel, ident16 = env.la_sel16, env.sa_counting[:, 4, :]
    scale = HD ** -0.5
    with ExitStack() as ctx:
        sb = lambda n, s, t=F32: ctx.enter_context(nc.sbuf_tensor("la_" + n, s, t))
        qt = sb("q_t", [P, S])
        kp = sb("k_padded", [P, WIN + S])
        vp = sb("v_padded", [P, WIN + S])
        hm = sb("head_mask_between_zeros", [P, (2 * RG - 1) * H])
        pr = sb("products", [P, 4, S])
        sT = sb("scores_t", [P, 2, S])
        D = sb("weights", [P, TB, WIN, H])
        D3 = sb("weights_parts", [P, TB, NT2, 3, TG * H], BF16)
        mx = sb("max", [P, TB, H])
        zs = sb("sum", [P, TB, H])
        pt = sb("weights_t", [TR, 2, S], BF16)
        yt = sb("y_t", [P, S])
        s = semaphores(nc, ctx, LN_SEMS + "proj q pr sc st ts dd ex pn part left hm pt pte bc pv yt yte y ld")
        psA, psS = ps[4:6], ps[0:4]
        psB, psT, psYT, psY = ps[0:3], ps[4:6], ps[3], ps[6]
        with nc.Block() as block:
            @block.sync
            def _(sp):
                load_experts(sp, env, b, s["ld"])
                for name in LIGHTNING_CONSTANTS:
                    at = tuple(slice(None) for _ in env.w[name].shape)
                    sp.dma_start(env.w[name][at], env.d[name]).then_inc(s["ld"], 16)
                sp.wait_ge(s["ld"], 48 + 16 * len(LIGHTNING_CONSTANTS))

            @block.tensor
            def _(t):
                for m in range(3):
                    t.matmul(ps[m][:, :], W[:, m * P:(m + 1) * P], XT[:, :], start=True, stop=True).then_inc(s["proj"], 1)

                def turn_scores(g):
                    t.wait_ge(s["st"], g + 1)
                    for c in range(TB):
                        ins = t.transpose(psS[c][:, g * P:(g + 1) * P], sT[:, g % 2, c * P:(c + 1) * P], env.ident[:, :])
                    ins.then_inc(s["ts"], 1)

                t.wait_ge(s["q"], 3)
                t.wait_ge(s["hm"], 1)
                for r in range(WIN):
                    g, i = divmod(r, RG)
                    if i == 0 and g >= 2:
                        t.wait_ge(s["st"], g - 1)
                    t.wait_ge(s["pr"], r + 1)
                    t.matmul(psA[g % 2][:, :], hm[:, (RG - 1 - i) * H:(2 * RG - 1 - i) * H], pr[:, r % 4, :],
                             start=(i == 0), stop=(i == RG - 1)).then_inc(s["sc"], 1)
                    if i == 1 and g >= 1:
                        turn_scores(g - 1)
                turn_scores(NG - 1)

                def turn_weights(g):
                    if g >= 2:
                        t.wait_ge(s["pte"], g - 1)
                    for c in range(TB):
                        if g == 0:
                            t.wait_ge(s["part"], 2 * TB + c + 1)
                        ins = t.matmul(psT[g % 2][0:TR, c * P:(c + 1) * P],
                                       D3[:, c, g, :, :].rearrange("p a r -> p (a r)"), ident16, start=True, stop=True)
                    ins.then_inc(s["pt"], 1)

                turn_weights(0)
                for g in range(NT2 + 1):
                    if g < NT2:
                        t.wait_ge(s["pte"], g + 1)
                        for r in (TG * g, TG * g + 1):
                            if r >= 3:
                                t.wait_ge(s["pv"], r - 2)
                            t.matmul(psB[r % 3][:, :], sel[0:TR, r % TG, :], pt[0:TR, g % 2, :], start=True, stop=True)\
                                .then_inc(s["bc"], 1)
                    if g + 1 < NT2:
                        turn_weights(g + 1)
                    if g >= 1:
                        t.wait_ge(s["left"], 2 * TB + g)
                        t.matmul(psYT[:, :], Wo[:, :], pr[:, TG * (g - 1) % 4, :], start=(g == 1), stop=(g == NT2))\
                            .then_inc(s["yt"], 1)
                t.wait_ge(s["yte"], 1)
                for c in range(TB):
                    ins = t.transpose(psY[:, c * P:(c + 1) * P], yt[:, c * P:(c + 1) * P], env.ident[:, :])
                ins.then_inc(s["y"], 1)
                turn_tokens(t, s, X, ps[0:2], env.ident)

            @block.scalar
            def _(a):
                for m, dst in enumerate((qt[:, :], kp[:, WIN:], vp[:, WIN:])):
                    a.wait_ge(s["proj"], m + 1)
                    a.activation(dst, ps[m][:, :], ACT.Copy).then_inc(s["q"], 1)
                for g in range(NG):
                    a.wait_ge(s["sc"], RG * (g + 1))
                    if g >= 2:
                        a.wait_ge(s["ts"], g - 1)
                    a.activation(sT[:, g % 2, :], psA[g % 2][:, :], ACT.Copy).then_inc(s["st"], 1)
                for c in range(TB):
                    a.wait_ge(s["dd"], c + 1)
                    a.activation(D[:, c, :, :], D[:, c, :, :], ACT.Exp, scale=scale).then_inc(s["ex"], 1)
                for i in range(3):
                    for c in range(TB):
                        a.wait_ge(s["pn"], c + 1)
                        if i:
                            a.wait_ge(s["left"], (i - 1) * TB + c + 1)
                        a.activation(D3[:, c, :, i, :], D[:, c, :, :].rearrange("p (g r) h -> p g (r h)", r=TG),
                                     ACT.Copy).then_inc(s["part"], 1)
                for g in range(NT2):
                    a.wait_ge(s["pt"], g + 1)
                    if g >= 2:
                        a.wait_ge(s["bc"], TG * (g - 1))
                    a.activation(pt[0:TR, g % 2, :], psT[g % 2][0:TR, :], ACT.Copy).then_inc(s["pte"], 1)
                a.wait_ge(s["yt"], NT2)
                a.activation(yt[:, :], psYT[:, :], ACT.Copy).then_inc(s["yte"], 1)
                std_and_turn(a, s, w, XT, ps[0:2], env.eps, ACT.Gelu)

            @block.gpsimd
            def _(g):
                g.memset(kp[:, 0:WIN], 0.0)
                g.memset(vp[:, 0:WIN], 0.0)
                g.memset(hm[:, 0:(RG - 1) * H], 0.0)
                g.memset(hm[:, RG * H:], 0.0)
                g.tensor_copy(hm[:, (RG - 1) * H:RG * H], env.head_mask[:, :]).then_inc(s["hm"], 1)

            @block.vector
            def _(v):
                chain = Chain(v, s["chain"])
                v.wait_ge(s["q"], 2)
                v.wait_ge(s["hm"], 1)
                for r in range(WIN):
                    if r >= 4:
                        v.wait_ge(s["sc"], r - 3)
                    v.scalar_tensor_tensor(out=pr[:, r % 4, :], in0=kp[:, r + 1:r + 1 + S], scalar=Ec[:, r:r + 1],
                                           in1=qt[:, :], op0=ALU.add, op1=ALU.mult).then_inc(s["pr"], 1)
                v.wait_ge(s["ts"], NG)
                for c in range(TB):
                    src = psS[c][:, :].rearrange("p (r h) -> p r h", h=H)
                    if c == 0:
                        chain(v.tensor_tensor(D[:, 0, :, :], src, msk[:, :, None].broadcast_to([P, WIN, H]), ALU.add))
                        src = D[:, 0, :, :]
                    chain(v.tensor_reduce(mx[:, c, :], src.rearrange("p r h -> p h r"), AX.X, ALU.max))
                    v.tensor_tensor(D[:, c, :, :], src, mx[:, c, None, :].broadcast_to([P, WIN, H]), ALU.subtract)\
                        .then_inc(s["dd"], 1)
                for c in range(TB):
                    v.wait_ge(s["ex"], c + 1)
                    chain(v.tensor_reduce(zs[:, c, :], D[:, c, :, :].rearrange("p r h -> p h r"), AX.X, ALU.add))
                    chain(v.reciprocal(zs[:, c, :], zs[:, c, :]))
                    v.tensor_tensor(D[:, c, :, :], D[:, c, :, :], zs[:, c, None, :].broadcast_to([P, WIN, H]),
                                    ALU.mult).then_inc(s["pn"], 1)
                for i in range(2):
                    for c in range(TB):
                        v.wait_ge(s["part"], i * TB + c + 1)
                        x = D[:, c, :, :].rearrange("p (g r) h -> p g (r h)", r=TG)
                        v.tensor_tensor(x, x, D3[:, c, :, i, :], ALU.subtract).then_inc(s["left"], 1)
                v.wait_ge(s["q"], 3)
                for r in range(WIN):
                    v.wait_ge(s["bc"], r + 1)
                    if r >= 4:
                        v.wait_ge(s["yt"], r // TG - 1)
                    v.tensor_tensor(pr[:, r % 4, :], psB[r % 3][:, :], vp[:, r + 1:r + 1 + S], ALU.mult).then_inc(s["pv"], 1)
                    if r % TG:
                        v.wait_ge(s["pv"], r + 1)
                        v.tensor_tensor(pr[:, (r - 1) % 4, :], pr[:, (r - 1) % 4, :], pr[:, r % 4, :], ALU.add)\
                            .then_inc(s["left"], 1)
                v.wait_ge(s["y"], 1)
                normalise(v, chain, s, w, psY, X)
        nc.all_engine_barrier(sems_to_clear=s["numbers"])


def context_mlp(nc, env, w, b):
    X, XT, ps = w.X, w.XT, w.ps
    with ExitStack() as ctx:
        g = ctx.enter_context(nc.sbuf_tensor("cm_gelu", [SK, S], F32))
        s = semaphores(nc, ctx, LN_SEMS + "h g gh y")
        with nc.Block() as block:
            @block.tensor
            def _(t):
                t.matmul(ps[1][0:SK, :], w.ctxT[:, :], XT[:, :], start=True, stop=True).then_inc(s["h"], 1)
                t.wait_ge(s["gh"], 1)
                for c in range(TB):
                    ins = t.matmul(ps[2][:, c * P:(c + 1) * P], g[:, c * P:(c + 1) * P], w.ctx[:, :], start=True, stop=True)
                ins.then_inc(s["y"], 1)
                turn_tokens(t, s, X, ps[0:2], env.ident)

            @block.scalar
            def _(a):
                a.wait_ge(s["h"], 1)
                a.activation(g[:, :], ps[1][0:SK, :], ACT.Gelu).then_inc(s["g"], 1)
                std_and_turn(a, s, w, XT, ps[0:2], env.eps, ACT.Copy)

            @block.vector
            def _(v):
                chain = Chain(v, s["chain"])
                v.wait_ge(s["g"], 1)
                v.tensor_tensor(g[:, :], ps[1][0:SK, :], g[:, :], ALU.mult).then_inc(s["gh"], 1)
                v.wait_ge(s["y"], 1)
                normalise(v, chain, s, w, ps[2], X)
        nc.all_engine_barrier(sems_to_clear=s["numbers"])


def grouped_mlp(nc, env, w, b):
    NH = 4
    X, XT, ps = w.X, w.XT, w.ps
    W, cols, row = env.w["gm_w"], env.w["gm_cols"], env.w["gm_row"]
    with ExitStack() as ctx:
        sb = lambda n, s: ctx.enter_context(nc.sbuf_tensor("gm_" + n, s, F32))
        xn = sb("xn_t", [P, S])
        xa = sb("x_attn_t", [P, S])
        hT = sb("h_t", [P, TB, NH, P])
        eo = sb("eo_t", [P, TB, P])
        y = sb("y", [P, TB, P])
        s = semaphores(nc, ctx, LN_SEMS + "var0 sd0 xh xt xnt at xa h he e ee y ye")
        psE, psN = ps[6], ps[7]
        with nc.Block() as block:
            @block.tensor
            def _(t):
                for c in range(TB):
                    t.wait_ge(s["xh"], c + 1)
                    ins = t.transpose(ps[0][:, c * P:(c + 1) * P], w.R[:, c, :], env.ident[:, :])
                ins.then_inc(s["xt"], 1)
                t.wait_ge(s["xnt"], 1)
                t.matmul(ps[1][:, :], W[:, 0, :], xn[:, :], start=True, stop=True).then_inc(s["at"], 1)
                t.wait_ge(s["xa"], 1)
                for c in range(TB):
                    for n in range(NH):
                        ins = t.matmul(ps[2 + c][:, n * P:(n + 1) * P], env.gm1[:, c, n, :], xa[:, c * P:(c + 1) * P],
                                       start=True, stop=True)
                    ins.then_inc(s["h"], 1)
                for c in range(TB):
                    for n in range(NH):
                        t.wait_ge(s["he"], NH * c + n + 1)
                        ins = t.matmul(psE[:, c * P:(c + 1) * P], env.gm2[:, c, n, :], hT[:, c, n, :],
                                       start=(n == 0), stop=(n == NH - 1))
                ins.then_inc(s["e"], 1)
                for c in range(TB):
                    t.wait_ge(s["ee"], c + 1)
                    t.matmul(psN[:, c * P:(c + 1) * P], eo[:, c, :], W[:, 1, :], start=True, stop=False)
                    ins = t.matmul(psN[:, c * P:(c + 1) * P], env.one_row[0:1, :], row[0:1, :], start=False, stop=True)
                ins.then_inc(s["y"], 1)
                turn_tokens(t, s, X, ps[0:2], env.ident)

            @block.scalar
            def _(a):
                a.wait_ge(s["var0"], 1)
                a.activation(w.sd[:, :], w.mv[:, :, 1], ACT.Sqrt, bias=env.eps[:, 0:1]).then_inc(s["sd0"], 1)
                a.wait_ge(s["xt"], 1)
                a.activation(xn[:, :], ps[0][:, :], ACT.Identity, scale=cols[:, 0:1], bias=cols[:, 1:2]).then_inc(s["xnt"], 1)
                for c in range(TB):
                    a.wait_ge(s["h"], c + 1)
                    for n in range(NH):
                        a.activation(hT[:, c, n, :], ps[2 + c][:, n * P:(n + 1) * P], ACT.Gelu,
                                     bias=env.gmb[:, c, n:n + 1]).then_inc(s["he"], 1)
                a.wait_ge(s["y"], 1)
                a.activation(y[:, :, :], psN[:, :].rearrange("p (c n) -> p c n", c=TB), ACT.Gelu).then_inc(s["ye"], 1)
                std_and_turn(a, s, w, XT, ps[0:2], env.eps, ACT.Silu)

            @block.vector
            def _(v):
                chain = Chain(v, s["chain"])
                layer_norm_stats(v, chain, X, w.st, w.mv, TB, s["var0"])
                v.wait_ge(s["sd0"], 1)
                chain(v.reciprocal(w.rs[:, :], w.sd[:, :]))
                for c in range(TB):
                    v.tensor_scalar(w.R[:, c, :], X[:, c, :], w.mv[:, c, 0:1], w.rs[:, c:c + 1],
                                    ALU.subtract, ALU.mult).then_inc(s["xh"], 1)
                v.wait_ge(s["at"], 1)
                v.scalar_tensor_tensor(out=xa[:, :], in0=ps[1][:, :], scalar=cols[:, 2:3], in1=XT[:, :],
                                       op0=ALU.add, op1=ALU.add).then_inc(s["xa"], 1)
                v.wait_ge(s["e"], 1)
                for c in range(TB):
                    v.tensor_scalar(eo[:, c, :], psE[:, c * P:(c + 1) * P], env.gmb[:, c, NH:NH + 1], None, ALU.add)\
                        .then_inc(s["ee"], 1)
                v.wait_ge(s["ye"], 1)
                normalise(v, chain, s, w, y, X)
        nc.all_engine_barrier(sems_to_clear=s["numbers"])


def lightning(nc, env, w, b):
    HQ, KV, W2 = 16, 4, 64
    NQ, NK = HQ * W2 // P, KV * W2 // P
    X, XT, ps = w.X, w.XT, w.ps
    wq, wk, wv, wo, rope, decay = (env.w["lt_" + n] for n in ("wq", "wk", "wv", "wo", "rope", "decay"))
    with ExitStack() as ctx:
        sb = lambda n, s: ctx.enter_context(nc.sbuf_tensor("lt_" + n, s, F32))
        qk = sb("q_k_t", [P, NQ + NK, S])
        tmp = sb("rope_tmp", [P, 2, 2, S])
        vv = sb("v", [P, TB, KV * W2])
        pd = sb("decayed", [P, 4, S])
        ot = sb("o_t", [P, 2, S])
        s = semaphores(nc, ctx, LN_SEMS + "vp ve pj r1 qk sc pd av oe y")
        NC_ = NQ + NK
        pair = lambda i: (ps[2 * (i % 2)], ps[2 * (i % 2) + 1])
        psO, psY = ps[4:6], ps[7]
        items = [(m, r, j) for m in range(NQ) for r in range(2) for j in range(TB)]
        with nc.Block() as block:
            @block.tensor
            def _(t):
                for c in range(TB):
                    ins = t.matmul(ps[4 + c // 2][:, (c % 2) * 256:(c % 2 + 1) * 256], XT[:, c * P:(c + 1) * P], wv[:, :],
                                   start=True, stop=True)
                ins.then_inc(s["vp"], 1)
                for i in range(NC_):
                    if i >= 2:
                        t.wait_ge(s["r1"], 2 * (i - 1))
                    wt, m = (wk, i) if i < NK else (wq, i - NK)
                    for x in range(2):
                        t.matmul(pair(i)[x][:, :], wt[:, x, m, :], XT[:, :], start=True, stop=True).then_inc(s["pj"], 1)
                t.wait_ge(s["r1"], 2 * NC_)
                t.wait_ge(s["ve"], 2)

                def score(i):
                    m, r, j = items[i]
                    if i >= 4:
                        t.wait_ge(s["pd"], i - 3)
                    t.wait_ge(s["qk"], NK + m + 1)
                    rows = slice(W2 * r, W2 * r + W2)
                    t.matmul(ps[i % 4][:, j * P:S], qk[rows, m // 4, j * P:(j + 1) * P], qk[rows, NK + m, j * P:S],
                             start=True, stop=True).then_inc(s["sc"], 1)

                def weigh(i):
                    m, r, j = items[i]
                    t.wait_ge(s["pd"], i + 1)
                    if m >= 2 and r == 0 and j == 0:
                        t.wait_ge(s["oe"], m - 1)
                    kv = 2 * (m // 4) + r
                    t.matmul(psO[m % 2][W2 * r:W2 * r + W2, j * P:S], vv[:, j, kv * W2:(kv + 1) * W2], pd[:, i % 4, j * P:S],
                             start=(j == 0), stop=(j == TB - 1), skip_group_check=True).then_inc(s["av"], 1)

                def out(m):
                    t.wait_ge(s["oe"], m + 1)
                    for c in range(TB):
                        ins = t.matmul(psY[:, c * P:(c + 1) * P], ot[:, m % 2, c * P:(c + 1) * P], wo[:, m, :],
                                       start=(m == 0 and c == 0), stop=(m == NQ - 1), skip_group_check=True)
                    ins.then_inc(s["y"], 1)

                N = len(items)
                for i in range(N + 2):
                    if i < N:
                        score(i)
                    if i >= 2:
                        weigh(i - 2)
                    if i % 8 == 3 and i >= 11:
                        out((i - 11) // 8)
                out(NQ - 1)
                turn_tokens(t, s, X, ps[0:2], env.ident)

            @block.scalar
            def _(a):
                a.wait_ge(s["vp"], 1)
                for x in range(2):
                    a.activation(vv[:, 2 * x:2 * x + 2, :], ps[4 + x][:, :].rearrange("p (c n) -> p c n", c=2), ACT.Copy)\
                        .then_inc(s["ve"], 1)
                for m in range(NQ):
                    a.wait_ge(s["av"], 8 * (m + 1))
                    if m >= 2:
                        a.wait_ge(s["y"], m - 1)
                    a.activation(ot[:, m % 2, :], psO[m % 2][:, :], ACT.Copy).then_inc(s["oe"], 1)
                std_and_turn(a, s, w, XT, ps[0:2], env.eps, ACT.Exp)

            @block.gpsimd
            def _(g):
                for i in range(NC_):
                    g.wait_ge(s["r1"], 2 * (i + 1))
                    g.tensor_tensor(qk[:, i, :], tmp[:, i % 2, 0, :], tmp[:, i % 2, 1, :], ALU.add).then_inc(s["qk"], 1)

            @block.vector
            def _(v):
                chain = Chain(v, s["chain"])
                for i in range(NC_):
                    if i >= 2:
                        v.wait_ge(s["qk"], i - 1)
                    for x in range(2):
                        v.wait_ge(s["pj"], 2 * i + x + 1)
                        v.tensor_tensor(tmp[:, i % 2, x, :], pair(i)[x][:, :], rope[:, x, :], ALU.mult).then_inc(s["r1"], 1)
                for i, (m, r, j) in enumerate(items):
                    h = 8 * (m // 4) + 4 * r + m % 4
                    v.wait_ge(s["sc"], i + 1)
                    if i >= 4:
                        v.wait_ge(s["av"], i - 3)
                    v.tensor_tensor(pd[:, i % 4, j * P:S], ps[i % 4][:, j * P:S], decay[:, h, 0:S - j * P], ALU.mult)\
                        .then_inc(s["pd"], 1)
                v.wait_ge(s["y"], NQ)
                normalise(v, chain, s, w, psY, X)
        nc.all_engine_barrier(sems_to_clear=s["numbers"])


def shared_moe(nc, env, w, b):
    E, NH = 8, 4
    X, XT, ps = w.X, w.XT, w.ps
    wg, w1, w2 = env.w["sm_gate"], env.w["sm_w1"], env.w["sm_w2"]
    with ExitStack() as ctx:
        sb = lambda n, s: ctx.enter_context(nc.sbuf_tensor("sm_" + n, s, F32))
        lg = sb("gates", [P, TB, E])
        top = sb("top", [P, TB, E])
        z = sb("z", [P, TB])
        dn = sb("denom", [P, TB])
        hT = sb("h_t", [P, NH, S])
        y = sb("y", [P, TB, P])
        s = semaphores(nc, ctx, LN_SEMS + "lg sub ex h he y")
        with nc.Block() as block:
            @block.tensor
            def _(t):
                for c in range(TB):
                    ins = t.matmul(ps[1][:, c * E:(c + 1) * E], XT[:, c * P:(c + 1) * P], wg[:, :], start=True, stop=True)
                ins.then_inc(s["lg"], 1)
                for n in range(NH):
                    t.matmul(ps[2 + n][:, :], w1[:, n, :], XT[:, :], start=True, stop=True).then_inc(s["h"], 1)
                for c in range(TB):
                    for n in range(NH):
                        t.wait_ge(s["he"], n + 1)
                        ins = t.matmul(ps[6][:, c * P:(c + 1) * P], hT[:, n, c * P:(c + 1) * P], w2[:, n, :],
                                       start=(n == 0), stop=(n == NH - 1))
                ins.then_inc(s["y"], 1)
                turn_tokens(t, s, X, ps[0:2], env.ident)

            @block.scalar
            def _(a):
                a.wait_ge(s["sub"], 1)
                a.activation(lg[:, :, :], lg[:, :, :], ACT.Exp).then_inc(s["ex"], 1)
                for n in range(NH):
                    a.wait_ge(s["h"], n + 1)
                    a.activation(hT[:, n, :], ps[2 + n][:, :], ACT.Relu).then_inc(s["he"], 1)
                std_and_turn(a, s, w, XT, ps[0:2], env.eps, ACT.Exp)

            @block.vector
            def _(v):
                chain = Chain(v, s["chain"])
                bc = lambda a: a[:, :, None].broadcast_to([P, TB, E])
                v.wait_ge(s["lg"], 1)
                L = ps[1][:, 0:TB * E].rearrange("p (t e) -> p t e", e=E)
                chain(v.tensor_reduce(z[:, :], L, AX.X, ALU.max))
                v.tensor_tensor(lg[:, :, :], L, bc(z[:, :]), ALU.subtract).then_inc(s["sub"], 1)
                v.wait_ge(s["ex"], 1)
                chain(v.tensor_reduce(z[:, :], lg[:, :, :], AX.X, ALU.add))
                chain(v.reciprocal(z[:, :], z[:, :]))
                chain(v.tensor_tensor(lg[:, :, :], lg[:, :, :], bc(z[:, :]), ALU.mult))
                for c in range(TB):
                    ins = v.max(top[:, c, :], lg[:, c, :])
                chain(ins)
                chain(v.tensor_tensor(dn[:, :], top[:, :, 0], top[:, :, 1], ALU.add))
                chain(v.tensor_scalar(dn[:, :], dn[:, :], 1.1920929e-07, None, ALU.max))
                chain(v.reciprocal(dn[:, :], dn[:, :]))
                chain(v.tensor_tensor(top[:, :, 0:2], top[:, :, 0:2], dn[:, :, None].broadcast_to([P, TB, 2]), ALU.mult))
                chain(v.tensor_tensor(z[:, :], top[:, :, 0], top[:, :, 1], ALU.add))
                v.wait_ge(s["y"], 1)
                for c in range(TB):
                    ins = v.tensor_scalar(y[:, c, :], ps[6][:, c * P:(c + 1) * P], z[:, c:c + 1], None, ALU.mult)
                chain(ins)
                normalise(v, chain, s, w, y, X)
        nc.all_engine_barrier(sems_to_clear=s["numbers"])


def sparse_attention(nc, env, w, b):
    KEEP = 64
    NONE, MASKED = -1e30, -1e32
    G3 = 3 * H
    GH = 4
    GR = GH * (HD + 1)
    NR = 3 * HD
    X, XT, ps = w.X, w.XT, w.ps
    W, Wo, desc = (env.w["sa_" + n] for n in ("w", "wo", "desc"))
    own_ge, own_gt, all_before, mask, ident16 = (env.sa_counting[:, i, :] for i in range(5))
    scr = env.scratch
    scale = HD ** -0.5
    SLOTS = [[(0, 0, 0)], [(0, 1, 0), (0, 3, 3 * P)], [(0, 2, 0), (1, 2, 2 * P)], [(1, 0, 0)], [(1, 1, 0), (1, 3, 3 * P)]]
    NS, PAIRS = len(SLOTS), H // 2
    N = NS * PAIRS
    place = {(hh, jt): (sl, col) for sl, parts in enumerate(SLOTS) for hh, jt, col in parts}
    width = lambda jt: (TB - jt) * P
    with ExitStack() as ctx:
        sb = lambda n, s, t=F32: ctx.enter_context(nc.sbuf_tensor("sa_" + n, s, t))
        kst = sb("k_stack", [4 * NR, H, S], BF16)
        qst = sb("q_stack", [4 * NR, H, S], BF16)
        ex = sb("exp", [P, PAIRS, NS, S])
        qt = sb("q_t", [P, S])
        qs = sb("q_sign", [P, S], BF16)
        rp = sb("threshold_parts", [P, 3, S], BF16)
        v1 = sb("v_and_one", [P, TB, H, HD + 1])
        zr = sb("one_over_sum", [P, TB, H])
        with ExitStack() as early:
            sb = lambda n, s, t=F32: early.enter_context(nc.sbuf_tensor("sa_" + n, s, t))
            qkv = sb("qkv", [P, TB, 3 * P])
            ab = sb("abs", [P, 2, 3 * P])
            m = sb("feature_max", [P, 2, G3])
            L = sb("level", [P, 2, 2, S])
            y = sb("passed_on", [P, 2, S])
            M = sb("running_max", [P, 2, S])
            kt = sb("k_t", [P, S])
            tmp = sb("tmp", [P, 2, S])
            thr = sb("minus_threshold", [P, 2, S])
            kp = sb("k_parts", [P, 3, S], BF16)
            qp = sb("q_parts", [P, 3, S], BF16)
        sb = lambda n, s, t=F32: ctx.enter_context(nc.sbuf_tensor("sa_" + n, s, t))
        gg = sb("ge_gt", [P, 2, 2, NS, S], BF16)
        vz = sb("v_and_one_padded", [P, TB, H, GR])
        wt = sb("weighed", [GR, H // GH, S])
        o = sb("o", [P, TB, P])
        ot = sb("o_t", [P, S])
        s = semaphores(nc, ctx, LN_SEMS + "pj pje keep tk tke y0 mx ones split kp qp mxp rp qs stored k_in q_in s_done exp "
                                          "d cmp cnt sel vz pv wt tt on ott ote y pc")
        psS, psD, psC, psO, psY = ps[0:2], ps[2:4], ps[4:6], ps[2], ps[3]
        psW, psB = (ps[0], ps[1], ps[6], ps[7]), ps[0:2]
        with nc.Block() as block:
            @block.sync
            def _(sp):
                rows = lambda a: scr[a].rearrange("p (f h) n -> (p f) h n", h=H)
                part = lambda a, p: scr[a, p].rearrange("(f h) n -> f h n", h=H)

                def store(a, src, ready, n):
                    sp.wait_ge(s[ready], 1)
                    sp.dma_start(scr[a].rearrange("p r n -> r p n"), src[:, :, :]).then_inc(s["stored"], 16)
                    sp.wait_ge(s["stored"], 16 * n)

                store(0, kp, "kp", 1)
                for i in range(3):
                    sp.dma_start(kst[NR + i * NR:NR + (i + 1) * NR, :, :], rows(0)).then_inc(s["k_in"], 16)
                store(1, qp, "qp", 2)
                for i in range(3):
                    for j in range(3):
                        at = NR + i * NR + j * HD
                        sp.dma_start(qst[at:at + HD, :, :], part(1, i)).then_inc(s["q_in"], 16)
                store(2, kp, "mxp", 3)
                sp.dma_start(qst[0:NR, :, :], rows(2)).then_inc(s["q_in"], 16)
                sp.wait_ge(s["qs"], 1)
                sp.dma_start(scr[4, 0], qs[:, :]).then_inc(s["stored"], 16)
                sp.wait_ge(s["stored"], 64)
                sp.wait_ge(s["s_done"], N)
                for j in range(3):
                    at = NR + j * HD
                    sp.dma_start(qst[at:at + HD, :, :], part(4, 0)).then_inc(s["q_in"], 16)
                store(3, rp, "rp", 5)
                sp.dma_start(qst[0:NR, :, :], rows(3)).then_inc(s["q_in"], 16)

            @block.tensor
            def _(t):
                for c in range(TB):
                    t.matmul(ps[c][:, 0:3 * P], XT[:, c * P:(c + 1) * P], W[:, :], start=True, stop=True).then_inc(s["pj"], 1)
                for c in range(TB):
                    t.wait_ge(s["keep"], c + 1)
                    for x in range(2):
                        ins = t.transpose(ps[4 + x][:, c * P:(c + 1) * P], qkv[:, c, x * P:(x + 1) * P], env.ident[:, :])
                ins.then_inc(s["tk"], 1)

                def scores(bank, sl, pair, rows):
                    for i, (hh, jt, col) in enumerate(SLOTS[sl]):
                        h = 2 * pair + hh
                        t.matmul(bank[:, col:col + P], ident16, mask, start=(i == 0), stop=False, skip_group_check=True)
                        ins = t.matmul(bank[:, col:col + width(jt)], kst[0:rows, h, jt * P:(jt + 1) * P],
                                       qst[0:rows, h, jt * P:S], start=False, stop=True, skip_group_check=True)
                    return ins

                t.wait_ge(s["pje"], TB)
                t.wait_ge(s["ones"], 1)
                t.wait_ge(s["k_in"], 48)
                t.wait_ge(s["q_in"], 160)
                for k in range(N):
                    if k >= 2:
                        t.wait_ge(s["exp"], k - 1)
                    scores(psS[k % 2], k % NS, k // NS, 4 * NR).then_inc(s["s_done"], 1)

                def compare(k):
                    if k >= 2:
                        t.wait_ge(s["cmp"], k - 1)
                    scores(psD[k % 2], k % NS, k // NS, 2 * NR).then_inc(s["d"], 1)

                def count(k):
                    pair, sl = divmod(k, NS)
                    g = gg[:, pair % 2]
                    if k % NS == 0:
                        t.wait_ge(s["cmp"], k + NS)
                    if k >= 2:
                        t.wait_ge(s["sel"], k - 1)
                    bank = psC[k % 2]
                    for i, (hh, jt, col) in enumerate(SLOTS[sl]):
                        out = bank[:, col:col + width(jt)]
                        own = slice(col, col + width(jt))
                        t.matmul(out, own_ge, g[:, 0, sl, own], start=(i == 0), stop=False, skip_group_check=True)
                        for j2 in range(TB):
                            s2, c2 = place[hh, j2]
                            if j2 < jt:
                                c2 += (jt - j2) * P
                                t.matmul(out, all_before, g[:, 0, s2, c2:c2 + width(jt)], start=False, stop=False,
                                         skip_group_check=True)
                            if j2 > jt:
                                c1 = col + (j2 - jt) * P
                                t.matmul(bank[:, c1:c1 + width(j2)], all_before, g[:, 1, s2, c2:c2 + width(j2)],
                                         start=False, stop=False, skip_group_check=True)
                        ins = t.matmul(out, own_gt, g[:, 1, sl, own], start=False, stop=True, skip_group_check=True)
                    ins.then_inc(s["cnt"], 1)

                def weigh(pair):
                    t.wait_ge(s["vz"], 1)
                    t.wait_ge(s["sel"], NS * (pair + 1))
                    for hh in range(2):
                        h = 2 * pair + hh
                        for jt in range(TB):
                            sl, col = place[hh, jt]
                            ins = t.matmul(psW[h // GH][0:GR, jt * P:S], vz[:, jt, h, :],
                                           ex[:, pair, sl, col:col + width(jt)], start=(h % GH == 0 and jt == 0),
                                           stop=(h % GH == GH - 1 and jt == TB - 1), skip_group_check=True)
                    ins.then_inc(s["pv"], 1)

                def turn_back(g):
                    t.wait_ge(s["wt"], max(g + 1, 2))
                    for c in range(TB):
                        at = (c % 2) * H * (HD + 1) + g * GR
                        ins = t.transpose(psB[c // 2][:, at:at + GR], wt[:, g, c * P:(c + 1) * P],
                                          env.ident[0:GR, 0:GR])
                    ins.then_inc(s["tt"], 1)

                t.wait_ge(s["q_in"], 160 + 64)
                for k in range(N + NS):
                    if k < N:
                        compare(k)
                    if k >= NS:
                        count(k - NS)
                    if k % NS == NS - 1 and k // NS >= 2:
                        weigh(k // NS - 2)
                for g in range(2):
                    turn_back(g)
                weigh(PAIRS - 1)
                for g in range(2, 4):
                    turn_back(g)
                for c in range(TB):
                    t.wait_ge(s["on"], c + 1)
                    t.transpose(psO[:, c * P:(c + 1) * P], o[:, c, :], env.ident[:, :]).then_inc(s["ott"], 1)
                t.wait_ge(s["ote"], 1)
                for c in range(TB):
                    ins = t.matmul(psY[:, c * P:(c + 1) * P], ot[:, c * P:(c + 1) * P], Wo[:, :], start=True, stop=True)
                ins.then_inc(s["y"], 1)
                turn_tokens(t, s, X, ps[0:2], env.ident)

            @block.scalar
            def _(a):
                for c in range(TB):
                    a.wait_ge(s["pj"], c + 1)
                    a.activation(qkv[:, c, :], ps[c][:, 0:3 * P], ACT.Copy).then_inc(s["pje"], 1)
                a.wait_ge(s["tk"], 1)
                for sg in range(2):
                    a.activation(y[:, sg, :], ps[5][:, :], ACT.Copy, scale=1.0 - 2 * sg).then_inc(s["y0"], 1)
                a.activation(kt[:, :], ps[5][:, :], ACT.Copy).then_inc(s["tke"], 1)
                a.activation(qt[:, :], ps[4][:, :], ACT.Copy).then_inc(s["tke"], 1)
                for k in range(N):
                    a.wait_ge(s["s_done"], k + 1)
                    a.activation(ex[:, k // NS, k % NS, :], psS[k % 2][:, :], ACT.Exp, scale=scale).then_inc(s["exp"], 1)
                for g in range(H // GH):
                    a.wait_ge(s["pv"], GH // 2 * (g + 1))
                    a.activation(wt[:, g, :], psW[g][0:GR, :], ACT.Copy).then_inc(s["wt"], 1)
                a.wait_ge(s["ott"], TB)
                a.activation(ot[:, :], psO[:, :], ACT.Copy).then_inc(s["ote"], 1)
                std_and_turn(a, s, w, XT, ps[0:2], env.eps, ACT.Exp)

            @block.gpsimd
            def _(g):
                pool = Chain(g, s["pc"])
                g.memset(kst[0:NR, :, :], 1.0).then_inc(s["ones"], 1)
                g.wait_ge(s["tke"], 2)

                def split(x, parts, done):
                    for i in range(3):
                        ins = g.tensor_copy(parts[:, i, :], x)
                        if i < 2:
                            pool(ins)
                            pool(g.tensor_tensor(x, x, parts[:, i, :], ALU.subtract))
                    ins.then_inc(s[done], 1)

                split(kt[:, :], kp, "kp")
                pool(g.tensor_copy(tmp[:, 0, :], qt[:, :]))
                split(tmp[:, 0, :], qp, "qp")
                g.wait_ge(s["qp"], 1)
                g.wait_ge(s["mx"], 2)
                pool(g.tensor_scalar(tmp[:, 0, :], qt[:, :], 0.0, None, ALU.max))
                pool(g.tensor_tensor(tmp[:, 0, :], tmp[:, 0, :], M[:, 0, :], ALU.mult))
                pool(g.tensor_scalar(tmp[:, 1, :], qt[:, :], 0.0, None, ALU.min))
                pool(g.tensor_tensor(tmp[:, 1, :], tmp[:, 1, :], M[:, 1, :], ALU.mult))
                pool(g.tensor_tensor(tmp[:, 1, :], tmp[:, 1, :], tmp[:, 0, :], ALU.subtract))
                g.wait_ge(s["stored"], 16)
                split(tmp[:, 1, :], kp, "mxp")
                g.wait_ge(s["stored"], 48)
                g.wait_ge(s["rp"], 1)
                pool(g.memset(vz[:, :, :, :], 0.0))
                for h in range(H):
                    at = (h % GH) * (HD + 1)
                    ins = g.tensor_copy(vz[:, :, h, at:at + HD + 1], v1[:, :, h, :])
                ins.then_inc(s["vz"], 1)

            @block.vector
            def _(v):
                chain = Chain(v, s["chain"])
                chain(v.memset(v1[:, :, :, :], 1.0))
                for c in range(TB):
                    v.wait_ge(s["pje"], c + 1)
                    grouped = lambda x: x.rearrange("p (g f h) -> p g h f", f=HD, h=H)
                    x = grouped(qkv[:, c, :])
                    z = grouped(ab[:, c % 2, :])
                    best = m[:, c % 2, :].rearrange("p (g h) -> p g h", h=H)
                    bc = m[:, c % 2, :].rearrange("p (g h) -> p g h", h=H)[:, :, :, None].broadcast_to([P, 3, H, HD])
                    chain(v.scalar_tensor_tensor(out=ab[:, c % 2, :], in0=qkv[:, c, :], scalar=-1.0, in1=qkv[:, c, :],
                                                 op0=ALU.mult, op1=ALU.max))
                    chain(v.tensor_reduce(best, z, AX.X, ALU.max))
                    chain(v.tensor_tensor(z, z, bc, ALU.is_equal))
                    chain(v.tensor_tensor(z, z, desc[:, None, None, :].broadcast_to([P, 3, H, HD]), ALU.mult))
                    chain(v.tensor_reduce(best, z, AX.X, ALU.max))
                    chain(v.tensor_tensor(z, z, bc, ALU.is_equal))
                    v.tensor_tensor(qkv[:, c, 0:2 * P], qkv[:, c, 0:2 * P], ab[:, c % 2, 0:2 * P], ALU.mult)\
                        .then_inc(s["keep"], 1)
                    chain(v.tensor_tensor(v1[:, c, :, 0:HD], x[:, 2], z[:, 2], ALU.mult))

                kept, passed = [0, 0], [None, None]
                for level in range(KEEP):
                    for sg in range(2):
                        if level == 0:
                            v.wait_ge(s["y0"], sg + 1)
                        else:
                            chain.wait_for(passed[sg])
                        dst = M[:, sg, :] if level == 0 else L[:, sg, level % 2, level:S]
                        ins = v.tensor_tensor_scan(dst, y[:, sg, level:S], y[:, sg, level:S], NONE, ALU.max, ALU.max)
                        kept[sg] = chain.mark(ins)
                    for sg in range(2):
                        chain.wait_for(kept[sg])
                        if level == 0:
                            v.sem_inc(s["mx"], 1)
                        if level < KEEP - 1:
                            src = M[:, sg, 0:S - 1] if level == 0 else L[:, sg, level % 2, level:S - 1]
                            passed[sg] = chain.mark(v.tensor_tensor(y[:, sg, level + 1:S], src, y[:, sg, level + 1:S],
                                                                    ALU.min))
                    if level == 1:
                        v.wait_ge(s["tke"], 2)
                        chain(v.tensor_scalar(thr[:, 0, :], qt[:, :], 0.0, None, ALU.is_lt))
                        chain(v.scalar_tensor_tensor(out=qs[:, :], in0=qt[:, :], scalar=0.0, in1=thr[:, 0, :],
                                                     op0=ALU.is_gt, op1=ALU.subtract))
                        v.sem_inc(s["qs"], 1)
                last = (KEEP - 1) % 2
                chain(v.memset(L[:, :, last, 0:KEEP - 1], NONE))
                chain(v.scalar_tensor_tensor(out=thr[:, 0, :], in0=qt[:, :], scalar=0.0, in1=L[:, 0, last, :],
                                             op0=ALU.is_gt, op1=ALU.mult))
                chain(v.scalar_tensor_tensor(out=thr[:, 1, :], in0=qt[:, :], scalar=0.0, in1=L[:, 1, last, :],
                                             op0=ALU.is_lt, op1=ALU.mult))
                x = thr[:, 1, :]
                chain(v.scalar_tensor_tensor(out=x, in0=thr[:, 0, :], scalar=-1.0, in1=x, op0=ALU.mult, op1=ALU.subtract))
                for i in range(3):
                    chain(v.tensor_copy(rp[:, i, :], x))
                    if i < 2:
                        chain(v.tensor_tensor(x, x, rp[:, i, :], ALU.subtract))
                v.sem_inc(s["rp"], 1)

                def against(k):
                    pair, sl = divmod(k, NS)
                    v.wait_ge(s["d"], k + 1)
                    if pair >= 2 and sl == 0:
                        v.wait_ge(s["cnt"], NS * (pair - 1))
                    v.tensor_scalar(gg[:, pair % 2, 0, sl, :], psD[k % 2][:, :], 0.0, None, ALU.is_ge)
                    v.tensor_scalar(gg[:, pair % 2, 1, sl, :], psD[k % 2][:, :], 0.0, None, ALU.is_gt).then_inc(s["cmp"], 1)

                def select(k):
                    v.wait_ge(s["cnt"], k + 1)
                    at = ex[:, k // NS, k % NS, :]
                    v.scalar_tensor_tensor(out=at, in0=psC[k % 2][:, :], scalar=KEEP - 0.5 - 1024.0, in1=at,
                                           op0=ALU.is_le, op1=ALU.mult).then_inc(s["sel"], 1)

                v.wait_ge(s["exp"], N)
                for k in range(N + NS):
                    if k < N:
                        against(k)
                    if k >= NS:
                        select(k - NS)
                v.wait_ge(s["tt"], H // GH)
                for c in range(TB):
                    n = H * (HD + 1)
                    got = psB[c // 2][:, (c % 2) * n:(c % 2 + 1) * n].rearrange("p (h n) -> p h n", h=H)
                    chain(v.reciprocal(zr[:, c, :], got[:, :, HD]))
                    v.tensor_tensor(o[:, c, :].rearrange("p (h n) -> p h n", n=HD), got[:, :, 0:HD],
                                    zr[:, c, :, None].broadcast_to([P, H, HD]), ALU.mult).then_inc(s["on"], 1)
                v.wait_ge(s["y"], 1)
                normalise(v, chain, s, w, psY, X)
        nc.all_engine_barrier(sems_to_clear=s["numbers"])


def sign_linear(nc, env, w, b):
    LIMIT = 100.0
    X, XT, ps = w.X, w.XT, w.ps
    W, cols = env.w["sl_w"], env.w["sl_cols"]
    with ExitStack() as ctx:
        sb = lambda n, s: ctx.enter_context(nc.sbuf_tensor("sl_" + n, s, F32))
        sg = sb("signs", [P, P])
        yt = sb("y_t", [P, S])
        s = semaphores(nc, ctx, LN_SEMS + "sg yt cl y")
        with nc.Block() as block:
            @block.tensor
            def _(t):
                t.wait_ge(s["sg"], 1)
                t.matmul(ps[1][:, :], sg[:, :], XT[:, :], start=True, stop=True).then_inc(s["yt"], 1)
                t.wait_ge(s["cl"], 1)
                for c in range(TB):
                    ins = t.transpose(ps[2][:, c * P:(c + 1) * P], yt[:, c * P:(c + 1) * P], env.ident[:, :])
                ins.then_inc(s["y"], 1)
                turn_tokens(t, s, X, ps[0:2], env.ident)

            @block.scalar
            def _(a):
                std_and_turn(a, s, w, XT, ps[0:2], env.eps, ACT.Copy)

            @block.vector
            def _(v):
                chain = Chain(v, s["chain"])
                chain(v.tensor_scalar(sg[:, :], W[:, :], 0.0, 2.0, ALU.is_ge, ALU.mult))
                v.tensor_scalar(sg[:, :], sg[:, :], -1.0, None, ALU.add).then_inc(s["sg"], 1)
                v.wait_ge(s["yt"], 1)
                chain(v.tensor_scalar(yt[:, :], ps[1][:, :], cols[:, 0:1], cols[:, 1:2], ALU.mult, ALU.add))
                v.tensor_scalar(yt[:, :], yt[:, :], -LIMIT, LIMIT, ALU.max, ALU.min).then_inc(s["cl"], 1)
                v.wait_ge(s["y"], 1)
                normalise(v, chain, s, w, ps[2], X)
        nc.all_engine_barrier(sems_to_clear=s["numbers"])


def late_layouts(np, i):
    f32 = np.float32
    o = {}
    WIN = 32
    o["la_w"] = i["L1_attn_w_qkv"].T
    o["la_e"] = np.tile(i["L1_attn_rel_emb"][64 - WIN + 1:65].T, (H, 1))
    o["la_wo"] = i["L1_attn_w_out"].T
    sel = np.zeros((3, 2, H, 2, H, HD), f32)
    for r in range(2):
        for h in range(H):
            sel[:, r, h, r, h, :] = 1.0
    o["la_sel"] = sel.reshape(6 * H, 2, P)
    t, r = np.arange(P)[:, None], np.arange(WIN)[None]
    o["la_mask"] = np.where(t + r < WIN - 1, -1e30, 0.0).astype(f32)
    o["gm_w"] = np.stack([i["L1_ffn_attn_w"].T, i["L1_ffn_next_w"].T], 1)
    o["gm_cols"] = np.stack([i["L1_ffn_ln_scale"], i["L1_ffn_ln_bias"], i["L1_ffn_attn_b"]], 1)
    o["gm_row"] = i["L1_ffn_next_b"][None]
    two = lambda a: a.reshape((2, 4) + a.shape[1:])
    o["gm_w1"] = two(i["L1_ffn_w1"].reshape(8, P, 4, P)).transpose(0, 2, 1, 3, 4)
    o["gm_w2"] = two(i["L1_ffn_w2"].reshape(8, 4, P, P)).transpose(0, 3, 1, 2, 4)
    gb = np.concatenate([i["L1_ffn_b1"].reshape(8, 4, P), i["L1_ffn_b2"][:, None]], 1)
    o["gm_b"] = two(gb).transpose(0, 3, 1, 2)
    order = [8 * (m // 4) + 4 * r + m % 4 for m in range(8) for r in range(2)]
    swap = (np.arange(64) + 32) % 64
    wq = i["L2_attn_Wq"].reshape(16, 64, P)[order]
    wk = i["L2_attn_Wk"].reshape(4, 64, P)
    chunks = lambda a: np.stack([a.reshape(-1, P, P).transpose(2, 0, 1), a[:, swap].reshape(-1, P, P).transpose(2, 0, 1)], 1)
    o["lt_wq"], o["lt_wk"] = chunks(wq), chunks(wk)
    o["lt_wv"] = i["L2_attn_Wv"].T
    o["lt_wo"] = i["L2_attn_Wo"].T.reshape(16, 64, P)[order].reshape(8, P, P).transpose(1, 0, 2)
    inv = 1.0 / 10000.0 ** (np.arange(0, 64, 2, dtype=np.float64) / 64)
    freqs = np.outer(np.arange(S, dtype=np.float64), inv)
    emb = np.concatenate([freqs, freqs], -1).T
    sign = np.where(np.arange(64) < 32, -1.0, 1.0)[:, None]
    o["lt_rope"] = np.stack([np.tile(np.cos(emb), (2, 1)), np.tile(np.sin(emb) * sign, (2, 1))], 1).astype(f32)
    slope = 2.0 ** (-8.0 / 16 * (np.arange(16) + 1))
    lag = np.arange(S)[None] - np.arange(P)[:, None]
    o["lt_decay"] = np.where(lag[:, None] >= 0, np.exp(-slope[None, :, None] * np.maximum(lag, 0)[:, None]), 0.0).astype(f32)
    o["sm_gate"] = i["L2_ffn_Wg"]
    o["sm_w1"] = i["L2_ffn_w1"].reshape(P, 4, P)
    o["sm_w2"] = i["L2_ffn_w2"].reshape(4, P, P).transpose(1, 0, 2)
    by_feature = lambda a: a.T.reshape(P, H, HD).transpose(0, 2, 1).reshape(P, P)
    o["sa_w"] = np.concatenate([by_feature(i["L3_attn_" + n]) for n in ("wq", "wk", "wv")], 1)
    o["sa_wo"] = i["L3_attn_wo"].T
    o["sa_desc"] = np.tile(np.arange(8, 0, -1, dtype=f32), (P, 1))
    before, eye = np.triu(np.ones((P, P), f32), 1), np.eye(P, dtype=f32)
    o["sa_counting"] = np.stack([before - 1024 * eye, before.T - 1024 * eye, np.ones((P, P), f32),
                                 np.where(np.arange(P)[:, None] > np.arange(P)[None], -1e32, 0.0).astype(f32), eye], 1)
    o["sl_w"] = i["L3_ffn_weights"].T
    o["sl_cols"] = np.stack([i["L3_ffn_scale"], i["L3_ffn_bias"]], 1)
    return o


class Env:
    pass


def program(nc, d, out):
    env = Env()
    env.d = d
    env.scratch = nc.dram_tensor("scratch", (5, 3, P, S), BF16, kind="Internal").ap()
    env.mamba_layers = 4
    with ExitStack() as ctx:
        sb = lambda n, s: ctx.enter_context(nc.sbuf_tensor(n, s, F32))
        env.banks = [ctx.enter_context(nc.psum_tensor(f"bank{i}", [P, S], F32)) for i in range(8)]
        env.X = sb("x_tokens", [P, NT, P])
        env.ident = sb("identity", [P, P])
        env.eps = sb("eps", [P, 1])
        env.one = sb("ones", [P, 1])
        loads = [(env.X[:, :, :], d["x"].rearrange("b (c p) n -> p (b c) n", p=P)), (env.ident[:, :], d["ident"])]
        loads += load_common(nc, env, ctx)
        inputs_loaded, output_stored = (ctx.enter_context(nc.semaphore(n)) for n in ("inputs_loaded", "output_stored"))
        with nc.Block() as block:
            @block.sync
            def _(sp):
                for dst, src in loads:
                    sp.dma_start(dst, src).then_inc(inputs_loaded, 16)
                sp.wait_ge(inputs_loaded, 16 * len(loads))

            @block.vector
            def _(v):
                v.memset(env.eps[:, :], EPS)
                v.memset(env.one[:, :], 1.0)
                v.memset(env.one_row[:, :], 1.0)
        if 0 in STAGES:
            mamba(nc, env)
        if 1 in STAGES:
            with ExitStack() as inner:
                w = Batch(nc, inner, env.banks, "early_")
                with nc.Fori(0, B) as b:
                    enter_batch(nc, env, w, b)
                    cross_attention(nc, env, w, "x0", b, HD ** -0.5, True, False, False)
                    leave_batch(nc, env, w, b)
        if 2 in STAGES:
            moe(nc, env)
        if max(STAGES) >= 3:
            with ExitStack() as inner:
                w = Batch(nc, inner, env.banks, "late_")
                load_late(nc, env, inner)
                with nc.Fori(0, B) as b:
                    enter_batch(nc, env, w, b)
                    with ExitStack() as until_lightning:
                        place_early_weights(nc, env, until_lightning)
                        if 3 in STAGES:
                            local_attention(nc, env, w, b)
                        if 4 in STAGES:
                            context_mlp(nc, env, w, b)
                        if 5 in STAGES:
                            grouped_mlp(nc, env, w, b)
                        if 6 in STAGES:
                            lightning(nc, env, w, b)
                    if 7 in STAGES:
                        cross_attention(nc, env, w, "x2", b, HD ** -0.5, False, True, False)
                    if 8 in STAGES:
                        shared_moe(nc, env, w, b)
                    if 9 in STAGES:
                        sparse_attention(nc, env, w, b)
                    if 10 in STAGES:
                        cross_attention(nc, env, w, "x3", b, HD ** -0.5, False, True, True)
                    if 11 in STAGES:
                        sign_linear(nc, env, w, b)
                    leave_batch(nc, env, w, b)
        with nc.Block() as block:
            @block.sync
            def _(sp):
                sp.dma_start(out.rearrange("b (c p) n -> p (b c) n", p=P), env.X[:, :, :]).then_inc(output_stored, 16)
                sp.wait_ge(output_stored, 16)


def layouts(np, i):
    L, DI, NS, R, NF = 4, 256, 16, 8, 2
    halves = lambda a: np.moveaxis(a.reshape(L, NF, P, -1), 1, 2)
    pc = np.concatenate([i["L0_attn_conv_w"], i["L0_attn_conv_b"][..., None], i["L0_attn_b_dt"][..., None],
                         i["L0_attn_Dp"][..., None], i["L0_attn_A_log"]], -1)
    flat = lambda a: a.reshape(L, P, -1)
    f32 = np.float32
    o = {
        "x": i["x"],
        "ident": np.eye(P, dtype=f32),
        "mamba_w": np.concatenate([i["L0_attn_W_in"].transpose(0, 2, 1),
                                   flat(halves(i["L0_attn_W_x"].transpose(0, 2, 1))),
                                   flat(halves(i["L0_attn_W_out"].transpose(0, 2, 1))),
                                   flat(halves(pc)),
                                   i["L0_attn_ln_w"][..., None], i["L0_attn_ln_b"][..., None]], -1),
        "mamba_wdt": i["L0_attn_W_dt"].transpose(0, 2, 1),
        "ctx": i["ctx_1024"],
        "ctx_t": i["ctx_1024"].transpose(0, 2, 1),
        "mask": i["mask_BxSxS2_if1"],
        "head_mask": np.repeat(np.eye(H, dtype=f32), HD, axis=0),
        "x0_w": np.stack([i["L0_xattn_W_Q"], i["L0_xattn_W_K"], i["L0_xattn_W_V"], i["L0_xattn_W_O"]], 1),
        "tri": np.triu(np.ones((P, P), f32), 1),
        "desc": np.tile(np.arange(8, 0, -1, dtype=f32), (P, 1)),
        "moe_gate": i["L0_ffn_Wg"].T,
        "moe_w1": i["L0_ffn_W1"].reshape(8, P, 4, P),
        "moe_w2": i["L0_ffn_W2"].reshape(8, 4, P, P).transpose(0, 2, 1, 3),
        "moe_b1": i["L0_ffn_b1"].reshape(8, 4, P).transpose(0, 2, 1),
        "moe_b2": i["L0_ffn_b2"],
    }
    for pre, name in (("x2", "L2_xattn_"), ("x3", "L3_xattn_")):
        o[pre + "_w"] = np.stack([i[name + n].T for n in ("Wq", "Wk", "Wv", "Wo")], 1)
        o[pre + "_cols"] = np.stack([i[name + "bq"], i[name + "bk"]], 1)
        o[pre + "_rows"] = np.stack([i[name + "bv"], i[name + ("bo" if pre == "x3" else "bv")]])[None]
    sel = np.zeros((3, 2 * NS, 2 * NS, P), f32)
    for n in range(2 * NS):
        sel[:, n, n, :] = 1.0
    sel = sel.reshape(6 * NS, 2 * NS, P)
    o["mamba_sel"] = sel
    o.update(late_layouts(np, i))
    return o


def kernel(**inputs):
    import numpy as np
    import concourse.bacc as bacc
    from concourse.bass_utils import run_bass_kernel_spmd as run

    nc = bacc.Bacc("TRN2", target_bir_lowering=False, num_devices=1)
    arrays, d = {}, {}
    for name, a in layouts(np, inputs).items():
        a = np.ascontiguousarray(a)
        arrays["in_" + name] = a
        d[name] = nc.dram_tensor("in_" + name, a.shape, mybir.dt.from_np(a.dtype), kind="ExternalInput").ap()
    out = nc.dram_tensor("out", (B, S, P), F32, kind="ExternalOutput").ap()
    program(nc, d, out)
    return run(nc, [arrays], core_ids=[0]).results[0]["out"]
```

```python
import concourse.bass as bass
from concourse import mybir
from contextlib import ExitStack

F32 = mybir.dt.float32
I32 = mybir.dt.int32
BF16 = mybir.dt.bfloat16
F16 = mybir.dt.float16
ALU = mybir.AluOpType
ACT = mybir.ActivationFunctionType
AX = mybir.AxisListType

P = 128
B = 4
S = 512
TB = S // P
NT = B * TB
EPS = 1e-5
H = 16
HD = P // H
SK = 77
KP = 80
FIRST_SEM = 110


class Chain:

    def __init__(self, eng, sem):
        self.eng, self.sem, self.n = eng, sem, 0

    def __call__(self, ins):
        self.n += 1
        ins.then_inc(self.sem, 1)
        self.eng.wait_ge(self.sem, self.n)

    def mark(self, ins):
        self.n += 1
        ins.then_inc(self.sem, 1)
        return self.n

    def wait_for(self, n):
        self.eng.wait_ge(self.sem, n)


def semaphores(nc, ctx, names):
    names = names.split()
    handles = [ctx.enter_context(nc.semaphore(n, num=FIRST_SEM + i)) for i, n in enumerate(names)]
    return dict(zip(names, handles), numbers=range(FIRST_SEM, FIRST_SEM + len(names)))


def layer_norm_stats(v, chain, src, st, mv, tiles, s_var):
    for t in range(tiles):
        ins = v.bn_stats(st[:, t, :], src[:, t, :])
    chain(ins)
    for t in range(tiles):
        ins = v.bn_aggr(mv[:, t, :], st[:, t, :])
    ins.then_inc(s_var, 1)


def mamba(nc, env):
    DI, NS, R, K = 256, 16, 8, 4
    NF = DI // P
    X = env.X
    cols, at = {}, 0
    NX = 3 * 2 * NS
    for name, n in (("wi", 2 * DI), ("wx", NF * (R + 2 * NS)), ("wo", NF * P), ("pc", NF * (K + 3 + NS)), ("ln", 2)):
        cols[name] = (at, at + n)
        at += n
    with ExitStack() as ctx:
        sb = lambda n, s, t=F32: ctx.enter_context(nc.sbuf_tensor(n, s, t))
        wl = sb("mamba_w", [P, at])
        wdt = sb("mamba_wdt", [R, DI])
        sel32 = sb("state_selector_f32", [NX, 2 * NS, P])
        sel = sb("state_selector", [NX, 2 * NS, P], BF16)
        wx3 = sb("wx_three_times", [P, NF, NX])
        X0 = sb("x_before_mamba", [P, NT, P])
        xh = sb("x_normed", [P, NT, P])
        st = sb("bn_stats", [P, NT, 6])
        mv = sb("mean_var", [P, NT, 2])
        sd = sb("std", [P, NT])
        rs = sb("rstd", [P, NT])
        xn = sb("xn_t", [P, B, S])
        xp = sb("xs_padded", [P, 2, NF, K - 1 + S])
        sz = sb("silu_z", [P, B, NF, S])
        cv = sb("conv", [P, 2, NF, S])
        u = sb("u", [P, B, NF, S])
        xd = sb("dt_low_rank", [R, B, S])
        bc = sb("b_c_rows", [NX, 2, S])
        bc3 = sb("b_c_parts", [NX, B, S], BF16)
        dt = sb("dt", [P, B, NF, S])
        dtu = sb("dtu", [P, B, NF, S])
        an = sb("a_neg", [P, NF, NS])
        dA = sb("dA", [P, 4, S])
        dBu = sb("dBu", [P, 3, S])
        hs = sb("h_states", [P, 4, S])
        cs = sb("c_copy", [P, 2, S])
        hc = cv[:, :, :, :].rearrange("p a f s -> p (a f) s")
        yt = sb("y_t", [P, NF, S])
        ps = env.banks
        s = semaphores(nc, ctx, "m_w m_var m_sd m_vc m_xh m_xt m_xn m_pj m_pje m_cv m_u m_xd m_xde m_dtp m_v m_e m_l m_dt "
                          "m_wx m_bcx m_pc m_bce m_bcs m_ae m_a m_bc m_da m_dbu m_cs m_hs m_hc m_yt m_o m_sel m_xa m_ga m_ra")
        wi = wl[:, cols["wi"][0]:cols["wi"][1]]
        wx = wl[:, cols["wx"][0]:cols["wx"][1]].rearrange("p (f n) -> p f n", f=NF)
        wo = wl[:, cols["wo"][0]:cols["wo"][1]].rearrange("p (f n) -> p f n", f=NF)
        pc = wl[:, cols["pc"][0]:cols["pc"][1]].rearrange("p (f n) -> p f n", f=NF)
        lnw, lnb = (wl[:, cols["ln"][0] + i:cols["ln"][0] + i + 1] for i in range(2))
        CB, BDT, DP, AL = K, K + 1, K + 2, K + 3
        psB, psC = ps[0:2], ps[2:4]
        psY = lambda b, f: ps[4 + 2 * (b % 2) + f]

        with nc.Block() as block:
            @block.sync
            def _(sp_):
                sp_.dma_start(sel32[:, :, :], env.d["mamba_sel"]).then_inc(s["m_sel"], 16)
                sp_.wait_ge(s["m_sel"], 16)

            @block.vector
            def _(v):
                v.tensor_copy(X0[:, :, :], X[:, :, :])
                v.memset(xp[:, :, :, :], 0.0)
                v.wait_ge(s["m_sel"], 16)
                v.tensor_copy(sel[:, :, :], sel32[:, :, :])
        nc.all_engine_barrier(sems_to_clear=s["numbers"])

        def split(eng, chain, b, done):
            x, parts, rows = bc[:, b % 2, :], bc3[:, b, :], NX
            while rows:
                ins = eng.tensor_copy(parts[0:rows, :], x[0:rows, :])
                rows -= 2 * NS
                if rows:
                    chain(ins)
                    chain(eng.tensor_tensor(x[0:rows, :], x[0:rows, :], parts[0:rows, :], ALU.subtract))
            ins.then_inc(s[done], 1)

        with nc.Fori(0, env.mamba_layers) as layer:
            with nc.Block() as block:
                @block.sync
                def _(sp_):
                    sp_.dma_start(wl[:, :], env.d["mamba_w"][bass.ds(layer, 1), :, :].rearrange("o p n -> p (o n)"))\
                        .then_inc(s["m_w"], 16)
                    sp_.dma_start(wdt[:, :], env.d["mamba_wdt"][bass.ds(layer, 1), :, :].rearrange("o p n -> p (o n)"))\
                        .then_inc(s["m_w"], 16)

                @block.vector
                def _(v):
                    chain = Chain(v, s["m_vc"])
                    layer_norm_stats(v, chain, X, st, mv, NT, s["m_var"])
                    v.wait_ge(s["m_sd"], 1)
                    chain(v.reciprocal(rs[:, :], sd[:, :]))
                    for t in range(NT):
                        v.tensor_scalar(xh[:, t, :], X[:, t, :], mv[:, t, 0:1], rs[:, t:t + 1],
                                        ALU.subtract, ALU.mult).then_inc(s["m_xh"], 1)
                    v.wait_ge(s["m_w"], 32)
                    for b in range(B):
                        for f in range(NF):
                            v.wait_ge(s["m_xa"], NF * b + f + 1)
                            if b >= 2:
                                v.wait_ge(s["m_u"], NF * (b - 2) + f + 1)
                            c = cv[:, b % 2, f, :]
                            chain(v.tensor_scalar(c, xp[:, b % 2, f, 0:S], pc[:, f, 0:1], pc[:, f, CB:CB + 1],
                                                  ALU.mult, ALU.add))
                            for k in range(1, K):
                                ins = v.scalar_tensor_tensor(out=c, in0=xp[:, b % 2, f, k:k + S],
                                                             scalar=pc[:, f, k:k + 1], in1=c,
                                                             op0=ALU.mult, op1=ALU.add)
                                if k < K - 1:
                                    chain(ins)
                            ins.then_inc(s["m_cv"], 1)
                    v.wait_ge(s["m_ae"], 1)
                    v.tensor_scalar(an[:, :, :], an[:, :, :], -1.0, None, ALU.mult).then_inc(s["m_a"], 1)

                    v.wait_ge(s["m_u"], NF * B)
                    for i in range(B * NF):
                        b, f = divmod(i, NF)
                        v.wait_ge(s["m_dtp"], i + 1)
                        chain(v.tensor_scalar(dt[:, b, f, :], ps[i % 4][:, :], pc[:, f, BDT:BDT + 1], None, ALU.add))
                        v.scalar_tensor_tensor(out=dtu[:, b, f, :], in0=dt[:, b, f, :], scalar=-1.0,
                                               in1=dt[:, b, f, :], op0=ALU.mult, op1=ALU.max).then_inc(s["m_v"], 1)

                    v.wait_ge(s["m_bce"], B)
                    split(v, chain, B - 1, "m_bcx")

                    def softplus_out(i):
                        b, f = divmod(i, NF)
                        v.wait_ge(s["m_l"], i + 1)
                        chain(v.scalar_tensor_tensor(out=dt[:, b, f, :], in0=dt[:, b, f, :], scalar=0.0,
                                                     in1=dtu[:, b, f, :], op0=ALU.max, op1=ALU.add))
                        v.tensor_tensor(dtu[:, b, f, :], dt[:, b, f, :], u[:, b, f, :], ALU.mult).then_inc(s["m_dt"], 1)

                    for i in range(NF):
                        softplus_out(i)

                    def gate(b):
                        for f in range(NF):
                            v.wait_ge(s["m_ga"], NF * (NS * b + NS - 1) + f + 1)
                            if b >= 1:
                                v.wait_ge(s["m_o"], b)
                            chain(v.scalar_tensor_tensor(out=yt[:, f, :], in0=u[:, b, f, :], scalar=pc[:, f, DP:DP + 1],
                                                         in1=psY(b, f)[:, :], op0=ALU.mult, op1=ALU.add))
                            v.tensor_tensor(yt[:, f, :], yt[:, f, :], sz[:, b, f, :], ALU.mult).then_inc(s["m_yt"], 1)

                    def residual(b):
                        v.wait_ge(s["m_o"], b + 1)
                        v.tensor_tensor(X[:, TB * b:TB * b + TB, :], X[:, TB * b:TB * b + TB, :],
                                        psY(b, 0)[:, :].rearrange("p (c n) -> p c n", c=TB), ALU.add)\
                            .then_inc(s["m_ra"], 1)

                    def input_term(i):
                        j, f = divmod(i, NF)
                        b, n = divmod(j, NS)
                        v.wait_ge(s["m_bc"], j + 1)
                        if i >= 3:
                            v.wait_ge(s["m_hs"], i - 2)
                        v.tensor_tensor(dBu[:, i % 3, :], psB[n % 2][:, :], dtu[:, b, f, :], ALU.mult)\
                            .then_inc(s["m_dbu"], 1)

                    def scan(i):
                        v.wait_ge(s["m_dbu"], i + 1)
                        v.wait_ge(s["m_da"], i + 1)
                        if i >= 4:
                            v.wait_ge(s["m_hc"], i - 3)
                        v.tensor_tensor_scan(hs[:, i % 4, :], dA[:, i % 4, :], dBu[:, i % 3, :], 0.0,
                                             ALU.mult, ALU.add).then_inc(s["m_hs"], 1)

                    for i in range(B * NS * NF):
                        j, f = divmod(i, NF)
                        b, n = divmod(j, NS)
                        if f == 0 and n == 8 and b + 1 < B:
                            softplus_out(NF * b + NF)
                            softplus_out(NF * b + NF + 1)
                            v.wait_ge(s["m_dt"], NF * (b + 2))
                        if i == 0:
                            v.wait_ge(s["m_dt"], NF)
                        input_term(i)
                        if i >= 1:
                            scan(i - 1)
                        if f == 1 and b >= 1 and n == 2:
                            gate(b - 1)
                        if f == 1 and b >= 1 and n == 10:
                            residual(b - 1)
                    scan(B * NS * NF - 1)
                    gate(B - 1)
                    residual(B - 1)

                @block.gpsimd
                def _(g):
                    pool = Chain(g, s["m_pc"])
                    for b in range(B - 1):
                        g.wait_ge(s["m_bce"], b + 1)
                        split(g, pool, b, "m_bcs")
                    for i in range(B * NS * NF):
                        g.wait_ge(s["m_hs"], i + 1)
                        g.wait_ge(s["m_cs"], i // NF + 1)
                        if i >= 4:
                            g.wait_ge(s["m_ga"], i - 3)
                        g.tensor_tensor(hc[:, i % 4, :], hs[:, i % 4, :], cs[:, (i // NF) % 2, :], ALU.mult)\
                            .then_inc(s["m_hc"], 1)

                @block.scalar
                def _(a):
                    a.wait_ge(s["m_var"], 1)
                    a.activation(sd[:, :], mv[:, :, 1], ACT.Sqrt, bias=env.eps[:, 0:1]).then_inc(s["m_sd"], 1)
                    a.wait_ge(s["m_w"], 32)
                    for x in range(3):
                        ins = a.activation(wx3[:, :, 2 * NS * x:2 * NS * (x + 1)], wx[:, :, R:], ACT.Copy)
                    ins.then_inc(s["m_wx"], 1)

                    def normed(b):
                        a.wait_ge(s["m_xt"], b + 1)
                        a.activation(xn[:, b, :], ps[4 + b % 2][:, :], ACT.Identity, scale=lnw, bias=lnb)\
                            .then_inc(s["m_xn"], 1)

                    def inner(b):
                        for m in range(NF):
                            a.wait_ge(s["m_pj"], 4 * b + m + 1)
                            if b >= 2:
                                a.wait_ge(s["m_cv"], NF * (b - 2) + m + 1)
                            a.activation(xp[:, b % 2, m, K - 1:K - 1 + S], ps[m][:, :], ACT.Copy).then_inc(s["m_xa"], 1)

                    def low_rank(b):
                        a.wait_ge(s["m_xd"], b + 1)
                        a.activation(xd[:, b, :], ps[6][0:R, :], ACT.Copy).then_inc(s["m_xde"], 1)
                        if b >= 2:
                            a.wait_ge(s["m_bcs"], b - 1)
                        a.activation(bc[:, b % 2, :], ps[7][0:NX, :], ACT.Copy).then_inc(s["m_bce"], 1)

                    normed(0)
                    normed(1)
                    inner(0)
                    for b in range(B):
                        for m in range(NF):
                            a.wait_ge(s["m_pj"], 4 * b + NF + m + 1)
                            a.activation(sz[:, b, m, :], ps[NF + m][:, :], ACT.Silu).then_inc(s["m_pje"], 1)
                        if b + 2 < B:
                            normed(b + 2)
                        if b + 1 < B:
                            inner(b + 1)
                        for f in range(NF):
                            a.wait_ge(s["m_cv"], NF * b + f + 1)
                            a.activation(u[:, b, f, :], cv[:, b % 2, f, :], ACT.Silu).then_inc(s["m_u"], 1)
                        if b >= 1:
                            low_rank(b - 1)
                    low_rank(B - 1)
                    a.activation(an[:, :, :], pc[:, :, AL:AL + NS], ACT.Exp).then_inc(s["m_ae"], 1)
                    for i in range(B * NF):
                        a.wait_ge(s["m_v"], i + 1)
                        x = dtu[:, i // NF, i % NF, :]
                        a.activation(x, x, ACT.Exp, scale=-1.0).then_inc(s["m_e"], 1)
                    for i in range(B * NF):
                        a.wait_ge(s["m_e"], i + 1)
                        x = dtu[:, i // NF, i % NF, :]
                        a.activation(x, x, ACT.Ln, bias=env.one[:, 0:1]).then_inc(s["m_l"], 1)
                    a.wait_ge(s["m_a"], 1)
                    for j in range(B * NS):
                        b, n = divmod(j, NS)
                        for f in range(NF):
                            i = j * NF + f
                            a.wait_ge(s["m_dt"], NF * b + f + 1)
                            if i >= 4:
                                a.wait_ge(s["m_hs"], i - 3)
                            a.activation(dA[:, i % 4, :], dt[:, b, f, :], ACT.Exp, scale=an[:, f, n:n + 1])\
                                .then_inc(s["m_da"], 1)
                        a.wait_ge(s["m_bc"], j + 1)
                        if j >= 2:
                            a.wait_ge(s["m_hc"], NF * (j - 1))
                        a.activation(cs[:, j % 2, :], psC[j % 2][:, :], ACT.Copy).then_inc(s["m_cs"], 1)

                @block.tensor
                def _(t):
                    t.wait_ge(s["m_w"], 32)

                    def turn(b):
                        if b >= 2:
                            t.wait_ge(s["m_xn"], b - 1)
                        for c in range(TB):
                            t.wait_ge(s["m_xh"], TB * b + c + 1)
                            ins = t.transpose(ps[4 + b % 2][:, c * P:(c + 1) * P], xh[:, TB * b + c, :], env.ident[:, :])
                        ins.then_inc(s["m_xt"], 1)

                    def project(b):
                        t.wait_ge(s["m_xn"], b + 1)
                        if b >= 1:
                            t.wait_ge(s["m_xa"], NF * b)
                            t.wait_ge(s["m_pje"], NF * b)
                        for m in range(4):
                            t.matmul(ps[m][:, :], wi[:, m * P:(m + 1) * P], xn[:, b, :],
                                     start=True, stop=True).then_inc(s["m_pj"], 1)

                    def x_dbl(b):
                        if b >= 1:
                            t.wait_ge(s["m_xde"], b)
                            t.wait_ge(s["m_bce"], b)
                        t.wait_ge(s["m_wx"], 1)
                        for f in range(NF):
                            t.wait_ge(s["m_u"], NF * b + f + 1)
                            t.matmul(ps[6][0:R, :], wx[:, f, 0:R], u[:, b, f, :], start=(f == 0), stop=(f == NF - 1))
                            ins = t.matmul(ps[7][0:NX, :], wx3[:, f, :], u[:, b, f, :], start=(f == 0), stop=(f == NF - 1))
                        ins.then_inc(s["m_xd"], 1)

                    turn(0)
                    turn(1)
                    for b in range(B):
                        project(b)
                        if b + 2 < B:
                            turn(b + 2)
                        if b >= 1:
                            x_dbl(b - 1)
                    x_dbl(B - 1)
                    t.wait_ge(s["m_pje"], NF * B)
                    t.wait_ge(s["m_xa"], NF * B)
                    for i in range(B * NF):
                        b, f = divmod(i, NF)
                        t.wait_ge(s["m_xde"], b + 1)
                        if i >= 4:
                            t.wait_ge(s["m_v"], i - 3)
                        t.matmul(ps[i % 4][:, :], wdt[:, f * P:(f + 1) * P], xd[0:R, b, :],
                                 start=True, stop=True).then_inc(s["m_dtp"], 1)
                    t.wait_ge(s["m_v"], B * NF)

                    def spread(j):
                        b, n = divmod(j, NS)
                        if n == 0:
                            if b < B - 1:
                                t.wait_ge(s["m_bcs"], b + 1)
                            else:
                                t.wait_ge(s["m_bcx"], 1)
                        if j >= 2:
                            t.wait_ge(s["m_dbu"], NF * (j - 1))
                            t.wait_ge(s["m_cs"], j - 1)
                        t.matmul(psB[j % 2][:, :], sel[:, n, :], bc3[:, b, :], start=True, stop=True)
                        t.matmul(psC[j % 2][:, :], sel[:, NS + n, :], bc3[:, b, :], start=True, stop=True)\
                            .then_inc(s["m_bc"], 1)

                    def gather(i):
                        b, r = divmod(i, NF * NS)
                        n, f = divmod(r, NF)
                        t.wait_ge(s["m_hc"], i + 1)
                        if n == 0 and b >= 2:
                            t.wait_ge(s["m_ra"], b - 1)
                        t.matmul(psY(b, f)[:, :], env.ident[:, :], hc[:, i % 4, :], start=(n == 0), stop=(n == NS - 1))\
                            .then_inc(s["m_ga"], 1)

                    def out(b, c):
                        for f in range(NF):
                            t.wait_ge(s["m_yt"], NF * b + f + 1)
                            ins = t.matmul(psY(b, 0)[:, c * P:(c + 1) * P], yt[:, f, c * P:(c + 1) * P],
                                           wo[:, f, :], start=(f == 0), stop=(f == NF - 1))
                        if c == TB - 1:
                            ins.then_inc(s["m_o"], 1)

                    spread(0)
                    for b in range(B):
                        for n in range(NS):
                            j = b * NS + n
                            if j + 1 < B * NS:
                                spread(j + 1)
                            for f in range(NF if j else 0):
                                gather(NF * (j - 1) + f)
                            if b >= 1 and 4 <= n < 4 + TB:
                                out(b - 1, n - 4)
                    for f in range(NF):
                        gather(NF * (B * NS - 1) + f)
                    for c in range(TB):
                        out(B - 1, c)
            nc.all_engine_barrier(sems_to_clear=s["numbers"])

        with nc.Block() as block:
            finish_layer_norm(block, X, X0, xh, st, mv, sd, rs, NT, env, s["m_vc"], s["m_var"], s["m_sd"], s["m_v"])
        nc.all_engine_barrier(sems_to_clear=s["numbers"])


def finish_layer_norm(block, X, Y, R, st, mv, sd, rs, tiles, env, s_chain, s_var, s_sd, s_done):
    @block.vector
    def _(v):
        chain = Chain(v, s_chain)
        chain(v.tensor_tensor(R[:, :, :], X[:, :, :], Y[:, :, :], ALU.add))
        layer_norm_stats(v, chain, R, st, mv, tiles, s_var)
        v.wait_ge(s_sd, 1)
        chain(v.reciprocal(rs[:, :], sd[:, :]))
        for t in range(tiles):
            v.tensor_scalar(X[:, t, :], R[:, t, :], mv[:, t, 0:1], rs[:, t:t + 1], ALU.subtract, ALU.mult)\
                .then_inc(s_done, 1)

    @block.scalar
    def _(a):
        a.wait_ge(s_var, 1)
        a.activation(sd[:, :], mv[:, :, 1], ACT.Sqrt, bias=env.eps[:, 0:1]).then_inc(s_sd, 1)


def batch_tile(env, b):
    return lambda c: env.X[:, bass.ds(b * TB + c, 1), :].rearrange("p o n -> p (o n)")


def normalise(v, chain, sm, w, y, X, out=None):
    if len(y.shape) == 2:
        y = y[:, :].rearrange("p (c n) -> p c n", c=TB)
    chain(v.tensor_tensor(w.R[:, :, :], X[:, :, :], y[:, :, :], ALU.add))
    found = [chain.mark(v.bn_stats(w.st[:, c, :], w.R[:, c, :])) for c in range(TB)]
    for c in range(TB):
        chain.wait_for(found[c])
        ins = v.bn_aggr(w.mv[:, c, :], w.st[:, c, :])
    ins.then_inc(sm["var"], 1)
    v.wait_ge(sm["sd"], 1)
    chain(v.reciprocal(w.rs[:, :], w.sd[:, :]))
    for c in range(TB):
        v.tensor_scalar(out(c) if out else X[:, c, :], w.R[:, c, :], w.mv[:, c, 0:1], w.rs[:, c:c + 1],
                        ALU.subtract, ALU.mult).then_inc(sm["xn"], 1)


def turn_tokens(t, sm, X, banks, ident):
    for c in range(TB):
        t.wait_ge(sm["xn"], c + 1)
        ins = t.transpose(banks[c // 2][:, (c % 2) * P:(c % 2 + 1) * P], X[:, c, :], ident[:, :])
        if c % 2:
            ins.then_inc(sm["tr"], 1)


def std_and_turn(a, sm, w, XT, banks, eps, following):
    a.activation(w.scrap[:, 0:1], eps[:, 0:1], ACT.Sqrt)
    a.wait_ge(sm["var"], 1)
    a.activation(w.sd[:, :], w.mv[:, :, 1], ACT.Sqrt, bias=eps[:, 0:1]).then_inc(sm["sd"], 1)
    if following is None:
        return
    a.activation(w.scrap[:, 1:2], eps[:, 0:1], following)
    for i in range(2):
        a.wait_ge(sm["tr"], i + 1)
        a.activation(XT[:, 2 * i * P:2 * (i + 1) * P], banks[i][:, 0:2 * P], ACT.Copy)


LN_SEMS = "var sd xn tr chain "


class Batch:

    def __init__(self, nc, ctx, banks, tag):
        sb = lambda n, s: ctx.enter_context(nc.sbuf_tensor(tag + n, s, F32))
        self.X = sb("tokens", [P, TB, P])
        self.XT = sb("t", [P, S])
        self.ctxT = sb("ctx_t", [P, SK])
        self.ctx = sb("ctx", [SK, P])
        self.R = sb("residual", [P, TB, P])
        self.st = sb("bn_stats", [P, TB, 6])
        self.mv = sb("mean_var", [P, TB, 2])
        self.sd = sb("std", [P, TB])
        self.rs = sb("rstd", [P, TB])
        self.scrap = sb("scrap", [P, 2])
        self.ps = banks


def enter_batch(nc, env, w, b):
    with ExitStack() as ctx:
        s = semaphores(nc, ctx, "copied turned")
        with nc.Block() as block:
            @block.vector
            def _(v):
                v.tensor_copy(w.X[:, :, :], env.X[:, bass.ds(b * TB, TB), :]).then_inc(s["copied"], 1)

            @block.tensor
            def _(t):
                t.wait_ge(s["copied"], 1)
                for c in range(TB):
                    ins = t.transpose(w.ps[0][:, c * P:(c + 1) * P], w.X[:, c, :], env.ident[:, :])
                ins.then_inc(s["turned"], 1)

            @block.scalar
            def _(a):
                a.activation(w.ctxT[:, :], env.ctxT[:, bass.ds(b, 1), :].rearrange("p o n -> p (o n)"), ACT.Copy)
                a.activation(w.ctx[:, :], env.ctx[:, bass.ds(b, 1), :].rearrange("p o n -> p (o n)"), ACT.Copy)
                a.wait_ge(s["turned"], 1)
                a.activation(w.XT[:, :], w.ps[0][:, :], ACT.Copy)
        nc.all_engine_barrier(sems_to_clear=s["numbers"])


def cross_attention(nc, env, w, pre, b, scale, masked, biased, out_bias):
    wt = env.weights[pre]
    cols = env.columns.get(pre)
    rows = env.rows.get(pre)
    GH = (0, 6, 12, 16)
    NG = len(GH) - 1
    NCH, NW = H * KP // P, 5
    first = [x * P // KP for x in range(NW)]
    reach = [((x + 1) * P - 1) // KP + 1 - first[x] for x in range(NW)]
    AHEAD = NW * P // KP
    TQ = (0, 4, 8, NCH)
    last = pre == "x0"
    X, XT, ps = w.X, w.XT, w.ps
    with ExitStack() as ctx:
        sb = lambda n, s, t=F32: ctx.enter_context(nc.sbuf_tensor(pre + n, s, t))
        kt = sb("k_t", [P, SK])
        kb = sb("k_by_head", [P, H, SK])
        cx = sb("context_t_three_times", [P, 3, KP])
        vb = sb("v_of_chunk", [P, 2, NW, 3 * HD])
        qt = sb("q_t", [P, S])
        D = sb("scores", [P, 2, H, KP])
        mx = sb("max", [P, 2, H])
        zs = sb("sum", [P, 2, H])
        pt = sb("p_t", [P, NCH, P])
        o = sb("o", [P, 2, P])
        ot = sb("o_t", [P, 2, P])
        if masked:
            mi = sb("mask_int", [P, TB, SK], I32)
            mf = sb("mask", [P, TB, SK])
            pen = sb("penalty", [P, TB, SK])
        s = semaphores(nc, ctx, LN_SEMS + "proj empty cx kt q vb kb sc dd ex pt pte pv on ot ote y mk")
        psS, psT, psV, psO, psY = ps[0:3], ps[3:5], ps[5], ps[6], ps[7]
        with nc.Block() as block:
            @block.sync
            def _(sp):
                if masked:
                    src = env.d["mask"][bass.ds(b, 1), :, :].rearrange("o (c p) n -> p (o c) n", p=P)
                    sp.dma_start(mi[:, :, :], src).then_inc(s["mk"], 16)
                    sp.wait_ge(s["mk"], 16)

            @block.tensor
            def _(t):
                t.matmul(psS[0][:, 0:SK], wt[:, 1, :], w.ctxT[:, :], start=True, stop=True).then_inc(s["proj"], 1)
                t.matmul(psS[1][:, :], wt[:, 0, :], XT[:, :], start=True, stop=True).then_inc(s["proj"], 1)
                def scores(c):
                    t.wait_ge(s["kb"], 1)
                    t.wait_ge(s["q"], 1)
                    if c >= 1:
                        t.wait_ge(s["dd"], NG * c)
                    for g in range(NG):
                        n = (GH[g + 1] - GH[g]) * SK
                        t.matmul(psS[g][:, 0:n], qt[:, c * P:(c + 1) * P],
                                 kb[:, GH[g]:GH[g + 1], :].rearrange("p h n -> p (h n)"),
                                 start=True, stop=True).then_inc(s["sc"], 1)

                def values():
                    t.wait_ge(s["cx"], 1)
                    for x in range(NW):
                        out, at = psT[x // 4][:, (x % 4) * P:(x % 4 + 1) * P], x * P % KP
                        ins = t.matmul(out, cx[:, :, :].rearrange("p a n -> p (a n)")[:, at:at + P], wt[:, 2, :],
                                       start=True, stop=not biased)
                        if biased:
                            ins = t.matmul(out, env.one_row[0:1, :], rows[0:1, 0, :], start=False, stop=True)
                    ins.then_inc(s["proj"], 1)

                def turn_and_weigh(c):
                    t.wait_ge(s["ex"], c + 1)
                    t.wait_ge(s["vb"], 1)
                    t.wait_ge(s["empty"], 2)
                    for q in range(len(TQ) - 1):
                        i = 3 * c + q
                        if i >= 2:
                            t.wait_ge(s["pte"], i - 1)
                        for k in range(TQ[q], TQ[q + 1]):
                            at = (k - TQ[q]) * P
                            ins = t.transpose(psT[i % 2][:, at:at + P],
                                              D[:, c % 2, :, :].rearrange("p h n -> p (h n)")[:, k * P:(k + 1) * P],
                                              env.ident[:, :])
                        ins.then_inc(s["pt"], 1)
                    if c >= 1:
                        t.wait_ge(s["on"], c)
                    for k in range(NCH):
                        if k in TQ:
                            t.wait_ge(s["pte"], 3 * c + TQ.index(k) + 1)
                        x = k % NW
                        h, n = first[x] + AHEAD * (k // NW), reach[x]
                        ins = t.matmul(psV[:, h * HD:(h + n) * HD], pt[:, k, :], vb[:, k // NW, x, 0:n * HD],
                                       start=(k == 0), stop=(k == NCH - 1), skip_group_check=True)
                    ins.then_inc(s["pv"], 1)

                def project(c):
                    t.wait_ge(s["on"], c + 1)
                    if c >= 1:
                        t.wait_ge(s["ote"], c)
                    t.transpose(psO[:, 0:P], o[:, c % 2, :], env.ident[:, :]).then_inc(s["ot"], 1)
                    t.wait_ge(s["ote"], c + 1)
                    ins = t.matmul(psY[:, c * P:(c + 1) * P], ot[:, c % 2, :], wt[:, 3, :], start=True, stop=not out_bias)
                    if out_bias:
                        ins = t.matmul(psY[:, c * P:(c + 1) * P], env.one_row[0:1, :], rows[0:1, 1, :],
                                       start=False, stop=True)
                    ins.then_inc(s["y"], 1)

                scores(0)
                values()
                for c in range(TB):
                    if c + 1 < TB:
                        scores(c + 1)
                    turn_and_weigh(c)
                    if c >= 1:
                        project(c - 1)
                project(TB - 1)
                if not last:
                    turn_tokens(t, s, X, ps[0:2], env.ident)

            @block.scalar
            def _(a):
                a.wait_ge(s["empty"], 1)
                a.activation(cx[:, :, 0:SK], w.ctxT[:, None, :].broadcast_to([P, 3, SK]), ACT.Copy).then_inc(s["cx"], 1)
                a.wait_ge(s["proj"], 1)
                if biased:
                    a.activation(kt[:, :], psS[0][:, 0:SK], ACT.Identity, bias=cols[:, 1:2]).then_inc(s["kt"], 1)
                else:
                    a.activation(kt[:, :], psS[0][:, 0:SK], ACT.Copy).then_inc(s["kt"], 1)
                a.wait_ge(s["proj"], 2)
                if biased:
                    a.activation(qt[:, :], psS[1][:, :], ACT.Identity, bias=cols[:, 0:1]).then_inc(s["q"], 1)
                else:
                    a.activation(qt[:, :], psS[1][:, :], ACT.Copy).then_inc(s["q"], 1)

                def exps(c):
                    a.wait_ge(s["dd"], NG * (c + 1))
                    a.activation(D[:, c % 2, :, 0:SK], D[:, c % 2, :, 0:SK], ACT.Exp, scale=scale).then_inc(s["ex"], 1)

                def p_out(c):
                    for q in range(len(TQ) - 1):
                        i = 3 * c + q
                        a.wait_ge(s["pt"], i + 1)
                        if c >= 1:
                            a.wait_ge(s["pv"], c)
                        n = TQ[q + 1] - TQ[q]
                        a.activation(pt[:, TQ[q]:TQ[q + 1], :],
                                     psT[i % 2][:, 0:n * P].rearrange("p (k n) -> p k n", k=n), ACT.Copy).then_inc(s["pte"], 1)

                def o_out(c):
                    a.wait_ge(s["ot"], c + 1)
                    if c >= 2:
                        a.wait_ge(s["y"], c - 1)
                    a.activation(ot[:, c % 2, :], psO[:, 0:P], ACT.Copy).then_inc(s["ote"], 1)

                for c in range(TB):
                    exps(c)
                    p_out(c)
                    if c >= 1:
                        o_out(c - 1)
                o_out(TB - 1)
                std_and_turn(a, s, w, XT, ps[0:2], env.eps, None if last else ACT.Exp if pre == "x2" else ACT.Copy)

            @block.gpsimd
            def _(g):
                g.memset(cx[:, :, SK:], 0.0).then_inc(s["empty"], 1)
                for i in range(2):
                    ins = g.memset(D[:, i, :, SK:], 0.0)
                ins.then_inc(s["empty"], 1)

            @block.vector
            def _(v):
                chain = Chain(v, s["chain"])
                v.wait_ge(s["kt"], 1)
                v.tensor_tensor(kb[:, :, :], kt[:, None, :].broadcast_to([P, H, SK]),
                                env.head_mask[:, :, None].broadcast_to([P, H, SK]), ALU.mult).then_inc(s["kb"], 1)
                if masked:
                    v.wait_ge(s["mk"], 16)
                    chain(v.tensor_scalar(mf[:, :, :], mi[:, :, :], 0.0, None, ALU.not_equal))
                    chain(v.tensor_scalar(pen[:, :, :], mf[:, :, :], -1.0, 1e9 / scale, ALU.add, ALU.mult))

                def shifted(c):
                    if c >= 2:
                        v.wait_ge(s["pt"], 3 * (c - 1))
                    for g in range(NG):
                        a0, a1 = GH[g], GH[g + 1]
                        src = psS[g][:, 0:(a1 - a0) * SK].rearrange("p (h n) -> p h n", n=SK)
                        d = D[:, c % 2, a0:a1, 0:SK]
                        v.wait_ge(s["sc"], NG * c + g + 1)
                        if masked:
                            m, q = (x[:, c:c + 1, :].broadcast_to([P, a1 - a0, SK]) for x in (mf, pen))
                            chain(v.tensor_tensor(d, src, m, ALU.mult))
                            chain(v.tensor_tensor(d, d, q, ALU.add))
                            src = d
                        chain(v.tensor_reduce(mx[:, c % 2, a0:a1], src, AX.X, ALU.max))
                        v.tensor_tensor(d, src, mx[:, c % 2, a0:a1, None].broadcast_to([P, a1 - a0, SK]),
                                        ALU.subtract).then_inc(s["dd"], 1)

                def weighed(c):
                    v.wait_ge(s["ex"], c + 1)
                    chain(v.tensor_reduce(zs[:, c % 2, :], D[:, c % 2, :, 0:SK], AX.X, ALU.add))
                    chain(v.reciprocal(zs[:, c % 2, :], zs[:, c % 2, :]))
                    v.wait_ge(s["pv"], c + 1)
                    if c >= 2:
                        v.wait_ge(s["ot"], c - 1)
                    v.tensor_tensor(o[:, c % 2, :].rearrange("p (h n) -> p h n", n=HD),
                                    psV[:, 0:P].rearrange("p (h n) -> p h n", n=HD),
                                    zs[:, c % 2, :, None].broadcast_to([P, H, HD]), ALU.mult).then_inc(s["on"], 1)

                shifted(0)
                v.wait_ge(s["proj"], 3)
                for x in range(NW):
                    at = (x % 4) * P + first[x] * HD
                    n = reach[x] * HD
                    for g in range(2):
                        ins = v.tensor_tensor(vb[:, g, x, 0:n], psT[x // 4][:, at + g * AHEAD * HD:at + g * AHEAD * HD + n],
                                              env.chunk_heads[:, x, 0:n], ALU.mult)
                ins.then_inc(s["vb"], 1)
                for c in range(TB):
                    if c + 1 < TB:
                        shifted(c + 1)
                    weighed(c)
                v.wait_ge(s["y"], TB)
                normalise(v, chain, s, w, psY, X, batch_tile(env, b) if last else None)
        nc.all_engine_barrier(sems_to_clear=s["numbers"])


def load_common(nc, env, ctx):
    d = env.d
    sb = lambda n, s: ctx.enter_context(nc.sbuf_tensor(n, s, F32))
    env.head_mask = sb("head_mask", [P, H])
    env.one_row = sb("one_row", [1, P])
    env.weights, env.columns, env.rows = {}, {}, {}
    env.ctxT = sb("context_t", [P, B, SK])
    env.ctx = sb("context", [SK, B, P])
    env.chunk_heads = sb("chunk_heads", [P, 5, 3 * HD])
    loads = [(env.head_mask[:, :], d["head_mask"]), (env.chunk_heads[:, :, :], d["chunk_heads"]), (env.ctxT[:, :, :], d["ctx_t"]), (env.ctx[:, :, :], d["ctx"])]
    for pre in ("x0", "x2", "x3"):
        env.weights[pre] = sb(pre + "_w", [P, 4, P])
        loads.append((env.weights[pre][:, :, :], d[pre + "_w"]))
        if pre != "x0":
            env.columns[pre] = sb(pre + "_cols", [P, 2])
            loads.append((env.columns[pre][:, :], d[pre + "_cols"]))
            env.rows[pre] = sb(pre + "_rows", [1, 2, P])
            loads.append((env.rows[pre][:, :, :], d[pre + "_rows"]))
    return loads


def moe(nc, env):
    E, HID = 8, 512
    NH = HID // P
    C = int(round(2 * B * S * 1.05 / E))
    X, d = env.X, env.d
    with ExitStack() as ctx:
        sb = lambda n, s: ctx.enter_context(nc.sbuf_tensor(n, s, F32))
        XT = sb("moe_x_t", [P, NT, P])
        wg = sb("gate_w", [P, E])
        tri = sb("strictly_before", [P, P])
        ones = sb("all_ones", [P, P])
        desc = sb("descending", [P, E])
        lg = sb("gates", [P, NT, E])
        g2 = sb("gates_left", [P, NT, E])
        tmp = sb("gate_tmp", [P, NT, E])
        m = sb("gate_max", [P, 2, NT])
        z = sb("gate_z", [P, NT])
        oh = sb("one_hot", [P, 2, NT, E])
        tot = sb("tile_totals", [P, 2 * NT, E])
        run_ = sb("running_totals", [P, 2 * NT, E])
        cw = sb("combine_w", [P, E, NT])
        w1 = sb("moe_w1", [P, 2, NH, P])
        w2 = sb("moe_w2", [P, 2, NH, P])
        b1 = sb("moe_b1", [P, 2, NH])
        b2 = sb("moe_b2", [P, 2, P])
        hT = sb("moe_h_t", [P, 2, NH, S])
        acc = sb("moe_acc", [P, NT, P])
        st = sb("moe_bn", [P, NT, 6])
        mv = sb("moe_mv", [P, NT, 2])
        sd = sb("moe_sd", [P, NT])
        rs = sb("moe_rs", [P, NT])
        ps = env.banks
        s = semaphores(nc, ctx, "e_ld e_ahead e_bias e_tr e_xt e_lg e_chain e_sub e_exp e_oh e_cnt e_w e_h e_he e_y e_acc e_var e_sd e_done")
        def load_expert(sp, e, x, sem):
            for dst, src in ((w1, "moe_w1"), (w2, "moe_w2")):
                sp.dma_start(dst[:, x, :, :], d[src][bass.ds(e, 1), :, :, :].rearrange("o p a b -> p (o a) b")).then_inc(sem, 16)
            sp.dma_start(b1[:, x, :], d["moe_b1"][bass.ds(e, 1), :, :].rearrange("o p a -> p (o a)")).then_inc(sem, 16)
            sp.dma_start(b2[:, x, :], d["moe_b2"][bass.ds(e, 1), :, :].rearrange("o p n -> p (o n)")).then_inc(sem, 16)

        with nc.Block() as block:
            @block.sync
            def _(sp):
                for dst, src in ((wg[:, :], "moe_gate"), (tri[:, :], "tri"), (desc[:, :], "desc")):
                    sp.dma_start(dst, d[src]).then_inc(s["e_ld"], 16)
                load_expert(sp, 0, 0, s["e_ahead"])
                sp.wait_ge(s["e_ahead"], 64)

            @block.tensor
            def _(t):
                for b in range(B):
                    if b >= 2:
                        t.wait_ge(s["e_xt"], b - 1)
                    for c in range(TB):
                        ins = t.transpose(ps[b % 2][:, c * P:(c + 1) * P], X[:, TB * b + c, :], env.ident[:, :])
                    ins.then_inc(s["e_tr"], 1)
                t.wait_ge(s["e_ld"], 48)
                for c in range(NT):
                    t.wait_ge(s["e_xt"], c // TB + 1)
                    ins = t.matmul(ps[2][:, c * E:(c + 1) * E], XT[:, c, :], wg[:, :], start=True, stop=True)
                ins.then_inc(s["e_lg"], 1)
                t.wait_ge(s["e_oh"], 2)
                o = oh[:, :, :, :].rearrange("p k t e -> p (k t e)")
                t.matmul(ps[3][:, 0:2 * NT * E], tri[:, :], o, start=True, stop=True)
                t.matmul(ps[4][:, 0:2 * NT * E], ones[:, :], o, start=True, stop=True).then_inc(s["e_cnt"], 1)

            @block.scalar
            def _(a):
                for b in range(B):
                    a.wait_ge(s["e_tr"], b + 1)
                    a.activation(XT[:, TB * b:TB * b + TB, :], ps[b % 2][:, :].rearrange("p (c n) -> p c n", c=TB),
                                 ACT.Copy).then_inc(s["e_xt"], 1)
                a.wait_ge(s["e_sub"], 1)
                a.activation(lg[:, :, :], lg[:, :, :], ACT.Exp).then_inc(s["e_exp"], 1)

            @block.vector
            def _(v):
                chain = Chain(v, s["e_chain"])
                v.memset(ones[:, :], 1.0)
                v.memset(acc[:, :, :], 0.0)
                bc = lambda a: a[:, :, None].broadcast_to([P, NT, E])
                v.wait_ge(s["e_lg"], 1)
                L = ps[2][:, 0:NT * E].rearrange("p (t e) -> p t e", e=E)
                chain(v.tensor_reduce(z[:, :], L, AX.X, ALU.max))
                v.tensor_tensor(lg[:, :, :], L, bc(z[:, :]), ALU.subtract).then_inc(s["e_sub"], 1)
                v.wait_ge(s["e_exp"], 1)
                chain(v.tensor_reduce(z[:, :], lg[:, :, :], AX.X, ALU.add))
                chain(v.reciprocal(z[:, :], z[:, :]))
                chain(v.tensor_tensor(lg[:, :, :], lg[:, :, :], bc(z[:, :]), ALU.mult))
                v.wait_ge(s["e_ld"], 48)
                G = lg
                for k in range(2):
                    chain(v.tensor_reduce(m[:, k, :], G[:, :, :], AX.X, ALU.max))
                    chain(v.tensor_tensor(tmp[:, :, :], G[:, :, :], bc(m[:, k, :]), ALU.is_equal))
                    chain(v.tensor_tensor(tmp[:, :, :], tmp[:, :, :], desc[:, None, :].broadcast_to([P, NT, E]), ALU.mult))
                    chain(v.tensor_reduce(z[:, :], tmp[:, :, :], AX.X, ALU.max))
                    v.tensor_tensor(oh[:, k, :, :], tmp[:, :, :], bc(z[:, :]), ALU.is_equal).then_inc(s["e_oh"], 1)
                    if k == 0:
                        v.wait_ge(s["e_oh"], 1)
                        chain(v.scalar_tensor_tensor(out=g2[:, :, :], in0=oh[:, 0, :, :], scalar=-2.0, in1=lg[:, :, :],
                                                     op0=ALU.mult, op1=ALU.add))
                        G = g2
                v.wait_ge(s["e_cnt"], 1)
                chain(v.tensor_copy(tot[:, :, :], ps[4][:, 0:2 * NT * E].rearrange("p (t e) -> p t e", e=E)))
                for e in range(E):
                    ins = v.tensor_tensor_scan(run_[:, :, e], ones[:, 0:2 * NT], tot[:, :, e], 0.0, ALU.mult, ALU.add)
                chain(ins)
                chain(v.tensor_tensor(run_[:, :, :], run_[:, :, :], tot[:, :, :], ALU.subtract))
                chain(v.tensor_tensor(run_[:, :, :], run_[:, :, :],
                                      ps[3][:, 0:2 * NT * E].rearrange("p (t e) -> p t e", e=E), ALU.add))
                o = oh[:, :, :, :].rearrange("p k t e -> p (k t) e")
                chain(v.scalar_tensor_tensor(out=run_[:, :, :], in0=run_[:, :, :], scalar=float(C), in1=o,
                                             op0=ALU.is_lt, op1=ALU.mult))
                for k in range(2):
                    ins = v.tensor_tensor(tot[:, k * NT:(k + 1) * NT, :], run_[:, k * NT:(k + 1) * NT, :],
                                          bc(m[:, k, :]), ALU.mult)
                chain(ins)
                v.tensor_tensor(cw[:, :, :].rearrange("p e t -> p t e"), tot[:, 0:NT, :], tot[:, NT:2 * NT, :], ALU.add)
        nc.all_engine_barrier(sems_to_clear=s["numbers"])

        cwe = sb("combine_w_pair", [P, 2, NT])
        with nc.Fori(0, E // 2) as pair:
            with nc.Block() as block:
                @block.sync
                def _(sp):
                    load_expert(sp, pair * 2 + 1, 1, s["e_ld"])
                    sp.wait_ge(s["e_acc"], B * TB)
                    load_expert(sp, (pair * 2 + 2) % E, 0, s["e_ahead"])
                    sp.wait_ge(s["e_ahead"], 64)

                @block.tensor
                def _(t):
                    def up(i):
                        x, b = divmod(i, B)
                        if i == B:
                            t.wait_ge(s["e_ld"], 64)
                        for n in range(NH):
                            k = NH * i + n
                            if k >= 4:
                                t.wait_ge(s["e_he"], k - 3)
                            t.matmul(ps[k % 4][:, :], w1[:, x, n, :],
                                     XT[:, TB * b:TB * b + TB, :].rearrange("p c n -> p (c n)"),
                                     start=True, stop=True).then_inc(s["e_h"], 1)

                    def down(i):
                        x, b = divmod(i, B)
                        if i >= 2:
                            t.wait_ge(s["e_acc"], TB * (i - 1))
                        for c in range(TB):
                            y = ps[4 + i % 2][:, c * P:(c + 1) * P]
                            for n in range(NH):
                                if c == 0:
                                    t.wait_ge(s["e_he"], NH * i + n + 1)
                                ins = t.matmul(y, hT[:, i % 2, n, c * P:(c + 1) * P], w2[:, x, n, :], start=(n == 0),
                                               stop=(n == NH - 1))
                            ins.then_inc(s["e_y"], 1)

                    up(0)
                    for i in range(2 * B):
                        if i + 1 < 2 * B:
                            up(i + 1)
                        down(i)

                @block.scalar
                def _(a):
                    for k in range(NH * 2 * B):
                        i, n = divmod(k, NH)
                        if i == B and n == 0:
                            a.wait_ge(s["e_ld"], 64)
                        a.wait_ge(s["e_h"], k + 1)
                        if i >= 2:
                            a.wait_ge(s["e_y"], TB * (i - 1))
                        a.activation(hT[:, i % 2, n, :], ps[k % 4][:, :], ACT.Gelu, bias=b1[:, i // B, n:n + 1])\
                            .then_inc(s["e_he"], 1)

                @block.vector
                def _(v):
                    v.tensor_copy(cwe[:, :, :], cw[:, bass.ds(pair * 2, 2), :]).then_inc(s["e_w"], 1)
                    v.wait_ge(s["e_w"], 1)
                    for k in range(2 * NT):
                        x, c = divmod(k, NT)
                        if x:
                            v.wait_ge(s["e_acc"], c + 1)
                        if k == NT:
                            v.wait_ge(s["e_ld"], 64)
                        v.scalar_tensor_tensor(out=acc[:, c, :], in0=b2[:, x, :], scalar=cwe[:, x, c:c + 1],
                                               in1=acc[:, c, :], op0=ALU.mult, op1=ALU.add).then_inc(s["e_bias"], 1)
                        v.wait_ge(s["e_y"], TB * (k // TB + 1))
                        v.wait_ge(s["e_bias"], k + 1)
                        v.scalar_tensor_tensor(out=acc[:, c, :],
                                               in0=ps[4 + (k // TB) % 2][:, (c % TB) * P:(c % TB + 1) * P],
                                               scalar=cwe[:, x, c:c + 1], in1=acc[:, c, :],
                                               op0=ALU.mult, op1=ALU.add).then_inc(s["e_acc"], 1)
            nc.all_engine_barrier(sems_to_clear=s["numbers"])
        with nc.Block() as block:
            finish_layer_norm(block, X, acc, XT, st, mv, sd, rs, NT, env, s["e_chain"], s["e_var"], s["e_sd"], s["e_done"])
        nc.all_engine_barrier(sems_to_clear=s["numbers"])


def load_late(nc, env, ctx):
    d = env.d
    env.w = {}
    with ExitStack() as inner:
        s = semaphores(nc, inner, "late_loaded")
        with nc.Block() as block:
            @block.sync
            def _(sp):
                names = ("la_w", "la_e", "la_wo", "la_mask", "gm_w", "gm_cols", "gm_row",
                         "sm_gate", "sm_w1", "sm_w2", "sa_w", "sa_wo", "sa_desc", "sa_heads", "sl_w", "sl_cols")
                for name in names:
                    shape = list(d[name].shape)
                    env.w[name] = ctx.enter_context(nc.sbuf_tensor(name, shape, F32))
                    at = tuple(slice(None) for _ in shape)
                    sp.dma_start(env.w[name][at], d[name]).then_inc(s["late_loaded"], 16)
                sp.wait_ge(s["late_loaded"], 16 * len(names))
        nc.all_engine_barrier(sems_to_clear=s["numbers"])
    env.sa_counting = ctx.enter_context(nc.sbuf_tensor("sa_counting16", [P, 5, P], BF16))
    env.la_sel16 = ctx.enter_context(nc.sbuf_tensor("la_sel16", [6 * H, 2, P], BF16))
    with ExitStack() as inner:
        sel = inner.enter_context(nc.sbuf_tensor("la_sel", [6 * H, 2, P], F32))
        counting = inner.enter_context(nc.sbuf_tensor("sa_counting", [P, 5, P], F32))
        s = semaphores(nc, inner, "counting_loaded")
        with nc.Block() as block:
            @block.sync
            def _(sp):
                sp.dma_start(counting[:, :, :], d["sa_counting"]).then_inc(s["counting_loaded"], 16)
                sp.dma_start(sel[:, :, :], d["la_sel"]).then_inc(s["counting_loaded"], 16)

            @block.vector
            def _(v):
                v.wait_ge(s["counting_loaded"], 32)
                v.tensor_copy(env.la_sel16[:, :, :], sel[:, :, :])
                v.tensor_copy(env.sa_counting[:, :, :], counting[:, :, :])
        nc.all_engine_barrier(sems_to_clear=s["numbers"])


def load_experts(sp, env, b, sem):
    d, group = env.d, b % 2
    for dst, src in ((env.gm1, "gm_w1"), (env.gm2, "gm_w2"), (env.gmb, "gm_b")):
        at = tuple(slice(None) for _ in dst.shape)
        n = d[src][(bass.ds(group, 1),) + at]
        n = n.rearrange("o p a b c -> p (o a) b c") if len(n.shape) == 5 else n.rearrange("o p a b -> p (o a) b")
        sp.dma_start(dst[at], n).then_inc(sem, 16)


LIGHTNING_CONSTANTS = ("lt_decay", "lt_rope", "lt_wq", "lt_wk", "lt_wv", "lt_wo")


def place_early_weights(nc, env, ctx):
    sb = lambda n, s: ctx.enter_context(nc.sbuf_tensor(n, s, F32))
    env.gm1 = sb("gm_w1", [P, TB, 4, P])
    env.gm2 = sb("gm_w2", [P, TB, 4, P])
    env.gmb = sb("gm_b", [P, TB, 5])
    for name in LIGHTNING_CONSTANTS:
        env.w[name] = ctx.enter_context(nc.sbuf_tensor(name, list(env.d[name].shape), F32))


def local_attention(nc, env, w, b):
    WIN = 32
    RG = P // H
    NG = WIN // RG
    TG = 2
    NT2 = WIN // TG
    TR = 3 * TG * H
    X, XT, ps = w.X, w.XT, w.ps
    W, Ec, Wo, msk = (env.w[n] for n in ("la_w", "la_e", "la_wo", "la_mask"))
    sel, ident16 = env.la_sel16, env.sa_counting[:, 4, :]
    scale = HD ** -0.5
    with ExitStack() as ctx:
        sb = lambda n, s, t=F32: ctx.enter_context(nc.sbuf_tensor("la_" + n, s, t))
        qt = sb("q_t", [P, S])
        kp = sb("k_padded", [P, WIN + S])
        vp = sb("v_padded", [P, WIN + S])
        hm = sb("head_mask_between_zeros", [P, (2 * RG - 1) * H])
        pr = sb("products", [P, 6, S])
        sT = sb("scores_t", [P, 2, S])
        D = sb("weights", [P, TB, WIN, H])
        D3 = sb("weights_parts", [P, TB, NT2, 3, TG * H], BF16)
        mx = sb("max", [P, TB, H])
        zs = sb("sum", [P, TB, H])
        pt = sb("weights_t", [TR, 2, S], BF16)
        yt = sb("y_t", [P, S])
        s = semaphores(nc, ctx, LN_SEMS + "proj q pr sc st ts dd ex pn part left hm pt pte bc pv two yt yte y ld")
        psA, psS = ps[4:6], ps[0:4]
        psB, psT, psYT, psY = ps[0:3], ps[4:6], ps[3], ps[6]
        with nc.Block() as block:
            @block.sync
            def _(sp):
                load_experts(sp, env, b, s["ld"])
                for name in LIGHTNING_CONSTANTS:
                    at = tuple(slice(None) for _ in env.w[name].shape)
                    sp.dma_start(env.w[name][at], env.d[name]).then_inc(s["ld"], 16)
                sp.wait_ge(s["ld"], 48 + 16 * len(LIGHTNING_CONSTANTS))

            @block.tensor
            def _(t):
                for m in range(3):
                    t.matmul(ps[m][:, :], W[:, m * P:(m + 1) * P], XT[:, :], start=True, stop=True).then_inc(s["proj"], 1)

                def turn_scores(g):
                    t.wait_ge(s["st"], g + 1)
                    for c in range(TB):
                        ins = t.transpose(psS[c][:, g * P:(g + 1) * P], sT[:, g % 2, c * P:(c + 1) * P], env.ident[:, :])
                    ins.then_inc(s["ts"], 1)

                t.wait_ge(s["q"], 3)
                t.wait_ge(s["hm"], 1)
                for r in range(WIN):
                    g, i = divmod(r, RG)
                    if i == 0 and g >= 2:
                        t.wait_ge(s["st"], g - 1)
                    t.wait_ge(s["pr"], r + 1)
                    t.matmul(psA[g % 2][:, :], hm[:, (RG - 1 - i) * H:(2 * RG - 1 - i) * H], pr[:, r % 4, :],
                             start=(i == 0), stop=(i == RG - 1)).then_inc(s["sc"], 1)
                    if i == 1 and g >= 1:
                        turn_scores(g - 1)
                turn_scores(NG - 1)

                def turn_weights(g):
                    if g >= 2:
                        t.wait_ge(s["pte"], g - 1)
                    for c in range(TB):
                        if g == 0:
                            t.wait_ge(s["part"], 2 * TB + c + 1)
                        ins = t.matmul(psT[g % 2][0:TR, c * P:(c + 1) * P],
                                       D3[:, c, g, :, :].rearrange("p a r -> p (a r)"), ident16, start=True, stop=True)
                    ins.then_inc(s["pt"], 1)

                turn_weights(0)
                for g in range(NT2 + 2):
                    if g < NT2:
                        t.wait_ge(s["pte"], g + 1)
                        for r in (TG * g, TG * g + 1):
                            if r >= 3:
                                t.wait_ge(s["pv"], r - 2)
                            t.matmul(psB[r % 3][:, :], sel[0:TR, r % TG, :], pt[0:TR, g % 2, :], start=True, stop=True)\
                                .then_inc(s["bc"], 1)
                    if g + 1 < NT2:
                        turn_weights(g + 1)
                    if g >= 2:
                        t.wait_ge(s["two"], g - 1)
                        t.matmul(psYT[:, :], Wo[:, :], pr[:, TG * (g - 2) % 6, :], start=(g == 2), stop=(g == NT2 + 1))\
                            .then_inc(s["yt"], 1)
                t.wait_ge(s["yte"], 1)
                for c in range(TB):
                    ins = t.transpose(psY[:, c * P:(c + 1) * P], yt[:, c * P:(c + 1) * P], env.ident[:, :])
                ins.then_inc(s["y"], 1)
                turn_tokens(t, s, X, ps[0:2], env.ident)

            @block.scalar
            def _(a):
                for m, dst in enumerate((qt[:, :], kp[:, WIN:], vp[:, WIN:])):
                    a.wait_ge(s["proj"], m + 1)
                    a.activation(dst, ps[m][:, :], ACT.Copy).then_inc(s["q"], 1)
                for g in range(NG):
                    a.wait_ge(s["sc"], RG * (g + 1))
                    if g >= 2:
                        a.wait_ge(s["ts"], g - 1)
                    a.activation(sT[:, g % 2, :], psA[g % 2][:, :], ACT.Copy).then_inc(s["st"], 1)
                for c in range(TB):
                    a.wait_ge(s["dd"], c + 1)
                    a.activation(D[:, c, :, :], D[:, c, :, :], ACT.Exp, scale=scale).then_inc(s["ex"], 1)
                for i in range(3):
                    for c in range(TB):
                        a.wait_ge(s["pn"], c + 1)
                        if i:
                            a.wait_ge(s["left"], (i - 1) * TB + c + 1)
                        a.activation(D3[:, c, :, i, :], D[:, c, :, :].rearrange("p (g r) h -> p g (r h)", r=TG),
                                     ACT.Copy).then_inc(s["part"], 1)
                for g in range(NT2):
                    a.wait_ge(s["pt"], g + 1)
                    if g >= 2:
                        a.wait_ge(s["bc"], TG * (g - 1))
                    a.activation(pt[0:TR, g % 2, :], psT[g % 2][0:TR, :], ACT.Copy).then_inc(s["pte"], 1)
                a.wait_ge(s["yt"], NT2)
                a.activation(yt[:, :], psYT[:, :], ACT.Copy).then_inc(s["yte"], 1)
                std_and_turn(a, s, w, XT, ps[0:2], env.eps, ACT.Gelu)

            @block.gpsimd
            def _(g):
                g.memset(kp[:, 0:WIN], 0.0)
                g.memset(vp[:, 0:WIN], 0.0)
                g.memset(hm[:, 0:(RG - 1) * H], 0.0)
                g.memset(hm[:, RG * H:], 0.0)
                g.tensor_copy(hm[:, (RG - 1) * H:RG * H], env.head_mask[:, :]).then_inc(s["hm"], 1)
                for r in range(0, WIN, TG):
                    g.wait_ge(s["pv"], r + TG)
                    g.tensor_tensor(pr[:, r % 6, :], pr[:, r % 6, :], pr[:, (r + 1) % 6, :], ALU.add).then_inc(s["two"], 1)

            @block.vector
            def _(v):
                chain = Chain(v, s["chain"])
                v.wait_ge(s["q"], 2)
                v.wait_ge(s["hm"], 1)
                for r in range(WIN):
                    if r >= 4:
                        v.wait_ge(s["sc"], r - 3)
                    v.scalar_tensor_tensor(out=pr[:, r % 4, :], in0=kp[:, r + 1:r + 1 + S], scalar=Ec[:, r:r + 1],
                                           in1=qt[:, :], op0=ALU.add, op1=ALU.mult).then_inc(s["pr"], 1)
                v.wait_ge(s["ts"], NG)
                for c in range(TB):
                    src = psS[c][:, :].rearrange("p (r h) -> p r h", h=H)
                    if c == 0:
                        chain(v.tensor_tensor(D[:, 0, :, :], src, msk[:, :, None].broadcast_to([P, WIN, H]), ALU.add))
                        src = D[:, 0, :, :]
                    chain(v.tensor_reduce(mx[:, c, :], src.rearrange("p r h -> p h r"), AX.X, ALU.max))
                    v.tensor_tensor(D[:, c, :, :], src, mx[:, c, None, :].broadcast_to([P, WIN, H]), ALU.subtract)\
                        .then_inc(s["dd"], 1)
                for c in range(TB):
                    v.wait_ge(s["ex"], c + 1)
                    chain(v.tensor_reduce(zs[:, c, :], D[:, c, :, :].rearrange("p r h -> p h r"), AX.X, ALU.add))
                    chain(v.reciprocal(zs[:, c, :], zs[:, c, :]))
                    v.tensor_tensor(D[:, c, :, :], D[:, c, :, :], zs[:, c, None, :].broadcast_to([P, WIN, H]),
                                    ALU.mult).then_inc(s["pn"], 1)
                for i in range(2):
                    for c in range(TB):
                        v.wait_ge(s["part"], i * TB + c + 1)
                        x = D[:, c, :, :].rearrange("p (g r) h -> p g (r h)", r=TG)
                        v.tensor_tensor(x, x, D3[:, c, :, i, :], ALU.subtract).then_inc(s["left"], 1)
                v.wait_ge(s["q"], 3)
                for r in range(WIN):
                    v.wait_ge(s["bc"], r + 1)
                    if r >= 6:
                        v.wait_ge(s["yt"], r // TG - 2)
                    v.tensor_tensor(pr[:, r % 6, :], psB[r % 3][:, :], vp[:, r + 1:r + 1 + S], ALU.mult).then_inc(s["pv"], 1)
                v.wait_ge(s["y"], 1)
                normalise(v, chain, s, w, psY, X)
        nc.all_engine_barrier(sems_to_clear=s["numbers"])


def context_mlp(nc, env, w, b):
    X, XT, ps = w.X, w.XT, w.ps
    with ExitStack() as ctx:
        g = ctx.enter_context(nc.sbuf_tensor("cm_gelu", [SK, S], F32))
        s = semaphores(nc, ctx, LN_SEMS + "h g gh y")
        with nc.Block() as block:
            @block.tensor
            def _(t):
                t.matmul(ps[1][0:SK, :], w.ctxT[:, :], XT[:, :], start=True, stop=True).then_inc(s["h"], 1)
                t.wait_ge(s["gh"], 1)
                for c in range(TB):
                    ins = t.matmul(ps[2][:, c * P:(c + 1) * P], g[:, c * P:(c + 1) * P], w.ctx[:, :], start=True, stop=True)
                ins.then_inc(s["y"], 1)
                turn_tokens(t, s, X, ps[0:2], env.ident)

            @block.scalar
            def _(a):
                a.wait_ge(s["h"], 1)
                a.activation(g[:, :], ps[1][0:SK, :], ACT.Gelu).then_inc(s["g"], 1)
                std_and_turn(a, s, w, XT, ps[0:2], env.eps, ACT.Copy)

            @block.vector
            def _(v):
                chain = Chain(v, s["chain"])
                v.wait_ge(s["g"], 1)
                v.tensor_tensor(g[:, :], ps[1][0:SK, :], g[:, :], ALU.mult).then_inc(s["gh"], 1)
                v.wait_ge(s["y"], 1)
                normalise(v, chain, s, w, ps[2], X)
        nc.all_engine_barrier(sems_to_clear=s["numbers"])


def grouped_mlp(nc, env, w, b):
    NH = 4
    X, XT, ps = w.X, w.XT, w.ps
    W, cols, row = env.w["gm_w"], env.w["gm_cols"], env.w["gm_row"]
    with ExitStack() as ctx:
        sb = lambda n, s: ctx.enter_context(nc.sbuf_tensor("gm_" + n, s, F32))
        xn = sb("xn_t", [P, S])
        xa = sb("x_attn_t", [P, S])
        hT = sb("h_t", [P, TB, NH, P])
        eo = sb("eo_t", [P, TB, P])
        y = sb("y", [P, TB, P])
        s = semaphores(nc, ctx, LN_SEMS + "var0 sd0 xh xt xnt at xa h he e ee y ye")
        psE, psN = ps[6], ps[7]
        with nc.Block() as block:
            @block.tensor
            def _(t):
                for c in range(TB):
                    t.wait_ge(s["xh"], c + 1)
                    ins = t.transpose(ps[0][:, c * P:(c + 1) * P], w.R[:, c, :], env.ident[:, :])
                ins.then_inc(s["xt"], 1)
                t.wait_ge(s["xnt"], 1)
                t.matmul(ps[1][:, :], W[:, 0, :], xn[:, :], start=True, stop=True).then_inc(s["at"], 1)
                t.wait_ge(s["xa"], 1)
                for c in range(TB):
                    for n in range(NH):
                        ins = t.matmul(ps[2 + c][:, n * P:(n + 1) * P], env.gm1[:, c, n, :], xa[:, c * P:(c + 1) * P],
                                       start=True, stop=True)
                    ins.then_inc(s["h"], 1)
                for c in range(TB):
                    for n in range(NH):
                        t.wait_ge(s["he"], NH * c + n + 1)
                        ins = t.matmul(psE[:, c * P:(c + 1) * P], env.gm2[:, c, n, :], hT[:, c, n, :],
                                       start=(n == 0), stop=(n == NH - 1))
                ins.then_inc(s["e"], 1)
                for c in range(TB):
                    t.wait_ge(s["ee"], c + 1)
                    t.matmul(psN[:, c * P:(c + 1) * P], eo[:, c, :], W[:, 1, :], start=True, stop=False)
                    ins = t.matmul(psN[:, c * P:(c + 1) * P], env.one_row[0:1, :], row[0:1, :], start=False, stop=True)
                ins.then_inc(s["y"], 1)
                turn_tokens(t, s, X, ps[0:2], env.ident)

            @block.scalar
            def _(a):
                a.wait_ge(s["var0"], 1)
                a.activation(w.sd[:, :], w.mv[:, :, 1], ACT.Sqrt, bias=env.eps[:, 0:1]).then_inc(s["sd0"], 1)
                a.wait_ge(s["xt"], 1)
                a.activation(xn[:, :], ps[0][:, :], ACT.Identity, scale=cols[:, 0:1], bias=cols[:, 1:2]).then_inc(s["xnt"], 1)
                for c in range(TB):
                    a.wait_ge(s["h"], c + 1)
                    for n in range(NH):
                        a.activation(hT[:, c, n, :], ps[2 + c][:, n * P:(n + 1) * P], ACT.Gelu,
                                     bias=env.gmb[:, c, n:n + 1]).then_inc(s["he"], 1)
                a.wait_ge(s["y"], 1)
                a.activation(y[:, :, :], psN[:, :].rearrange("p (c n) -> p c n", c=TB), ACT.Gelu).then_inc(s["ye"], 1)
                std_and_turn(a, s, w, XT, ps[0:2], env.eps, ACT.Silu)

            @block.vector
            def _(v):
                chain = Chain(v, s["chain"])
                layer_norm_stats(v, chain, X, w.st, w.mv, TB, s["var0"])
                v.wait_ge(s["sd0"], 1)
                chain(v.reciprocal(w.rs[:, :], w.sd[:, :]))
                for c in range(TB):
                    v.tensor_scalar(w.R[:, c, :], X[:, c, :], w.mv[:, c, 0:1], w.rs[:, c:c + 1],
                                    ALU.subtract, ALU.mult).then_inc(s["xh"], 1)
                v.wait_ge(s["at"], 1)
                v.scalar_tensor_tensor(out=xa[:, :], in0=ps[1][:, :], scalar=cols[:, 2:3], in1=XT[:, :],
                                       op0=ALU.add, op1=ALU.add).then_inc(s["xa"], 1)
                v.wait_ge(s["e"], 1)
                for c in range(TB):
                    v.tensor_scalar(eo[:, c, :], psE[:, c * P:(c + 1) * P], env.gmb[:, c, NH:NH + 1], None, ALU.add)\
                        .then_inc(s["ee"], 1)
                v.wait_ge(s["ye"], 1)
                normalise(v, chain, s, w, y, X)
        nc.all_engine_barrier(sems_to_clear=s["numbers"])


def lightning(nc, env, w, b):
    HQ, KV, W2 = 16, 4, 64
    NQ, NK = HQ * W2 // P, KV * W2 // P
    X, XT, ps = w.X, w.XT, w.ps
    wq, wk, wv, wo, rope, decay = (env.w["lt_" + n] for n in ("wq", "wk", "wv", "wo", "rope", "decay"))
    with ExitStack() as ctx:
        sb = lambda n, s: ctx.enter_context(nc.sbuf_tensor("lt_" + n, s, F32))
        qk = sb("q_k_t", [P, NQ + NK, S])
        tmp = sb("rope_tmp", [P, 2, 2, S])
        vv = sb("v", [P, TB, KV * W2])
        pd = sb("decayed", [P, 4, S])
        ot = sb("o_t", [P, 2, S])
        s = semaphores(nc, ctx, LN_SEMS + "vp ve pj r1 qk sc pd av oe y")
        NC_ = NQ + NK
        pair = lambda i: (ps[2 * (i % 2)], ps[2 * (i % 2) + 1])
        psO, psY = ps[4:6], ps[7]
        items = [(m, r, j) for m in range(NQ) for r in range(2) for j in range(TB)]
        with nc.Block() as block:
            @block.tensor
            def _(t):
                for c in range(TB):
                    ins = t.matmul(ps[4 + c // 2][:, (c % 2) * 256:(c % 2 + 1) * 256], XT[:, c * P:(c + 1) * P], wv[:, :],
                                   start=True, stop=True)
                ins.then_inc(s["vp"], 1)
                for i in range(NC_):
                    if i >= 2:
                        t.wait_ge(s["r1"], 2 * (i - 1))
                    wt, m = (wk, i) if i < NK else (wq, i - NK)
                    for x in range(2):
                        t.matmul(pair(i)[x][:, :], wt[:, x, m, :], XT[:, :], start=True, stop=True).then_inc(s["pj"], 1)
                t.wait_ge(s["r1"], 2 * NC_)
                t.wait_ge(s["ve"], 2)

                def score(i):
                    m, r, j = items[i]
                    if i >= 4:
                        t.wait_ge(s["pd"], i - 3)
                    t.wait_ge(s["qk"], NK + m + 1)
                    rows = slice(W2 * r, W2 * r + W2)
                    t.matmul(ps[i % 4][:, j * P:S], qk[rows, m // 4, j * P:(j + 1) * P], qk[rows, NK + m, j * P:S],
                             start=True, stop=True).then_inc(s["sc"], 1)

                def weigh(i):
                    m, r, j = items[i]
                    t.wait_ge(s["pd"], i + 1)
                    if m >= 2 and r == 0 and j == 0:
                        t.wait_ge(s["oe"], m - 1)
                    kv = 2 * (m // 4) + r
                    t.matmul(psO[m % 2][W2 * r:W2 * r + W2, j * P:S], vv[:, j, kv * W2:(kv + 1) * W2], pd[:, i % 4, j * P:S],
                             start=(j == 0), stop=(j == TB - 1), skip_group_check=True).then_inc(s["av"], 1)

                def out(m):
                    t.wait_ge(s["oe"], m + 1)
                    for c in range(TB):
                        ins = t.matmul(psY[:, c * P:(c + 1) * P], ot[:, m % 2, c * P:(c + 1) * P], wo[:, m, :],
                                       start=(m == 0 and c == 0), stop=(m == NQ - 1), skip_group_check=True)
                    ins.then_inc(s["y"], 1)

                N = len(items)
                for i in range(N + 2):
                    if i < N:
                        score(i)
                    if i >= 2:
                        weigh(i - 2)
                    if i % 8 == 3 and i >= 11:
                        out((i - 11) // 8)
                out(NQ - 1)
                turn_tokens(t, s, X, ps[0:2], env.ident)

            @block.scalar
            def _(a):
                a.wait_ge(s["vp"], 1)
                for x in range(2):
                    a.activation(vv[:, 2 * x:2 * x + 2, :], ps[4 + x][:, :].rearrange("p (c n) -> p c n", c=2), ACT.Copy)\
                        .then_inc(s["ve"], 1)
                for m in range(NQ):
                    a.wait_ge(s["av"], 8 * (m + 1))
                    if m >= 2:
                        a.wait_ge(s["y"], m - 1)
                    a.activation(ot[:, m % 2, :], psO[m % 2][:, :], ACT.Copy).then_inc(s["oe"], 1)
                std_and_turn(a, s, w, XT, ps[0:2], env.eps, ACT.Exp)

            @block.gpsimd
            def _(g):
                for i in range(NC_):
                    g.wait_ge(s["r1"], 2 * (i + 1))
                    g.tensor_tensor(qk[:, i, :], tmp[:, i % 2, 0, :], tmp[:, i % 2, 1, :], ALU.add).then_inc(s["qk"], 1)

            @block.vector
            def _(v):
                chain = Chain(v, s["chain"])
                for i in range(NC_):
                    if i >= 2:
                        v.wait_ge(s["qk"], i - 1)
                    for x in range(2):
                        v.wait_ge(s["pj"], 2 * i + x + 1)
                        v.tensor_tensor(tmp[:, i % 2, x, :], pair(i)[x][:, :], rope[:, x, :], ALU.mult).then_inc(s["r1"], 1)
                for i, (m, r, j) in enumerate(items):
                    h = 8 * (m // 4) + 4 * r + m % 4
                    v.wait_ge(s["sc"], i + 1)
                    if i >= 4:
                        v.wait_ge(s["av"], i - 3)
                    v.tensor_tensor(pd[:, i % 4, j * P:S], ps[i % 4][:, j * P:S], decay[:, h, 0:S - j * P], ALU.mult)\
                        .then_inc(s["pd"], 1)
                v.wait_ge(s["y"], NQ)
                normalise(v, chain, s, w, psY, X)
        nc.all_engine_barrier(sems_to_clear=s["numbers"])


def shared_moe(nc, env, w, b):
    E, NH = 8, 4
    X, XT, ps = w.X, w.XT, w.ps
    wg, w1, w2 = env.w["sm_gate"], env.w["sm_w1"], env.w["sm_w2"]
    with ExitStack() as ctx:
        sb = lambda n, s: ctx.enter_context(nc.sbuf_tensor("sm_" + n, s, F32))
        lg = sb("gates", [P, TB, E])
        top = sb("top", [P, TB, E])
        z = sb("z", [P, TB])
        dn = sb("denom", [P, TB])
        hT = sb("h_t", [P, NH, S])
        y = sb("y", [P, TB, P])
        s = semaphores(nc, ctx, LN_SEMS + "lg sub ex h he y")
        with nc.Block() as block:
            @block.tensor
            def _(t):
                for c in range(TB):
                    ins = t.matmul(ps[1][:, c * E:(c + 1) * E], XT[:, c * P:(c + 1) * P], wg[:, :], start=True, stop=True)
                ins.then_inc(s["lg"], 1)
                for n in range(NH):
                    t.matmul(ps[2 + n][:, :], w1[:, n, :], XT[:, :], start=True, stop=True).then_inc(s["h"], 1)
                for c in range(TB):
                    for n in range(NH):
                        t.wait_ge(s["he"], n + 1)
                        ins = t.matmul(ps[6][:, c * P:(c + 1) * P], hT[:, n, c * P:(c + 1) * P], w2[:, n, :],
                                       start=(n == 0), stop=(n == NH - 1))
                ins.then_inc(s["y"], 1)
                turn_tokens(t, s, X, ps[0:2], env.ident)

            @block.scalar
            def _(a):
                a.wait_ge(s["sub"], 1)
                a.activation(lg[:, :, :], lg[:, :, :], ACT.Exp).then_inc(s["ex"], 1)
                for n in range(NH):
                    a.wait_ge(s["h"], n + 1)
                    a.activation(hT[:, n, :], ps[2 + n][:, :], ACT.Relu).then_inc(s["he"], 1)
                std_and_turn(a, s, w, XT, ps[0:2], env.eps, ACT.Exp)

            @block.vector
            def _(v):
                chain = Chain(v, s["chain"])
                bc = lambda a: a[:, :, None].broadcast_to([P, TB, E])
                v.wait_ge(s["lg"], 1)
                L = ps[1][:, 0:TB * E].rearrange("p (t e) -> p t e", e=E)
                chain(v.tensor_reduce(z[:, :], L, AX.X, ALU.max))
                v.tensor_tensor(lg[:, :, :], L, bc(z[:, :]), ALU.subtract).then_inc(s["sub"], 1)
                v.wait_ge(s["ex"], 1)
                chain(v.tensor_reduce(z[:, :], lg[:, :, :], AX.X, ALU.add))
                chain(v.reciprocal(z[:, :], z[:, :]))
                chain(v.tensor_tensor(lg[:, :, :], lg[:, :, :], bc(z[:, :]), ALU.mult))
                for c in range(TB):
                    ins = v.max(top[:, c, :], lg[:, c, :])
                chain(ins)
                chain(v.tensor_tensor(dn[:, :], top[:, :, 0], top[:, :, 1], ALU.add))
                chain(v.tensor_scalar(dn[:, :], dn[:, :], 1.1920929e-07, None, ALU.max))
                chain(v.reciprocal(dn[:, :], dn[:, :]))
                chain(v.tensor_tensor(top[:, :, 0:2], top[:, :, 0:2], dn[:, :, None].broadcast_to([P, TB, 2]), ALU.mult))
                chain(v.tensor_tensor(z[:, :], top[:, :, 0], top[:, :, 1], ALU.add))
                v.wait_ge(s["y"], 1)
                for c in range(TB):
                    ins = v.tensor_scalar(y[:, c, :], ps[6][:, c * P:(c + 1) * P], z[:, c:c + 1], None, ALU.mult)
                chain(ins)
                normalise(v, chain, s, w, y, X)
        nc.all_engine_barrier(sems_to_clear=s["numbers"])


def sparse_attention(nc, env, w, b):
    KEEP = 64
    FROM = 12
    LOWEST = -3e38
    NONE, MASKED = -2048.0, -1e32
    G3 = 3 * H
    GH = 4
    GR = GH * (HD + 1)
    NR = 3 * HD
    X, XT, ps = w.X, w.XT, w.ps
    W, Wo, desc = (env.w["sa_" + n] for n in ("w", "wo", "desc"))
    own_ge, own_gt, all_before, mask, ident16 = (env.sa_counting[:, i, :] for i in range(5))
    scr = env.scratch
    scale = HD ** -0.5
    SLOTS = [[(0, 0, 0)], [(0, 1, 0), (0, 3, 3 * P)], [(0, 2, 0), (1, 2, 2 * P)], [(1, 0, 0)], [(1, 1, 0), (1, 3, 3 * P)]]
    NS, PAIRS = len(SLOTS), H // 2
    N = NS * PAIRS
    place = {(hh, jt): (sl, col) for sl, parts in enumerate(SLOTS) for hh, jt, col in parts}
    width = lambda jt: (TB - jt) * P
    with ExitStack() as ctx:
        sb = lambda n, s, t=F32: ctx.enter_context(nc.sbuf_tensor("sa_" + n, s, t))
        kst = sb("k_stack", [4 * NR, H, S], BF16)
        qst = sb("q_stack", [4 * NR, H, S], BF16)
        ex = sb("exp", [P, PAIRS, NS, S])
        qt = sb("q_t", [P, S])
        qs = sb("q_sign", [P, S], BF16)
        rp = sb("threshold_parts", [P, 3, S], BF16)
        v1 = sb("v_and_one", [P, TB, H, HD + 1])
        zr = sb("one_over_sum", [P, TB, H])
        with ExitStack() as early:
            sb = lambda n, s, t=F32: early.enter_context(nc.sbuf_tensor("sa_" + n, s, t))
            qkv = sb("qkv", [P, TB, 3 * P])
            ab = sb("abs", [P, 2, 3 * P])
            m = sb("feature_max", [P, 2, G3])
            L = sb("level", [P, 2, 2, S], F16)
            mk = sb("minus_k_t", [P, S])
            kap = sb("k_of_head", [P, TB, H])
            sg0 = sb("below_zero", [P, TB, H], BF16)
            rk = sb("rank", [P, TB, H])
            one16 = sb("ones_row", [P, S], BF16)
            low = sb("none_row", [P, S], BF16)
            hd16 = sb("rows_of_head", [P, H], BF16)
            junk = sb("compared", [P, 2, 2, S], BF16)
            kh = sb("k_rank", [P, TB, P], F16)
            krt = sb("k_rank_t", [P, S])
            id16 = sb("plus_minus_identity", [P, 2, P], F16)
            M = sb("running_max", [P, 2, S])
            kt = sb("k_t", [P, S])
            tmp = sb("tmp", [P, 2, S])
            thr = sb("minus_threshold", [P, 2, S])
            kp = sb("k_parts", [P, 3, S], BF16)
            qp = sb("q_parts", [P, 3, S], BF16)
        sb = lambda n, s, t=F32: ctx.enter_context(nc.sbuf_tensor("sa_" + n, s, t))
        gg = sb("ge_gt", [P, 2, 2, NS, S], BF16)
        vz = sb("v_and_one_padded", [P, TB, H, GR])
        wt = sb("weighed", [GR, H // GH, S])
        o = sb("o", [P, TB, P])
        ot = sb("o_t", [P, S])
        s = semaphores(nc, ctx, LN_SEMS + "pj pje keep tk tke y0 mx ones kp qp mxp rp qs stored k_in q_in s_done exp "
                                          "ng z kr dc ac rk yi krt rkp l0 l1 p0 p1 d cmp cnt sel vz pv wt tt on ott ote y pc")
        psS, psD, psC, psO, psY = ps[0:2], ps[2:4], ps[4:6], ps[2], ps[3]
        psW, psB, psQ = (ps[0], ps[1], ps[6], ps[7]), ps[0:2], ps[6:8]
        with nc.Block() as block:
            @block.sync
            def _(sp):
                rows = lambda a: scr[a].rearrange("p (f h) n -> (p f) h n", h=H)
                part = lambda a, p: scr[a, p].rearrange("(f h) n -> f h n", h=H)

                def store(a, src, ready, n):
                    sp.wait_ge(s[ready], 1)
                    sp.dma_start(scr[a].rearrange("p r n -> r p n"), src[:, :, :]).then_inc(s["stored"], 16)
                    sp.wait_ge(s["stored"], 16 * n)

                store(0, kp, "kp", 1)
                for i in range(3):
                    sp.dma_start(kst[NR + i * NR:NR + (i + 1) * NR, :, :], rows(0)).then_inc(s["k_in"], 16)
                store(1, qp, "qp", 2)
                for i in range(3):
                    for j in range(3):
                        at = NR + i * NR + j * HD
                        sp.dma_start(qst[at:at + HD, :, :], part(1, i)).then_inc(s["q_in"], 16)
                store(2, kp, "mxp", 3)
                sp.dma_start(qst[0:NR, :, :], rows(2)).then_inc(s["q_in"], 16)
                sp.wait_ge(s["qs"], 1)
                sp.dma_start(scr[4, 0], qs[:, :]).then_inc(s["stored"], 16)
                sp.wait_ge(s["stored"], 64)
                store(5, qp, "rkp", 5)
                sp.wait_ge(s["s_done"], N)
                sp.dma_start(kst[NR:2 * NR, :, :], rows(5)).then_inc(s["q_in"], 16)
                for j in range(3):
                    at = NR + j * HD
                    sp.dma_start(qst[at:at + HD, :, :], part(4, 0)).then_inc(s["q_in"], 16)
                store(3, rp, "rp", 6)
                sp.dma_start(qst[0:NR, :, :], rows(3)).then_inc(s["q_in"], 16)

            @block.tensor
            def _(t):
                for c in range(TB):
                    t.matmul(ps[c][:, 0:3 * P], XT[:, c * P:(c + 1) * P], W[:, :], start=True, stop=True).then_inc(s["pj"], 1)
                for c in range(TB):
                    t.wait_ge(s["keep"], c + 1)
                    for x in range(2):
                        ins = t.transpose(ps[4 + x][:, c * P:(c + 1) * P], qkv[:, c, x * P:(x + 1) * P], env.ident[:, :])
                ins.then_inc(s["tk"], 1)

                def scores(bank, sl, pair, rows):
                    for i, (hh, jt, col) in enumerate(SLOTS[sl]):
                        h = 2 * pair + hh
                        t.matmul(bank[:, col:col + P], ident16, mask, start=(i == 0), stop=False, skip_group_check=True)
                        ins = t.matmul(bank[:, col:col + width(jt)], kst[0:rows, h, jt * P:(jt + 1) * P],
                                       qst[0:rows, h, jt * P:S], start=False, stop=True, skip_group_check=True)
                    return ins

                t.wait_ge(s["kp"], 1)
                for i in range(H // 2):
                    for x, used in enumerate(("dc", "ac")):
                        if i >= 2:
                            t.wait_ge(s[used], TB * (i - 1))
                        h = i + x * H // 2
                        for p in range(3):
                            ins = t.matmul(ps[2 * x + i % 2][:, :], hd16[:, h:h + 1].broadcast_to([P, P]), kp[:, p, :],
                                           start=(p == 0), stop=(p == 2))
                        ins.then_inc(s["kr"], 1)
                t.wait_ge(s["ng"], 1)
                for c in range(TB):
                    ins = t.matmul(ps[4][:, 0:H], all_before, sg0[:, c, :], start=(c == 0), stop=(c == TB - 1))
                ins.then_inc(s["z"], 1)
                for c in range(TB):
                    t.wait_ge(s["rk"], c + 1)
                    for x in range(2):
                        ins = t.matmul(psQ[x][:, c * P:(c + 1) * P], kh[:, c, :], id16[:, x, :], start=(c == 0),
                                       stop=(c == TB - 1), skip_group_check=True)
                ins.then_inc(s["yi"], 1)
                t.wait_ge(s["krt"], 1)

                def first_scores(k):
                    if k == 0:
                        t.wait_ge(s["pje"], TB)
                        t.wait_ge(s["ones"], 1)
                        t.wait_ge(s["k_in"], 48)
                        t.wait_ge(s["q_in"], 160)
                    if k >= 2:
                        t.wait_ge(s["exp"], k - 1)
                    scores(psS[k % 2], k % NS, k // NS, 4 * NR).then_inc(s["s_done"], 1)

                for level in range(KEEP - 1):
                    for x in range(2):
                        t.wait_ge(s["l%d" % x], level + 1)
                        held = L[:, x, level % 2, :]
                        out = psQ[x][:, level + 1:S]
                        t.matmul(out, id16[:, 0, :], held[:, level:S - 1], start=False, stop=False, skip_group_check=True)
                        t.matmul(out, id16[:, 1, :], held[:, level + 1:S], start=False, stop=True, skip_group_check=True)\
                            .then_inc(s["p%d" % x], 1)
                    if 0 <= level - FROM < N:
                        first_scores(level - FROM)

                def compare(k):
                    if k >= 2:
                        t.wait_ge(s["cmp"], k - 1)
                    scores(psD[k % 2], k % NS, k // NS, 2 * NR).then_inc(s["d"], 1)

                def count(k):
                    pair, sl = divmod(k, NS)
                    g = gg[:, pair % 2]
                    if k % NS == 0:
                        t.wait_ge(s["cmp"], k + NS)
                    if k >= 2:
                        t.wait_ge(s["sel"], k - 1)
                    bank = psC[k % 2]
                    for i, (hh, jt, col) in enumerate(SLOTS[sl]):
                        out = bank[:, col:col + width(jt)]
                        own = slice(col, col + width(jt))
                        t.matmul(out, own_ge, g[:, 0, sl, own], start=(i == 0), stop=False, skip_group_check=True)
                        for j2 in range(TB):
                            s2, c2 = place[hh, j2]
                            if j2 < jt:
                                c2 += (jt - j2) * P
                                t.matmul(out, all_before, g[:, 0, s2, c2:c2 + width(jt)], start=False, stop=False,
                                         skip_group_check=True)
                            if j2 > jt:
                                c1 = col + (j2 - jt) * P
                                t.matmul(bank[:, c1:c1 + width(j2)], all_before, g[:, 1, s2, c2:c2 + width(j2)],
                                         start=False, stop=False, skip_group_check=True)
                        ins = t.matmul(out, own_gt, g[:, 1, sl, own], start=False, stop=True, skip_group_check=True)
                    ins.then_inc(s["cnt"], 1)

                def weigh(pair, part):
                    hh, jt = divmod(part, TB)
                    h = 2 * pair + hh
                    if part == 0:
                        t.wait_ge(s["vz"], 1)
                        t.wait_ge(s["sel"], NS * (pair + 1))
                    sl, col = place[hh, jt]
                    ins = t.matmul(psW[h // GH][0:GR, jt * P:S], vz[:, jt, h, :], ex[:, pair, sl, col:col + width(jt)],
                                   start=(h % GH == 0 and jt == 0), stop=(h % GH == GH - 1 and jt == TB - 1),
                                   skip_group_check=True)
                    if part == 2 * TB - 1:
                        ins.then_inc(s["pv"], 1)

                def turn_back(g):
                    t.wait_ge(s["wt"], max(g + 1, 2))
                    for c in range(TB):
                        at = (c % 2) * H * (HD + 1) + g * GR
                        ins = t.transpose(psB[c // 2][:, at:at + GR], wt[:, g, c * P:(c + 1) * P],
                                          env.ident[0:GR, 0:GR])
                    ins.then_inc(s["tt"], 1)

                t.wait_ge(s["q_in"], 160 + 80)
                for k in range(N + NS):
                    if k < N:
                        compare(k)
                    if k >= NS:
                        count(k - NS)
                    if k // NS >= 2:
                        for part in (2 * (k % NS), 2 * (k % NS) + 1):
                            if part < 2 * TB:
                                weigh(k // NS - 2, part)
                for g in range(2):
                    turn_back(g)
                for part in range(2 * TB):
                    weigh(PAIRS - 1, part)
                for g in range(2, 4):
                    turn_back(g)
                for c in range(TB):
                    t.wait_ge(s["on"], c + 1)
                    t.transpose(psO[:, c * P:(c + 1) * P], o[:, c, :], env.ident[:, :]).then_inc(s["ott"], 1)
                t.wait_ge(s["ote"], 1)
                for c in range(TB):
                    ins = t.matmul(psY[:, c * P:(c + 1) * P], ot[:, c * P:(c + 1) * P], Wo[:, :], start=True, stop=True)
                ins.then_inc(s["y"], 1)
                turn_tokens(t, s, X, ps[0:2], env.ident)

            @block.scalar
            def _(a):
                for c in range(TB):
                    a.wait_ge(s["pj"], c + 1)
                    a.activation(qkv[:, c, :], ps[c][:, 0:3 * P], ACT.Copy).then_inc(s["pje"], 1)
                a.wait_ge(s["tk"], 1)
                a.activation(kt[:, :], ps[5][:, :], ACT.Copy).then_inc(s["tke"], 1)
                a.activation(qt[:, :], ps[4][:, :], ACT.Copy).then_inc(s["tke"], 1)
                a.activation(mk[:, :], ps[5][:, :], ACT.Copy, scale=-1.0).then_inc(s["y0"], 1)
                a.wait_ge(s["ng"], 1)
                for i in range(H // 2):
                    a.wait_ge(s["kr"], 2 * i + 2)
                    h = i + H // 2
                    for c in range(TB):
                        if TB * i + c >= 2:
                            a.wait_ge(s["ac"], TB * i + c - 1)
                        a.activation(junk[:, 1, c % 2, :], ps[2 + i % 2][:, :], ACT.Sign, scale=-1.0,
                                     bias=kap[:, c, h:h + 1], accum_out=rk[:, c, h:h + 1]).then_inc(s["ac"], 1)
                a.wait_ge(s["yi"], 1)
                a.activation(krt[:, :], psQ[0][:, :], ACT.Copy).then_inc(s["krt"], 1)
                for k in range(N):
                    a.wait_ge(s["s_done"], k + 1)
                    a.activation(ex[:, k // NS, k % NS, :], psS[k % 2][:, :], ACT.Exp, scale=scale).then_inc(s["exp"], 1)
                for g in range(H // GH):
                    a.wait_ge(s["pv"], GH // 2 * (g + 1))
                    a.activation(wt[:, g, :], psW[g][0:GR, :], ACT.Copy).then_inc(s["wt"], 1)
                a.wait_ge(s["ott"], TB)
                a.activation(ot[:, :], psO[:, :], ACT.Copy).then_inc(s["ote"], 1)
                std_and_turn(a, s, w, XT, ps[0:2], env.eps, ACT.Exp)

            @block.gpsimd
            def _(g):
                pool = Chain(g, s["pc"])
                g.memset(kst[0:NR, :, :], 1.0).then_inc(s["ones"], 1)
                g.wait_ge(s["tke"], 2)

                def split(x, parts, done):
                    for i in range(3):
                        ins = g.tensor_copy(parts[:, i, :], x)
                        if i < 2:
                            pool(ins)
                            pool(g.tensor_tensor(x, x, parts[:, i, :], ALU.subtract))
                    ins.then_inc(s[done], 1)

                pool(g.tensor_copy(tmp[:, 0, :], qt[:, :]))
                split(tmp[:, 0, :], qp, "qp")
                g.wait_ge(s["qp"], 1)
                g.wait_ge(s["mx"], 2)
                pool(g.tensor_scalar(tmp[:, 0, :], qt[:, :], 0.0, None, ALU.max))
                pool(g.tensor_tensor(tmp[:, 0, :], tmp[:, 0, :], M[:, 0, :], ALU.mult))
                pool(g.tensor_scalar(tmp[:, 1, :], qt[:, :], 0.0, None, ALU.min))
                pool(g.tensor_tensor(tmp[:, 1, :], tmp[:, 1, :], M[:, 1, :], ALU.mult))
                pool(g.tensor_tensor(tmp[:, 1, :], tmp[:, 1, :], tmp[:, 0, :], ALU.subtract))
                g.wait_ge(s["stored"], 16)
                g.wait_ge(s["kr"], H)
                split(tmp[:, 1, :], kp, "mxp")
                g.wait_ge(s["stored"], 32)
                g.wait_ge(s["krt"], 1)
                split(krt[:, :], qp, "rkp")
                g.wait_ge(s["stored"], 80)
                g.wait_ge(s["rp"], 1)
                pool(g.memset(vz[:, :, :, :], 0.0))
                for h in range(H):
                    at = (h % GH) * (HD + 1)
                    ins = g.tensor_copy(vz[:, :, h, at:at + HD + 1], v1[:, :, h, :])
                ins.then_inc(s["vz"], 1)

            @block.vector
            def _(v):
                chain = Chain(v, s["chain"])
                chain(v.memset(v1[:, :, :, :], 1.0))
                v.memset(one16[:, :], 1.0)
                v.memset(low[:, :], NONE)
                v.tensor_copy(hd16[:, :], env.w["sa_heads"][:, :])
                for x in range(2):
                    v.tensor_scalar(id16[:, x, :], env.ident[:, :], 1.0 - 2 * x, None, ALU.mult)
                for c in range(TB):
                    v.wait_ge(s["pje"], c + 1)
                    grouped = lambda x: x.rearrange("p (g f h) -> p g h f", f=HD, h=H)
                    x = grouped(qkv[:, c, :])
                    z = grouped(ab[:, c % 2, :])
                    best = m[:, c % 2, :].rearrange("p (g h) -> p g h", h=H)
                    bc = m[:, c % 2, :].rearrange("p (g h) -> p g h", h=H)[:, :, :, None].broadcast_to([P, 3, H, HD])
                    chain(v.scalar_tensor_tensor(out=ab[:, c % 2, :], in0=qkv[:, c, :], scalar=-1.0, in1=qkv[:, c, :],
                                                 op0=ALU.mult, op1=ALU.max))
                    chain(v.tensor_reduce(best, z, AX.X, ALU.max))
                    chain(v.tensor_tensor(z, z, bc, ALU.is_equal))
                    chain(v.tensor_tensor(z, z, desc[:, None, None, :].broadcast_to([P, 3, H, HD]), ALU.mult))
                    chain(v.tensor_reduce(best, z, AX.X, ALU.max))
                    chain(v.tensor_tensor(z, z, bc, ALU.is_equal))
                    v.tensor_tensor(qkv[:, c, 0:2 * P], qkv[:, c, 0:2 * P], ab[:, c % 2, 0:2 * P], ALU.mult)\
                        .then_inc(s["keep"], 1)
                    chain(v.tensor_tensor(v1[:, c, :, 0:HD], x[:, 2], z[:, 2], ALU.mult))
                    v.wait_ge(s["keep"], c + 1)
                    chain(v.tensor_reduce(kap[:, c, :], x[:, 1], AX.X, ALU.add))

                chain(v.tensor_scalar(sg0[:, :, :], kap[:, :, :], 0.0, None, ALU.is_lt))
                late = slice(H // 2, H)
                chain(v.scalar_tensor_tensor(out=sg0[:, :, late], in0=kap[:, :, late], scalar=0.0, in1=sg0[:, :, late],
                                             op0=ALU.is_gt, op1=ALU.subtract))
                v.sem_inc(s["ng"], 1)
                v.wait_ge(s["tke"], 1)
                left = kt[:, :]
                for i in range(3):
                    ins = v.tensor_copy(kp[:, i, :], left)
                    if i < 2:
                        chain(ins)
                        chain(v.tensor_tensor(tmp[:, 1, :], left, kp[:, i, :], ALU.subtract))
                        left = tmp[:, 1, :]
                ins.then_inc(s["kp"], 1)
                v.tensor_tensor_scan(M[:, 0, :], kt[:, :], kt[:, :], LOWEST, ALU.max, ALU.max).then_inc(s["mx"], 1)
                v.wait_ge(s["y0"], 1)
                v.tensor_tensor_scan(M[:, 1, :], mk[:, :], mk[:, :], LOWEST, ALU.max, ALU.max).then_inc(s["mx"], 1)
                for i in range(H // 2):
                    v.wait_ge(s["kr"], 2 * i + 1)
                    for c in range(TB):
                        if TB * i + c >= 2:
                            v.wait_ge(s["dc"], TB * i + c - 1)
                        v.scalar_tensor_tensor(out=junk[:, 0, c % 2, :], in0=ps[i % 2][:, :], scalar=kap[:, c, i:i + 1],
                                               in1=one16[:, :], op0=ALU.is_lt, op1=ALU.mult,
                                               accum_out=rk[:, c, i:i + 1]).then_inc(s["dc"], 1)
                v.wait_ge(s["z"], 1)
                v.wait_ge(s["dc"], TB * H // 2)
                v.wait_ge(s["ac"], TB * H // 2)
                half = slice(0, H // 2)
                chain(v.scalar_tensor_tensor(out=rk[:, :, half], in0=kap[:, :, half], scalar=0.0, in1=rk[:, :, half],
                                             op0=ALU.is_gt, op1=ALU.add))
                for x, op in ((0, ALU.subtract), (1, ALU.add)):
                    half = slice(x * H // 2, (x + 1) * H // 2)
                    chain(v.tensor_tensor(rk[:, :, half], rk[:, :, half], ps[4][:, None, half].broadcast_to([P, TB, H // 2]), op))
                for c in range(TB):
                    v.scalar_tensor_tensor(out=kh[:, c, :].rearrange("p (f h) -> p f h", h=H),
                                           in0=qkv[:, c, P:2 * P].rearrange("p (f h) -> p f h", h=H), scalar=0.0,
                                           in1=rk[:, c, None, :].broadcast_to([P, HD, H]), op0=ALU.not_equal,
                                           op1=ALU.mult).then_inc(s["rk"], 1)

                v.wait_ge(s["yi"], 1)
                v.wait_ge(s["krt"], 1)
                for level in range(KEEP):
                    for x in range(2):
                        if level:
                            v.wait_ge(s["p%d" % x], level)
                        came = psQ[x][:, level:S]
                        v.tensor_tensor_scan(L[:, x, level % 2, level:S], low[:, level:S], came, NONE, ALU.max, ALU.max)\
                            .then_inc(s["l%d" % x], 1)
                    if level == 1:
                        v.wait_ge(s["tke"], 2)
                        chain(v.tensor_scalar(thr[:, 0, :], qt[:, :], 0.0, None, ALU.is_lt))
                        chain(v.scalar_tensor_tensor(out=qs[:, :], in0=qt[:, :], scalar=0.0, in1=thr[:, 0, :],
                                                     op0=ALU.is_gt, op1=ALU.subtract))
                        v.sem_inc(s["qs"], 1)
                last = (KEEP - 1) % 2
                for x in range(2):
                    v.wait_ge(s["l%d" % x], KEEP)
                chain(v.memset(L[:, :, last, 0:KEEP - 1], NONE))
                chain(v.scalar_tensor_tensor(out=thr[:, 0, :], in0=qt[:, :], scalar=0.0, in1=L[:, 0, last, :],
                                             op0=ALU.is_gt, op1=ALU.mult))
                chain(v.scalar_tensor_tensor(out=thr[:, 1, :], in0=qt[:, :], scalar=0.0, in1=L[:, 1, last, :],
                                             op0=ALU.is_lt, op1=ALU.mult))
                x = thr[:, 1, :]
                chain(v.scalar_tensor_tensor(out=x, in0=thr[:, 0, :], scalar=-1.0, in1=x, op0=ALU.mult, op1=ALU.subtract))
                for i in range(3):
                    chain(v.tensor_copy(rp[:, i, :], x))
                    if i < 2:
                        chain(v.tensor_tensor(x, x, rp[:, i, :], ALU.subtract))
                v.sem_inc(s["rp"], 1)

                def against(k):
                    pair, sl = divmod(k, NS)
                    v.wait_ge(s["d"], k + 1)
                    if pair >= 2 and sl == 0:
                        v.wait_ge(s["cnt"], NS * (pair - 1))
                    v.tensor_scalar(gg[:, pair % 2, 0, sl, :], psD[k % 2][:, :], 0.0, None, ALU.is_ge)
                    v.tensor_scalar(gg[:, pair % 2, 1, sl, :], psD[k % 2][:, :], 0.0, None, ALU.is_gt).then_inc(s["cmp"], 1)

                def select(k):
                    v.wait_ge(s["cnt"], k + 1)
                    at = ex[:, k // NS, k % NS, :]
                    v.scalar_tensor_tensor(out=at, in0=psC[k % 2][:, :], scalar=KEEP - 0.5 - 1024.0, in1=at,
                                           op0=ALU.is_le, op1=ALU.mult).then_inc(s["sel"], 1)

                v.wait_ge(s["exp"], N)
                for k in range(N + NS):
                    if k < N:
                        against(k)
                    if k >= NS:
                        select(k - NS)
                v.wait_ge(s["tt"], H // GH)
                for c in range(TB):
                    n = H * (HD + 1)
                    got = psB[c // 2][:, (c % 2) * n:(c % 2 + 1) * n].rearrange("p (h n) -> p h n", h=H)
                    chain(v.reciprocal(zr[:, c, :], got[:, :, HD]))
                    v.tensor_tensor(o[:, c, :].rearrange("p (h n) -> p h n", n=HD), got[:, :, 0:HD],
                                    zr[:, c, :, None].broadcast_to([P, H, HD]), ALU.mult).then_inc(s["on"], 1)
                v.wait_ge(s["y"], 1)
                normalise(v, chain, s, w, psY, X)
        nc.all_engine_barrier(sems_to_clear=s["numbers"])


def sign_linear(nc, env, w, b):
    LIMIT = 100.0
    X, XT, ps = w.X, w.XT, w.ps
    W, cols = env.w["sl_w"], env.w["sl_cols"]
    with ExitStack() as ctx:
        sb = lambda n, s: ctx.enter_context(nc.sbuf_tensor("sl_" + n, s, F32))
        sg = sb("signs", [P, P])
        yt = sb("y_t", [P, S])
        s = semaphores(nc, ctx, LN_SEMS + "sg yt cl y")
        with nc.Block() as block:
            @block.tensor
            def _(t):
                t.wait_ge(s["sg"], 1)
                t.matmul(ps[1][:, :], sg[:, :], XT[:, :], start=True, stop=True).then_inc(s["yt"], 1)
                t.wait_ge(s["cl"], 1)
                for c in range(TB):
                    ins = t.transpose(ps[2][:, c * P:(c + 1) * P], yt[:, c * P:(c + 1) * P], env.ident[:, :])
                ins.then_inc(s["y"], 1)

            @block.scalar
            def _(a):
                std_and_turn(a, s, w, XT, ps[0:2], env.eps, None)

            @block.vector
            def _(v):
                chain = Chain(v, s["chain"])
                chain(v.tensor_scalar(sg[:, :], W[:, :], 0.0, 2.0, ALU.is_ge, ALU.mult))
                v.tensor_scalar(sg[:, :], sg[:, :], -1.0, None, ALU.add).then_inc(s["sg"], 1)
                v.wait_ge(s["yt"], 1)
                chain(v.tensor_scalar(yt[:, :], ps[1][:, :], cols[:, 0:1], cols[:, 1:2], ALU.mult, ALU.add))
                v.tensor_scalar(yt[:, :], yt[:, :], -LIMIT, LIMIT, ALU.max, ALU.min).then_inc(s["cl"], 1)
                v.wait_ge(s["y"], 1)
                normalise(v, chain, s, w, ps[2], X, batch_tile(env, b))
        nc.all_engine_barrier(sems_to_clear=s["numbers"])


def late_layouts(np, i):
    f32 = np.float32
    o = {}
    WIN = 32
    o["la_w"] = i["L1_attn_w_qkv"].T
    o["la_e"] = np.tile(i["L1_attn_rel_emb"][64 - WIN + 1:65].T, (H, 1))
    o["la_wo"] = i["L1_attn_w_out"].T
    sel = np.zeros((3, 2, H, 2, H, HD), f32)
    for r in range(2):
        for h in range(H):
            sel[:, r, h, r, h, :] = 1.0
    o["la_sel"] = sel.reshape(6 * H, 2, P)
    t, r = np.arange(P)[:, None], np.arange(WIN)[None]
    o["la_mask"] = np.where(t + r < WIN - 1, -1e30, 0.0).astype(f32)
    o["gm_w"] = np.stack([i["L1_ffn_attn_w"].T, i["L1_ffn_next_w"].T], 1)
    o["gm_cols"] = np.stack([i["L1_ffn_ln_scale"], i["L1_ffn_ln_bias"], i["L1_ffn_attn_b"]], 1)
    o["gm_row"] = i["L1_ffn_next_b"][None]
    two = lambda a: a.reshape((2, 4) + a.shape[1:])
    o["gm_w1"] = two(i["L1_ffn_w1"].reshape(8, P, 4, P)).transpose(0, 2, 1, 3, 4)
    o["gm_w2"] = two(i["L1_ffn_w2"].reshape(8, 4, P, P)).transpose(0, 3, 1, 2, 4)
    gb = np.concatenate([i["L1_ffn_b1"].reshape(8, 4, P), i["L1_ffn_b2"][:, None]], 1)
    o["gm_b"] = two(gb).transpose(0, 3, 1, 2)
    order = [8 * (m // 4) + 4 * r + m % 4 for m in range(8) for r in range(2)]
    swap = (np.arange(64) + 32) % 64
    wq = i["L2_attn_Wq"].reshape(16, 64, P)[order]
    wk = i["L2_attn_Wk"].reshape(4, 64, P)
    chunks = lambda a: np.stack([a.reshape(-1, P, P).transpose(2, 0, 1), a[:, swap].reshape(-1, P, P).transpose(2, 0, 1)], 1)
    o["lt_wq"], o["lt_wk"] = chunks(wq), chunks(wk)
    o["lt_wv"] = i["L2_attn_Wv"].T
    o["lt_wo"] = i["L2_attn_Wo"].T.reshape(16, 64, P)[order].reshape(8, P, P).transpose(1, 0, 2)
    inv = 1.0 / 10000.0 ** (np.arange(0, 64, 2, dtype=np.float64) / 64)
    freqs = np.outer(np.arange(S, dtype=np.float64), inv)
    emb = np.concatenate([freqs, freqs], -1).T
    sign = np.where(np.arange(64) < 32, -1.0, 1.0)[:, None]
    o["lt_rope"] = np.stack([np.tile(np.cos(emb), (2, 1)), np.tile(np.sin(emb) * sign, (2, 1))], 1).astype(f32)
    slope = 2.0 ** (-8.0 / 16 * (np.arange(16) + 1))
    lag = np.arange(S)[None] - np.arange(P)[:, None]
    o["lt_decay"] = np.where(lag[:, None] >= 0, np.exp(-slope[None, :, None] * np.maximum(lag, 0)[:, None]), 0.0).astype(f32)
    o["sm_gate"] = i["L2_ffn_Wg"]
    o["sm_w1"] = i["L2_ffn_w1"].reshape(P, 4, P)
    o["sm_w2"] = i["L2_ffn_w2"].reshape(4, P, P).transpose(1, 0, 2)
    by_feature = lambda a: a.T.reshape(P, H, HD).transpose(0, 2, 1).reshape(P, P)
    o["sa_w"] = np.concatenate([by_feature(i["L3_attn_" + n]) for n in ("wq", "wk", "wv")], 1)
    o["sa_wo"] = i["L3_attn_wo"].T
    o["sa_desc"] = np.tile(np.arange(8, 0, -1, dtype=f32), (P, 1))
    o["sa_heads"] = np.tile(np.eye(H, dtype=f32), (HD, 1))
    before, eye = np.triu(np.ones((P, P), f32), 1), np.eye(P, dtype=f32)
    o["sa_counting"] = np.stack([before - 1024 * eye, before.T - 1024 * eye, np.ones((P, P), f32),
                                 np.where(np.arange(P)[:, None] > np.arange(P)[None], -1e32, 0.0).astype(f32), eye], 1)
    o["sl_w"] = i["L3_ffn_weights"].T
    o["sl_cols"] = np.stack([i["L3_ffn_scale"], i["L3_ffn_bias"]], 1)
    return o


class Env:
    pass


def program(nc, d, out):
    env = Env()
    env.d = d
    env.scratch = nc.dram_tensor("scratch", (6, 3, P, S), BF16, kind="Internal").ap()
    env.mamba_layers = 4
    with ExitStack() as ctx:
        sb = lambda n, s: ctx.enter_context(nc.sbuf_tensor(n, s, F32))
        env.banks = [ctx.enter_context(nc.psum_tensor(f"bank{i}", [P, S], F32)) for i in range(8)]
        env.X = sb("x_tokens", [P, NT, P])
        env.ident = sb("identity", [P, P])
        env.eps = sb("eps", [P, 1])
        env.one = sb("ones", [P, 1])
        loads = [(env.X[:, :, :], d["x"].rearrange("b (c p) n -> p (b c) n", p=P)), (env.ident[:, :], d["ident"])]
        loads += load_common(nc, env, ctx)
        inputs_loaded, output_stored = (ctx.enter_context(nc.semaphore(n)) for n in ("inputs_loaded", "output_stored"))
        with nc.Block() as block:
            @block.sync
            def _(sp):
                for dst, src in loads:
                    sp.dma_start(dst, src).then_inc(inputs_loaded, 16)
                sp.wait_ge(inputs_loaded, 16 * len(loads))

            @block.vector
            def _(v):
                v.memset(env.eps[:, :], EPS)
                v.memset(env.one[:, :], 1.0)
                v.memset(env.one_row[:, :], 1.0)
        mamba(nc, env)
        with ExitStack() as inner:
            w = Batch(nc, inner, env.banks, "early_")
            with nc.Fori(0, B) as b:
                enter_batch(nc, env, w, b)
                cross_attention(nc, env, w, "x0", b, HD ** -0.5, True, False, False)
        moe(nc, env)
        with ExitStack() as inner:
            w = Batch(nc, inner, env.banks, "late_")
            load_late(nc, env, inner)
            with nc.Fori(0, B) as b:
                enter_batch(nc, env, w, b)
                with ExitStack() as until_lightning:
                    place_early_weights(nc, env, until_lightning)
                    local_attention(nc, env, w, b)
                    context_mlp(nc, env, w, b)
                    grouped_mlp(nc, env, w, b)
                    lightning(nc, env, w, b)
                cross_attention(nc, env, w, "x2", b, HD ** -0.5, False, True, False)
                shared_moe(nc, env, w, b)
                sparse_attention(nc, env, w, b)
                cross_attention(nc, env, w, "x3", b, HD ** -0.5, False, True, True)
                sign_linear(nc, env, w, b)
        with nc.Block() as block:
            @block.sync
            def _(sp):
                sp.dma_start(out.rearrange("b (c p) n -> p (b c) n", p=P), env.X[:, :, :]).then_inc(output_stored, 16)
                sp.wait_ge(output_stored, 16)


def layouts(np, i):
    L, DI, NS, R, NF = 4, 256, 16, 8, 2
    halves = lambda a: np.moveaxis(a.reshape(L, NF, P, -1), 1, 2)
    pc = np.concatenate([i["L0_attn_conv_w"], i["L0_attn_conv_b"][..., None], i["L0_attn_b_dt"][..., None],
                         i["L0_attn_Dp"][..., None], i["L0_attn_A_log"]], -1)
    flat = lambda a: a.reshape(L, P, -1)
    f32 = np.float32
    o = {
        "x": i["x"],
        "ident": np.eye(P, dtype=f32),
        "mamba_w": np.concatenate([i["L0_attn_W_in"].transpose(0, 2, 1),
                                   flat(halves(i["L0_attn_W_x"].transpose(0, 2, 1))),
                                   flat(halves(i["L0_attn_W_out"].transpose(0, 2, 1))),
                                   flat(halves(pc)),
                                   i["L0_attn_ln_w"][..., None], i["L0_attn_ln_b"][..., None]], -1),
        "mamba_wdt": i["L0_attn_W_dt"].transpose(0, 2, 1),
        "ctx": i["ctx_1024"].transpose(1, 0, 2),
        "ctx_t": i["ctx_1024"].transpose(2, 0, 1),
        "mask": i["mask_BxSxS2_if1"],
        "head_mask": np.repeat(np.eye(H, dtype=f32), HD, axis=0),
        "x0_w": np.stack([i["L0_xattn_W_Q"], i["L0_xattn_W_K"], i["L0_xattn_W_V"], i["L0_xattn_W_O"]], 1),
        "tri": np.triu(np.ones((P, P), f32), 1),
        "desc": np.tile(np.arange(8, 0, -1, dtype=f32), (P, 1)),
        "moe_gate": i["L0_ffn_Wg"].T,
        "moe_w1": i["L0_ffn_W1"].reshape(8, P, 4, P),
        "moe_w2": i["L0_ffn_W2"].reshape(8, 4, P, P).transpose(0, 2, 1, 3),
        "moe_b1": i["L0_ffn_b1"].reshape(8, 4, P).transpose(0, 2, 1),
        "moe_b2": np.repeat(i["L0_ffn_b2"][:, None], P, axis=1),
    }
    for pre, name in (("x2", "L2_xattn_"), ("x3", "L3_xattn_")):
        o[pre + "_w"] = np.stack([i[name + n].T for n in ("Wq", "Wk", "Wv", "Wo")], 1)
        o[pre + "_cols"] = np.stack([i[name + "bq"], i[name + "bk"]], 1)
        o[pre + "_rows"] = np.stack([i[name + "bv"], i[name + ("bo" if pre == "x3" else "bv")]])[None]
    sel = np.zeros((3, 2 * NS, 2 * NS, P), f32)
    for n in range(2 * NS):
        sel[:, n, n, :] = 1.0
    sel = sel.reshape(6 * NS, 2 * NS, P)
    o["mamba_sel"] = sel
    at = np.arange(5)[None] * P + np.arange(P)[:, None]
    own = at // KP - (np.arange(5) * P // KP)[None]
    o["chunk_heads"] = (own[:, :, None] == np.arange(3 * HD) // HD).astype(f32)
    o.update(late_layouts(np, i))
    return o


def kernel(**inputs):
    import numpy as np
    import concourse.bacc as bacc
    from concourse.bass_utils import run_bass_kernel_spmd as run

    nc = bacc.Bacc("TRN2", target_bir_lowering=False, num_devices=1)
    arrays, d = {}, {}
    for name, a in layouts(np, inputs).items():
        a = np.ascontiguousarray(a)
        arrays["in_" + name] = a
        d[name] = nc.dram_tensor("in_" + name, a.shape, mybir.dt.from_np(a.dtype), kind="ExternalInput").ap()
    out = nc.dram_tensor("out", (B, S, P), F32, kind="ExternalOutput").ap()
    program(nc, d, out)
    return run(nc, [arrays], core_ids=[0]).results[0]["out"]
```
